# Optimizing a Trainium2 kernel written in Bass

```python
import numpy as np
import jax
import jax.numpy as jnp

def _softmax(x, axis=-1):
    return jax.nn.softmax(x, axis=axis)

def _gelu(x):
    return jax.nn.gelu(x, approximate=True)

def _silu(x):
    return jax.nn.silu(x)

def _sigmoid(x):
    return jax.nn.sigmoid(x)

def _layernorm(x, axis=-1, eps=1e-05):
    m = jnp.mean(x, axis=axis, keepdims=True)
    v = jnp.var(x, axis=axis, keepdims=True)
    return (x - m) / jnp.sqrt(v + eps)

def _scatter_add(tgt, idx, src, axis=0):
    return tgt.at[idx].add(src)

def _segment_sum(src, seg, n):
    return jax.ops.segment_sum(src, seg, n)
kernel_name = 'mk_metaformer_d2_conv_nchw256_r2_0f2673'

def setup_inputs(seed: int=0):
    np.random.seed(seed)
    _w = jnp.asarray

    def _rec_inputs():
        import jax
        import jax.numpy as jnp
        _gk = jax.random.key(seed)
        x = -0.0001732 + 1 * jax.random.normal(jax.random.fold_in(_gk, 1), (2, 128, 48, 48), jnp.float32)
        return x
    x = _rec_inputs()

    def _L0_conv_setup():
        import jax, jax.numpy as jnp
        import numpy as np
        DIM = 128
        HEADS = 8
        P = 8
        S = 4

        def _pos_index(p):
            coord = np.arange(p)
            ii, jj = np.meshgrid(coord, coord, indexing='ij')
            cf = np.stack([ii.ravel(), jj.ravel()])
            rel = cf[:, :, None] - cf[:, None, :]
            rel = rel.transpose(1, 2, 0).copy()
            rel[:, :, 0] += p - 1
            rel[:, :, 1] += p - 1
            rel[:, :, 0] *= 2 * p - 1
            return jnp.asarray(rel.sum(-1))
        key = jax.random.key(seed)
        k1, k2, k3, k4, k5 = jax.random.split(key, 5)
        x = jax.random.normal(k1, (2, DIM, 48, 48), jnp.float32)
        qkv_w = jax.random.normal(k2, (3 * DIM,), jnp.float32) * 0.1 + 1.0
        qkv_b = jax.random.normal(k3, (3 * DIM,), jnp.float32) * 0.1
        out_w = jax.random.normal(k4, (DIM, DIM), jnp.float32) * 0.05
        pos_table = jax.random.normal(k5, ((2 * P - 1) ** 2, HEADS), jnp.float32) * 0.02
        return {'x': x, 'qkv_w': qkv_w, 'qkv_b': qkv_b, 'out_w': out_w, 'pos_table': pos_table}
    _L0_conv_all = _L0_conv_setup()
    _L0_conv_in = {k: v for k, v in _L0_conv_all.items() if k in ('qkv_w', 'qkv_b', 'out_w', 'pos_table')}
    del _L0_conv_all

    def _L0_ffn_setup():
        import jax, jax.numpy as jnp
        import numpy as np
        NUM_EXPERTS = 8
        TOP_K = 2
        B, S, D = (8, 4096, 128)

        def _moe(tokens, router_w, w1, b1, w2, b2):
            N = tokens.shape[0]
            E = router_w.shape[0]
            logits = tokens.astype(jnp.float32) @ router_w.astype(jnp.float32).T
            probs = jax.nn.softmax(logits, axis=-1)
            rw, re = jax.lax.top_k(probs, TOP_K)
            if TOP_K > 1:
                rw = rw / jnp.maximum(rw.sum(-1, keepdims=True), 1e-12)
            rw = rw.astype(tokens.dtype)
            combine = jnp.zeros((N, E), tokens.dtype).at[jnp.arange(N)[:, None], re].set(rw)
            out = tokens
            for e in range(E):
                h = jax.nn.gelu(tokens @ w1[e] + b1[e], approximate=False)
                y = h @ w2[e] + b2[e]
                out = out + combine[:, e:e + 1] * y
            return out
        key = jax.random.key(seed)
        ks = jax.random.split(key, 4)
        scale = 1.0 / np.sqrt(D).astype(np.float32)
        return {'input_embeddings': jax.random.normal(ks[0], (B, S, D), jnp.float32), 'router_w': jax.random.normal(ks[1], (NUM_EXPERTS, D), jnp.float32) * scale, 'w1': jax.random.normal(ks[2], (NUM_EXPERTS, D, D), jnp.float32) * scale, 'b1': jnp.zeros((NUM_EXPERTS, D), jnp.float32), 'w2': jax.random.normal(ks[3], (NUM_EXPERTS, D, D), jnp.float32) * scale, 'b2': jnp.zeros((NUM_EXPERTS, D), jnp.float32)}
    _L0_ffn_all = _L0_ffn_setup()
    _L0_ffn_in = {k: v for k, v in _L0_ffn_all.items() if k in ('router_w', 'w1', 'b1', 'w2', 'b2')}
    del _L0_ffn_all

    def _L1_conv_setup():
        import jax, jax.numpy as jnp
        import numpy as np
        from jax import lax
        IN_CHANNEL = 128
        C4 = IN_CHANNEL // 4
        LAYER_ARCH = 23
        IDX1 = LAYER_ARCH // 10
        IDX2 = LAYER_ARCH % 10
        GROUPS = 16
        EPS = 1e-05

        def _mask1(idx):
            m = np.zeros((1, 1, 9, 1, 1), np.float32)
            if idx == 3:
                m[:] = 1.0
            else:
                mgn = 3 - idx
                m[:, :, mgn:9 - mgn] = 1.0
            return jnp.asarray(m)

        def _mask2(idx):
            m = np.zeros((C4, 1, 9, 9), np.float32)
            if idx == 3:
                m[:] = 1.0
            else:
                mgn = 3 - idx
                m[:, :, mgn:9 - mgn, mgn:9 - mgn] = 1.0
            return jnp.asarray(m)

        def _group_norm(x, gamma, beta, groups=GROUPS, eps=EPS):
            B, C, H, W = x.shape
            xg = x.reshape(B, groups, C // groups * H * W)
            mu = xg.mean(-1, keepdims=True)
            var = xg.var(-1, keepdims=True)
            xn = ((xg - mu) * lax.rsqrt(var + eps)).reshape(B, C, H, W)
            return xn * gamma[None, :, None, None] + beta[None, :, None, None]
        key = jax.random.key(seed)
        ks = jax.random.split(key, 14)
        B, C, H, W = (8, IN_CHANNEL, 64, 64)
        return {'x': jax.random.normal(ks[0], (B, C, H, W), jnp.float32), 'W1': jax.random.normal(ks[1], (1, 1, 9, 1, 1), jnp.float32), 'W2': jax.random.normal(ks[2], (C4, 1, 9, 9), jnp.float32), 'conv1_w': jax.random.normal(ks[3], (C4, C), jnp.float32) * 0.05, 'conv1_b': jax.random.normal(ks[4], (C4,), jnp.float32) * 0.05, 'conv2_w': jax.random.normal(ks[5], (C, C4), jnp.float32) * 0.05, 'conv2_b': jax.random.normal(ks[6], (C,), jnp.float32) * 0.05, 'gn1_g': jax.random.normal(ks[7], (C4,), jnp.float32) * 0.1 + 1.0, 'gn1_b': jax.random.normal(ks[8], (C4,), jnp.float32) * 0.1, 'gnm_g': jax.random.normal(ks[9], (C4,), jnp.float32) * 0.1 + 1.0, 'gnm_b': jax.random.normal(ks[10], (C4,), jnp.float32) * 0.1, 'gn2_g': jax.random.normal(ks[11], (C,), jnp.float32) * 0.1 + 1.0, 'gn2_b': jax.random.normal(ks[12], (C,), jnp.float32) * 0.1}
    _L1_conv_all = _L1_conv_setup()
    _L1_conv_in = {k: v for k, v in _L1_conv_all.items() if k in ('W1', 'W2', 'conv1_w', 'conv1_b', 'conv2_w', 'conv2_b', 'gn1_g', 'gn1_b', 'gnm_g', 'gnm_b', 'gn2_g', 'gn2_b')}
    del _L1_conv_all

    def _L1_ffn_setup():
        import jax, jax.numpy as jnp
        import numpy as np
        D_MODEL = 128
        N_EXPERTS = 16
        HIDDEN = 256
        SCALE = 0.02
        key = jax.random.key(seed)
        ks = jax.random.split(key, 5)
        x = jax.random.normal(ks[0], (4, 4096, D_MODEL), dtype=jnp.float32)
        gate_w = jax.random.normal(ks[1], (D_MODEL, N_EXPERTS), dtype=jnp.float32) * SCALE
        gate_b = jnp.zeros((N_EXPERTS,), dtype=jnp.float32)
        w1 = jax.random.normal(ks[2], (N_EXPERTS, D_MODEL, HIDDEN), dtype=jnp.float32) * SCALE
        w2 = jax.random.normal(ks[3], (N_EXPERTS, D_MODEL, HIDDEN), dtype=jnp.float32) * SCALE
        w3 = jax.random.normal(ks[4], (N_EXPERTS, HIDDEN, D_MODEL), dtype=jnp.float32) * SCALE
        return {'x': x, 'gate_w': gate_w, 'gate_b': gate_b, 'w1': w1, 'w2': w2, 'w3': w3}
    _L1_ffn_all = _L1_ffn_setup()
    _L1_ffn_in = {k: v for k, v in _L1_ffn_all.items() if k in ('gate_w', 'gate_b', 'w1', 'w2', 'w3')}
    del _L1_ffn_all
    return {'x': x, 'L0_conv_qkv_w': _L0_conv_in['qkv_w'], 'L0_conv_qkv_b': _L0_conv_in['qkv_b'], 'L0_conv_out_w': _L0_conv_in['out_w'], 'L0_conv_pos_table': _L0_conv_in['pos_table'], 'L0_ffn_router_w': _L0_ffn_in['router_w'], 'L0_ffn_w1': _L0_ffn_in['w1'], 'L0_ffn_b1': _L0_ffn_in['b1'], 'L0_ffn_w2': _L0_ffn_in['w2'], 'L0_ffn_b2': _L0_ffn_in['b2'], 'L1_conv_W1': _L1_conv_in['W1'], 'L1_conv_W2': _L1_conv_in['W2'], 'L1_conv_conv1_w': _L1_conv_in['conv1_w'], 'L1_conv_conv1_b': _L1_conv_in['conv1_b'], 'L1_conv_conv2_w': _L1_conv_in['conv2_w'], 'L1_conv_conv2_b': _L1_conv_in['conv2_b'], 'L1_conv_gn1_g': _L1_conv_in['gn1_g'], 'L1_conv_gn1_b': _L1_conv_in['gn1_b'], 'L1_conv_gnm_g': _L1_conv_in['gnm_g'], 'L1_conv_gnm_b': _L1_conv_in['gnm_b'], 'L1_conv_gn2_g': _L1_conv_in['gn2_g'], 'L1_conv_gn2_b': _L1_conv_in['gn2_b'], 'L1_ffn_gate_w': _L1_ffn_in['gate_w'], 'L1_ffn_gate_b': _L1_ffn_in['gate_b'], 'L1_ffn_w1': _L1_ffn_in['w1'], 'L1_ffn_w2': _L1_ffn_in['w2'], 'L1_ffn_w3': _L1_ffn_in['w3']}

def reference(x, L0_conv_qkv_w, L0_conv_qkv_b, L0_conv_out_w, L0_conv_pos_table, L0_ffn_router_w, L0_ffn_w1, L0_ffn_b1, L0_ffn_w2, L0_ffn_b2, L1_conv_W1, L1_conv_W2, L1_conv_conv1_w, L1_conv_conv1_b, L1_conv_conv2_w, L1_conv_conv2_b, L1_conv_gn1_g, L1_conv_gn1_b, L1_conv_gnm_g, L1_conv_gnm_b, L1_conv_gn2_g, L1_conv_gn2_b, L1_ffn_gate_w, L1_ffn_gate_b, L1_ffn_w1, L1_ffn_w2, L1_ffn_w3):
    import jax
    import jax.numpy as jnp

    def _L0_conv_ref(x, qkv_w, qkv_b, out_w, pos_table):
        import jax, jax.numpy as jnp
        import numpy as np
        DIM = 128
        HEADS = 8
        P = 8
        S = 4

        def _pos_index(p):
            coord = np.arange(p)
            ii, jj = np.meshgrid(coord, coord, indexing='ij')
            cf = np.stack([ii.ravel(), jj.ravel()])
            rel = cf[:, :, None] - cf[:, None, :]
            rel = rel.transpose(1, 2, 0).copy()
            rel[:, :, 0] += p - 1
            rel[:, :, 1] += p - 1
            rel[:, :, 0] *= 2 * p - 1
            return jnp.asarray(rel.sum(-1))
        B, C, H, W = x.shape
        h, p, s = (HEADS, P, S)
        d = C // h
        pad = p - s
        xp = jnp.pad(x, ((0, 0), (0, 0), (0, pad), (0, pad)), mode='edge')
        x3 = jnp.concatenate([xp, xp, xp], axis=1)
        qkv = x3 * qkv_w[None, :, None, None] + qkv_b[None, :, None, None]
        n = (H + pad - p) // s + 1
        idx = (jnp.arange(n) * s)[:, None] + jnp.arange(p)[None, :]
        t = qkv[:, :, idx, :]
        t = t[:, :, :, :, idx]
        t = t.transpose(0, 1, 2, 4, 3, 5)
        t = t.reshape(B, 3, h, d, n * n, p * p).transpose(1, 0, 2, 4, 5, 3)
        q, k, v = (t[0] * d ** (-0.5), t[1], t[2])
        bias = pos_table[_pos_index(p)]
        bias = bias.transpose(2, 0, 1)
        attn = jnp.einsum('bhnqd,bhnkd->bhnqk', q, k) + bias[None, :, None]
        attn = jax.nn.softmax(attn, axis=-1)
        out = jnp.einsum('bhnqk,bhnkd->bhnqd', attn, v)
        out = out.reshape(B, h, n, n, p, p, d)[:, :, :, :, :s, :s]
        out = out.transpose(0, 1, 6, 2, 4, 3, 5).reshape(B, C, H, W)
        return jnp.einsum('oc,bchw->bohw', out_w, out)

    def _L0_ffn_ref(input_embeddings, router_w, w1, b1, w2, b2):
        import jax, jax.numpy as jnp
        import numpy as np
        NUM_EXPERTS = 8
        TOP_K = 2
        B, S, D = (8, 4096, 128)

        def _moe(tokens, router_w, w1, b1, w2, b2):
            N = tokens.shape[0]
            E = router_w.shape[0]
            logits = tokens.astype(jnp.float32) @ router_w.astype(jnp.float32).T
            probs = jax.nn.softmax(logits, axis=-1)
            rw, re = jax.lax.top_k(probs, TOP_K)
            if TOP_K > 1:
                rw = rw / jnp.maximum(rw.sum(-1, keepdims=True), 1e-12)
            rw = rw.astype(tokens.dtype)
            combine = jnp.zeros((N, E), tokens.dtype).at[jnp.arange(N)[:, None], re].set(rw)
            out = tokens
            for e in range(E):
                h = jax.nn.gelu(tokens @ w1[e] + b1[e], approximate=False)
                y = h @ w2[e] + b2[e]
                out = out + combine[:, e:e + 1] * y
            return out
        b, s, d = input_embeddings.shape
        tokens = input_embeddings.reshape(b * s, d)
        return _moe(tokens, router_w, w1, b1, w2, b2).reshape(b, s, d)

    def _L1_conv_ref(x, W1, W2, conv1_w, conv1_b, conv2_w, conv2_b, gn1_g, gn1_b, gnm_g, gnm_b, gn2_g, gn2_b):
        import jax, jax.numpy as jnp
        import numpy as np
        from jax import lax
        IN_CHANNEL = 128
        C4 = IN_CHANNEL // 4
        LAYER_ARCH = 23
        IDX1 = LAYER_ARCH // 10
        IDX2 = LAYER_ARCH % 10
        GROUPS = 16
        EPS = 1e-05

        def _mask1(idx):
            m = np.zeros((1, 1, 9, 1, 1), np.float32)
            if idx == 3:
                m[:] = 1.0
            else:
                mgn = 3 - idx
                m[:, :, mgn:9 - mgn] = 1.0
            return jnp.asarray(m)

        def _mask2(idx):
            m = np.zeros((C4, 1, 9, 9), np.float32)
            if idx == 3:
                m[:] = 1.0
            else:
                mgn = 3 - idx
                m[:, :, mgn:9 - mgn, mgn:9 - mgn] = 1.0
            return jnp.asarray(m)

        def _group_norm(x, gamma, beta, groups=GROUPS, eps=EPS):
            B, C, H, W = x.shape
            xg = x.reshape(B, groups, C // groups * H * W)
            mu = xg.mean(-1, keepdims=True)
            var = xg.var(-1, keepdims=True)
            xn = ((xg - mu) * lax.rsqrt(var + eps)).reshape(B, C, H, W)
            return xn * gamma[None, :, None, None] + beta[None, :, None, None]
        res = x
        h = jnp.einsum('bchw,oc->bohw', x, conv1_w) + conv1_b[None, :, None, None]
        h = _group_norm(h, gn1_g, gn1_b)
        x_sa = h
        w1m = W1 * _mask1(IDX1)
        y = lax.conv_general_dilated(h[:, None], w1m, window_strides=(1, 1, 1), padding=((4, 4), (0, 0), (0, 0)), dimension_numbers=('NCDHW', 'OIDHW', 'NCDHW'))[:, 0]
        w2m = W2 * _mask2(IDX2)
        y2 = lax.conv_general_dilated(x_sa, w2m, window_strides=(1, 1), padding=((4, 4), (4, 4)), dimension_numbers=('NCHW', 'OIHW', 'NCHW'), feature_group_count=C4)
        z = jax.nn.relu(_group_norm(y + y2, gnm_g, gnm_b))
        z = jnp.einsum('bchw,oc->bohw', z, conv2_w) + conv2_b[None, :, None, None]
        z = jax.nn.relu(_group_norm(z, gn2_g, gn2_b))
        return z + res

    def _L1_ffn_ref(x, gate_w, gate_b, w1, w2, w3):
        import jax, jax.numpy as jnp
        import numpy as np
        D_MODEL = 128
        N_EXPERTS = 16
        HIDDEN = 256
        SCALE = 0.02
        n_experts = w1.shape[0]
        logits = jnp.einsum('bsd,de->bse', x, gate_w) + gate_b
        probs = jax.nn.softmax(logits, axis=-1)
        top_probs, top_idx = jax.lax.top_k(probs, 2)
        top_probs = top_probs / jnp.sum(top_probs, axis=-1, keepdims=True)
        dispatch = jnp.sum(jax.nn.one_hot(top_idx, n_experts, dtype=x.dtype) * top_probs[..., None], axis=-2)
        h1 = jnp.einsum('bsd,edh->bseh', x, w1)
        h2 = jnp.einsum('bsd,edh->bseh', x, w2)
        hidden = jax.nn.silu(h1) * h2
        expert_out = jnp.einsum('bseh,eho->bseo', hidden, w3)
        return jnp.einsum('bseo,bse->bso', expert_out, dispatch)

    def _gn(v, G=32, eps=1e-05):
        B_, C_, H_, W_ = v.shape
        g = v.reshape(B_, G, C_ // G, H_, W_)
        m = jnp.mean(g, axis=(2, 3, 4), keepdims=True)
        s = jnp.var(g, axis=(2, 3, 4), keepdims=True)
        return ((g - m) / jnp.sqrt(s + eps)).reshape(v.shape)

    def _ln_c(v, eps=1e-06):
        m = jnp.mean(v, axis=1, keepdims=True)
        s = jnp.var(v, axis=1, keepdims=True)
        return (v - m) / jnp.sqrt(s + eps)

    def _ln_t(v, eps=1e-05):
        m = jnp.mean(v, axis=-1, keepdims=True)
        s = jnp.var(v, axis=-1, keepdims=True)
        return (v - m) / jnp.sqrt(s + eps)

    def _to_tokens(v):
        B_, C_, H_, W_ = v.shape
        return v.reshape(B_, C_, H_ * W_).transpose(0, 2, 1)

    def _from_tokens(t, like):
        B_, C_, H_, W_ = like.shape
        return t.transpose(0, 2, 1).reshape(B_, C_, H_, W_)
    x = x + _L0_conv_ref(_ln_c(x), L0_conv_qkv_w, L0_conv_qkv_b, L0_conv_out_w, L0_conv_pos_table)
    t = _to_tokens(x)
    t = t + _L0_ffn_ref(_ln_t(t), L0_ffn_router_w, L0_ffn_w1, L0_ffn_b1, L0_ffn_w2, L0_ffn_b2)
    x = _from_tokens(t, x)
    x = x + _L1_conv_ref(_ln_c(x), L1_conv_W1, L1_conv_W2, L1_conv_conv1_w, L1_conv_conv1_b, L1_conv_conv2_w, L1_conv_conv2_b, L1_conv_gn1_g, L1_conv_gn1_b, L1_conv_gnm_g, L1_conv_gnm_b, L1_conv_gn2_g, L1_conv_gn2_b)
    t = _to_tokens(x)
    t = t + _L1_ffn_ref(_ln_t(t), L1_ffn_gate_w, L1_ffn_gate_b, L1_ffn_w1, L1_ffn_w2, L1_ffn_w3)
    x = _from_tokens(t, x)
    return x

_drawn_inputs = setup_inputs


def setup_inputs(seed=0):
    import zlib

    import numpy as np

    out = dict(_drawn_inputs(seed))
    spreads = {'L0_ffn_b1': (0.0, 0.342), 'L0_ffn_b2': (0.0, 0.1), 'L1_ffn_gate_b': (0.0, 0.8)}
    factors = {'L0_conv_pos_table': 7.924,
     'L1_conv_conv1_b': 5.915,
     'L1_conv_gn1_g': 3.61,
     'L1_conv_gn1_b': 3.239,
     'L1_conv_gn2_b': 2.753,
     'L1_ffn_gate_w': 8.0,
     'L1_ffn_w1': 8.0,
     'L1_ffn_w2': 8.0,
     'L1_ffn_w3': 8.0}
    for name, (base, spread) in spreads.items():
        noise = np.random.default_rng([zlib.crc32(name.encode()), seed]).standard_normal(out[name].shape)
        drawn = base * np.exp(spread * noise) if base else spread * noise
        out[name] = jnp.asarray(drawn.astype(out[name].dtype))
    for name, factor in factors.items():
        out[name] = (out[name] * factor).astype(out[name].dtype)
    return out
```

```python
import concourse.bass as bass
from concourse import mybir
from contextlib import ExitStack


def metaformer_program(nc, x_tok, params, consts, pos_bias, out_wT, conv1_wT, conv2_wT, w2_rows, w1_conv,
                       router_wT, gate_wT, gate_b, moe0_w1, moe0_w2, moe0_b1, moe0_b2, moe1_w12, moe1_w3, out):
    fp32 = mybir.dt.float32
    i32 = mybir.dt.int32
    ALU = mybir.AluOpType
    ACT = mybir.ActivationFunctionType
    AX = mybir.AxisListType.X
    ds = bass.ds

    P = 128
    NB = 2
    IMG = 48
    NT = IMG * IMG
    TT = NT // P
    HEADS, HD, WS, WK = 8, 16, 4, 8
    NW = IMG // WS
    HW_ = NW // 2
    STEPS = 2 * NW
    Q = WS * WS
    KEYS = WK * WK
    PADI = IMG + WK - WS
    TG = 3
    NG = TT // TG
    EX = (8, 16)
    RING = 4
    TILES = tuple(-(-((2 * NT + (P - 1) * e) // P) // RING) * RING for e in EX)
    EMAX = max(EX)
    JMAX = max(TILES)
    C4 = 32
    CB, CX = NW + 2, IMG + 8
    HALF = NT // 4 // 2
    KX, KA = 9, 3

    names = {}
    ctx = ExitStack()
    with ctx:
        def sb(name, shape, dt=fp32):
            return ctx.enter_context(nc.sbuf_tensor(name, shape, dt))

        def S(name):
            if name not in names:
                names[name] = ctx.enter_context(nc.semaphore(name))
            return names[name]

        banks = [ctx.enter_context(nc.psum_tensor(f"bank{i}", [P, 512], fp32)) for i in range(8)]

        xs_dram = [[nc.dram_tensor(f"sorted_x{l}{b}", (TILES[l] * P, P), fp32).ap() for b in range(NB)] for l in range(2)]
        ys_dram = [[nc.dram_tensor(f"sorted_y{l}{b}", (TILES[l] * P, P), fp32).ap() for b in range(NB)] for l in range(2)]

        XT = [sb(f"residual{b}", [P, TT, P]) for b in range(NB)]
        TN = [sb(f"normed{b}", [P, TT, P]) for b in range(NB)]
        QY = [sb(f"qy{b}", [P, NT]) for b in range(NB)]
        CM = sb("chan_major", [P, NT])
        XPAD = [None] * NB
        KPAD = [None] * NB
        big = sb("padded_or_w12", [P, 4 * PADI * PADI])
        for b in range(NB):
            XPAD[b] = big[:, (2 * b) * PADI * PADI:(2 * b + 1) * PADI * PADI].rearrange("p (y x) -> p y x", x=PADI)
            KPAD[b] = big[:, (2 * b + 1) * PADI * PADI:(2 * b + 2) * PADI * PADI].rearrange("p (y x) -> p y x", x=PADI)
        W12 = big[:, 0:EX[1] * 512].rearrange("p (e h) -> p e h", h=512)
        W3 = sb("w3", [P, EX[1], 2, P])
        W1E = sb("moe0_w1", [P, EX[0], P])
        W2E = sb("moe0_w2", [P, EX[0], P])
        B1E = sb("moe0_b1", [P, EX[0], P])
        B2E = sb("moe0_b2", [P, EX[0], P])
        gath = sb("gathered_or_att", [P, 2 * TT * P])
        G = [gath[:, k * TT * P:(k + 1) * TT * P].rearrange("p (t c) -> p t c", c=P) for k in range(2)]
        W = HW_ * KEYS
        QBD = [gath[:, h * HW_ * P:(h + 1) * HW_ * P].rearrange("p (w m) -> p w m", m=P) for h in range(2)]
        o = 2 * HW_ * P
        VST, SB_, PE_, PN_ = ([gath[:, o + (2 * k + h) * W:o + (2 * k + h + 1) * W] for h in range(2)] for k in range(4))
        att2 = sb("att2_or_moe", [P, 2 * RING * P + 2 * P + 6 * 256])
        VTS, PTS = ([att2[:, (2 * k + h) * W:(2 * k + h + 1) * W] for h in range(2)] for k in range(2))
        OS = [att2[:, 4 * W + h * 192:4 * W + (h + 1) * 192].rearrange("p (a w q) -> p a w q", a=2, q=Q) for h in range(2)]
        TOEP = sb("toeplitz", [P, KA * KX, P])
        CON = sb("consts", [P, 5 * P + 8 + 2 + 32 + 7 * 32 + EMAX + JMAX + TT])
        IDN, TRI, ONE, G2, G8 = (CON[:, k * P:(k + 1) * P] for k in range(5))
        o = 5 * P
        HM, PAR, I32, DJ = CON[:, o:o + 8], CON[:, o + 8:o + 10], CON[:, o + 10:o + 42], CON[:, o + 42:o + 42 + 224]
        o += 42 + 224
        REV, JI, T128 = CON[:, o:o + EMAX], CON[:, o + EMAX:o + EMAX + JMAX], CON[:, o + EMAX + JMAX:o + EMAX + JMAX + TT]
        PRM = sb("params", [P, 16])
        (QW, QB, KW, KB, VW, VB, C1B, N1G, N1B, NMG, NMB, C2B, N2G, N2B) = (PRM[:, k:k + 1] for k in range(14))
        QS = sb("q_scaled", [P, 2])
        BIAS = sb("pos_bias", [P, KEYS])
        OWT = sb("out_w", [P, P])
        OWP = sb("out_w_parity", [P, 2, P])
        C1W = sb("conv1_w", [P, C4])
        C2W = sb("conv2_w", [P, P])
        W2R = sb("conv_rows", [P, 12, KX])
        W1C = sb("conv_chan", [P, 9])
        BAND = sb("band", [P, 32])
        RW = [sb("router_w", [P, EX[0]]), sb("gate_w", [P, EX[1]])]
        GB = sb("gate_b", [P, EX[1]])
        MXS = sb("score_max", [P, 2, HW_])
        RSM = sb("prob_sum", [P, 2, HW_])
        RRC = sb("prob_rsum", [P, 2, HW_])
        STT = sb("ln_stats", [P, TT, 6])
        LNV = sb("ln_values", [P, 6, TT])
        RT = sb("route", [P, 6, EMAX * TT])
        RS = sb("route_small", [P, 8, EMAX])
        RV = sb("route_rows", [P, 4, TT])
        EJ = sb("expert_cmp", [P, EMAX * JMAX // 2])
        EID = [[sb(f"expert_of_tile{l}{b}", [P, TILES[l]], i32) for b in range(NB)] for l in range(2)]
        POS = [sb(f"slot{b}", [P, 2, TT], i32) for b in range(NB)]
        GATE = [sb(f"gate{b}", [P, 2, TT]) for b in range(NB)]
        o = 0

        def carve(n, width):
            nonlocal o
            views = [att2[:, o + k * width:o + (k + 1) * width] for k in range(n)]
            o += n * width
            return views

        XS, YS, XTS, SG, HD_, HTS = carve(RING, P), carve(RING, P), carve(2, P), carve(2, 256), carve(2, 256), carve(2, 256)
        ZER = sb("zeros", [P, 512])
        HC = sb("conv_mid", [P, 2, HALF])
        HP = sb("conv_padded", [P, CB, CX])
        GST = sb("gn_stats", [P, 6, 6])
        GV = sb("gn_values", [P, 12])

        block = ctx.enter_context(nc.Block())

        order = ([("LNA", b) for b in range(NB)] + [("ATT", b) for b in range(NB)] +
                 [("R", 0, b) for b in range(NB)] + [("M", 0, b) for b in range(NB)] +
                 [p for b in range(NB) for p in (("X", b), ("R", 1, b))] +
                 [("M", 1, b) for b in range(NB)] + [("F", b) for b in range(NB)])
        group_base, n_groups = {}, 0
        for ph in order:
            for tag in {"LNA": ("a",), "R": ("y", "r") if ph[1] == 0 else ("r",), "X": ("c", "z")}.get(ph[0], ()):
                group_base[(tag,) + ph] = n_groups
                n_groups += NG

        def t_wait_full(eng, n):
            eng.wait_ge(S("t_full"), n + 1)

        lns = [ph for ph in order if ph[0] in ("LNA", "R", "X")]

        def pe_group(pe, n, srcs, ident=IDN):
            if n >= 2:
                pe.wait_ge(S("t_free"), n - 1)
            for k, a in enumerate(srcs):
                ins = nc.tensor.transpose(banks[n % 2][:, k * P:(k + 1) * P], a, ident)
            ins.then_inc(S("t_full"), 1)

        def ln_no(ph):
            return lns.index(ph) + 1

        def xs_value(j, r, b, J):
            if isinstance(j, int):
                return 16 * (j // RING + 1 + b * J // RING)
            return (j - r) * (16 // RING) + 16 * (1 + b * J // RING)

        def run(eng, lna, att, route, moe, conv, fin=None):
            for ph in order:
                if ph[0] == "LNA":
                    lna(ph[1])
                elif ph[0] == "ATT":
                    att(ph[1])
                elif ph[0] == "R":
                    route(ph[1], ph[2])
                elif ph[0] == "M":
                    moe(ph[1], ph[2])
                elif ph[0] == "X":
                    conv(ph[1])
                elif fin:
                    fin(ph[1])

        @block.sync
        def _(sp):
            for b in range(NB):
                sp.dma_start(XT[b][:, :, :], x_tok[b]).then_inc(S(f"x_in{b}"), 16)
                if b == 0:
                    sp.dma_start(CON[:, :], consts).then_inc(S("consts_in"), 16)
                    sp.dma_start(PRM[:, :], params).then_inc(S("consts_in"), 16)
                    sp.dma_start(BIAS[:, :], pos_bias).then_inc(S("consts_in"), 16)
                    sp.dma_start(OWT[:, :], out_wT).then_inc(S("consts_in"), 16)
            for dst, src in ((C1W, conv1_wT), (C2W, conv2_wT), (W1C, w1_conv), (RW[0], router_wT), (RW[1], gate_wT), (GB, gate_b)):
                sp.dma_start(dst[:, :], src).then_inc(S("small_in"), 16)
            sp.dma_start(W2R[:, :, :], w2_rows).then_inc(S("small_in"), 16)
            sp.dma_start(W1E[:, :, :], moe0_w1).then_inc(S("moe0_in"), 16)
            sp.dma_start(W2E[:, :, :], moe0_w2).then_inc(S("moe0_in"), 16)
            sp.dma_start(B1E[:, :, :], moe0_b1).then_inc(S("moe0_in"), 16)
            sp.dma_start(B2E[:, :, :], moe0_b2).then_inc(S("moe0_in"), 16)
            sp.dma_start(W3[:, :, :, :], moe1_w3).then_inc(S("moe1_in"), 16)
            sp.wait_ge(S("zeros_set"), 1)
            for l in range(2):
                for b in range(NB):
                    v = xs_dram[l][b].rearrange("(n r p) c -> n p r c", p=P, r=RING)
                    for n in range(TILES[l] // RING):
                        sp.dma_start(v[n], ZER[:, :].rearrange("p (r c) -> p r c", c=P)).then_inc(S(f"sorted_zero{l}{b}"), 16)

            def moe(l, b):
                J = TILES[l]

                def load(j, r):
                    if not isinstance(j, int) or j >= RING or b:
                        sp.wait_ge(S(f"x_transposed{l}"), j - RING + 1 + b * J)
                    sp.dma_start(XS[r][:, :], xs_dram[l][b].rearrange("(j p) c -> p j c", p=P)[:, ds(j, 1), :]).then_inc(S(f"xs_in{l}{r}"), 16)

                def store(j, r):
                    sp.wait_ge(S(f"y_ready{l}"), j + 1 + b * J)
                    sp.dma_start(ys_dram[l][b].rearrange("(j p) c -> p j c", p=P)[:, ds(j, 1), :], YS[r][:, :]).then_inc(S(f"ys_out{l}{r}"), 16)

                sp.wait_ge(S(f"scattered{l}{b}"), 16 * 2 * TT)
                for j in range(RING):
                    load(j, j)
                with sp.Fori(0, J // RING - 1) as turn:
                    i = turn * RING
                    for r in range(RING):
                        load(i + (RING + r), r)
                        store(i + r, r)
                for r in range(RING):
                    store(J - RING + r, r)

            sp.wait_ge(S("attn_y"), NB * STEPS)
            sp.wait_ge(S("scores"), NB * STEPS)
            sp.wait_ge(S("v_staged"), NB * STEPS)
            sp.dma_start(W12, moe1_w12).then_inc(S("moe1_in"), 16)
            moe(0, 0)
            moe(0, 1)
            moe(1, 0)
            moe(1, 1)
            for b in range(NB):
                for g in range(NG):
                    sp.wait_ge(S("out_ready"), b * NG + g + 1)
                    sp.dma_start(out[b, :, g * TG:(g + 1) * TG, :], XT[b][:, g * TG:(g + 1) * TG, :]).then_inc(S("out_stored"), 16)
            sp.wait_ge(S("out_stored"), 16 * NB * NG)

        @block.gpsimd
        def _(pool):
            nc.gpsimd.memset(ZER[:, :], 0.0).then_inc(S("zeros_set"), 1)
            nc.gpsimd.memset(HP[:, :, :], 0.0).then_inc(S("pad_zero"), 1)
            pool.wait_ge(S("consts_in"), 64)
            for b in range(NB):
                def step(s, hf, wy, last):
                    g = s + b * STEPS
                    if last >= 1:
                        if not isinstance(s, int) or g >= 2:
                            pool.wait_ge(S("scores"), g - 1)
                        out_ = QBD[hf].rearrange("p w (h q) -> p w h q", q=Q)
                        q_ = QY[b][:, :].rearrange("p (n q) -> p n q", q=Q)[:, ds(wy * NW + hf * HW_, HW_), :]
                        nc.gpsimd.tensor_tensor(out_, q_.unsqueeze(2).broadcast_to([P, HW_, HEADS, Q]),
                                                HM.unsqueeze(1).unsqueeze(3).broadcast_to([P, HW_, HEADS, Q]),
                                                ALU.mult).then_inc(S("qbd"), 1)

                def norm(s, hf):
                    g = s + b * STEPS
                    pool.wait_ge(S("rsum"), g + 1)
                    if not isinstance(s, int) or g >= 2:
                        pool.wait_ge(S("p_transposed"), g - 1)
                    pn = PN_[hf].rearrange("p (w k) -> p w k", k=KEYS)
                    pe_ = PE_[hf].rearrange("p (w k) -> p w k", k=KEYS)
                    nc.gpsimd.tensor_tensor(pn, pe_, RRC[:, hf, :].unsqueeze(2).broadcast_to([P, HW_, KEYS]), ALU.mult).then_inc(S("probs"), 1)

                pool.wait_ge(S("q_ready"), NG * (b + 1))
                step(0, 0, 0, 1)
                step(1, 1, 0, 1)
                norm(0, 0)
                with pool.Fori(1, NW) as i:
                    step(2 * i, 0, i, 1)
                    norm(2 * i - 1, 1)
                    step(2 * i + 1, 1, i, 1)
                    norm(2 * i, 0)
                norm(STEPS - 1, 1)

            def scatter(l, b):
                pool.wait_ge(S(f"routed{l}{b}"), 1)
                pool.wait_ge(S(f"sorted_zero{l}{b}"), 16 * (TILES[l] // RING))
                for t in range(TT):
                    for k in range(2):
                        nc.gpsimd.indirect_dma_start(xs_dram[l][b], bass.IndirectOffsetOnAxis(ap=POS[b][:, k, t:t + 1], axis=0),
                                                     TN[b][:, t, :], None).then_inc(S(f"scattered{l}{b}"), 16)

            def gather(l, b):
                n = l * NB + b
                for r in range(RING):
                    pool.wait_ge(S(f"ys_out{l}{r}"), 16 * (b + 1) * TILES[l] // RING)
                if n == 3:
                    pool.wait_ge(S("out_ready"), NG)
                elif n:
                    pool.wait_ge(S("combined"), n)
                for t in range(TT):
                    for k in range(2):
                        nc.gpsimd.indirect_dma_start(G[k][:, t, :], None, ys_dram[l][b],
                                                     bass.IndirectOffsetOnAxis(ap=POS[b][:, k, t:t + 1], axis=0)
                                                     ).then_inc(S(f"gathered{t // TG}"), 16)

            scatter(0, 0)
            scatter(0, 1)
            gather(0, 0)
            gather(0, 1)
            scatter(1, 0)
            scatter(1, 1)
            gather(1, 0)
            gather(1, 1)

        @block.tensor
        def _(pe):
            def lna(b):
                pe.wait_ge(S("ln_done"), ln_no(("LNA", b)))
                for g in range(NG):
                    pe_group(pe, group_base[("a", "LNA", b)] + g, [TN[b][:, g * TG + k, :] for k in range(TG)])

            def att(b):
                if b == 0:
                    pe.wait_ge(S("t_free"), NB * NG)
                pe.wait_ge(S("k_ready"), b + 1)

                def scores(s, hf, wy):
                    g = s + b * STEPS
                    pe.wait_ge(S("qbd"), g + 1)
                    if not isinstance(s, int) or g >= 2:
                        pe.wait_ge(S("biased"), g - 1)
                    for w in range(HW_):
                        wx = hf * HW_ + w
                        ins = nc.tensor.matmul(banks[2 + hf][:, w * KEYS:(w + 1) * KEYS], QBD[hf][:, w, :],
                                               KPAD[b][:, ds(wy * WS, WK), wx * WS:wx * WS + WK], start=True, stop=True)
                    ins.then_inc(S("scores"), 1)

                def transposes(s, hf):
                    g = s + b * STEPS
                    pe.wait_ge(S("probs"), g + 1)
                    if not isinstance(s, int) or g >= 1:
                        pe.wait_ge(S("pt_out"), g)
                    for p in range(HW_ // 2):
                        ins = nc.tensor.transpose(banks[5][:, p * P:(p + 1) * P], PN_[hf][:, p * P:(p + 1) * P], IDN)
                    ins.then_inc(S("p_transposed"), 1)
                    pe.wait_ge(S("v_staged"), g + 1)
                    if not isinstance(s, int) or g >= 1:
                        pe.wait_ge(S("vt_out"), g)
                    for p in range(HW_ // 2):
                        ins = nc.tensor.transpose(banks[0][:, p * P:(p + 1) * P], VST[hf][:, p * P:(p + 1) * P], IDN)
                    ins.then_inc(S("v_transposed"), 1)

                def weigh(s, hf):
                    g = s + b * STEPS
                    pe.wait_ge(S("k_ready"), b + 1)
                    pe.wait_ge(S("pt_out"), g + 1)
                    pe.wait_ge(S("vt_out"), g + 1)
                    if not isinstance(s, int) or g >= 1:
                        pe.wait_ge(S("o_out"), g)
                    for p in range(HW_ // 2):
                        for j in range(4):
                            for wl in range(2):
                                k = slice(64 * wl, 64 * wl + 64)
                                m = slice(p * P + 32 * j, p * P + 32 * j + 32)
                                ins = nc.tensor.matmul(banks[6 + wl][32 * j:32 * j + 32, p * 32:(p + 1) * 32],
                                                       VTS[hf][k, m], PTS[hf][k, m], start=True, stop=True)
                    ins.then_inc(S("weighed"), 1)

                def project(s, hf):
                    g = s + b * STEPS
                    pe.wait_ge(S("o_out"), g + 1)
                    if not isinstance(s, int) or g >= 1:
                        pe.wait_ge(S("attn_y"), g)
                    for a in range(2):
                        ins = nc.tensor.matmul(banks[1][:, 0:HW_ * Q], OWP[:, a, :], OS[hf][:, a, :, :].rearrange("p w q -> p (w q)"),
                                               start=(a == 0), stop=(a == 1))
                    ins.then_inc(S("projected"), 1)

                def step(s, hf, wy, isint):
                    if not isint or s >= 3 and s - 3 < STEPS:
                        transposes(s - 3, 1 - hf)
                    if not isint or s < STEPS:
                        scores(s, hf, wy)
                    if not isint or s >= 3 and s - 3 < STEPS:
                        weigh(s - 3, 1 - hf)
                    if not isint or s >= 4 and s - 4 < STEPS:
                        project(s - 4, hf)

                for s in range(4):
                    step(s, s % 2, s // 2, True)
                with pe.Fori(2, NW) as i:
                    step(2 * i, 0, i, False)
                    step(2 * i + 1, 1, i, False)
                for s in range(STEPS, STEPS + 4):
                    step(s, s % 2, s // 2, True)

            def route(l, b):
                if l == 0:
                    for g in range(NG):
                        if g == 0:
                            pe.wait_ge(S("attn_y"), NB * STEPS)
                            pe.wait_ge(S("o_out"), NB * STEPS)
                            pe.wait_ge(S("vt_out"), NB * STEPS)
                        pe_group(pe, group_base[("y", "R", 0, b)] + g, [QY[b][:, (g * TG + k) * P:(g * TG + k + 1) * P] for k in range(TG)])
                pe.wait_ge(S("ln_done"), ln_no(("R", l, b)))
                for g in range(NG):
                    pe_group(pe, group_base[("r", "R", l, b)] + g, [TN[b][:, g * TG + k, :] for k in range(TG)])
                E = EX[l]
                pe.wait_ge(S("t_free"), group_base[("r", "R", l, b)] + NG)
                if l == 0 and b == 0:
                    pe.wait_ge(S("small_in"), 16 * 7)
                for t in range(TT):
                    ins = nc.tensor.matmul(banks[2][:, t * E:(t + 1) * E], CM[:, t * P:(t + 1) * P], RW[l][:, :], start=True, stop=True)
                ins.then_inc(S("logits"), 1)
                n = l * NB + b
                pe.wait_ge(S("chosen"), n + 1)
                nc.tensor.matmul(banks[6][:, 0:TT * E], TRI, RT[:, 5, 0:TT * E], start=True, stop=True)
                nc.tensor.matmul(banks[7][:, 0:TT * E], ONE, RT[:, 5, 0:TT * E], start=True, stop=True).then_inc(S("prefix"), 1)

            def moe(l, b):
                J = TILES[l]
                if b == 0:
                    pe.wait_ge(S("moe0_in" if l == 0 else "moe1_in"), 64 if l == 0 else 32)
                    pe.wait_ge(S("t_free"), max(v for k, v in group_base.items() if k[1:3] == ("R", l)) + NG)
                pe.wait_ge(S(f"routed{l}{b}"), 1)
                IN = 2 * P if l else P

                def tx(j, r):
                    pe.wait_ge(S(f"xs_in{l}{r}"), xs_value(j, r, b, J))
                    if not isinstance(j, int) or b or j >= 2:
                        pe.wait_ge(S(f"xt_out{l}"), j - 1 + b * J)
                    nc.tensor.transpose(banks[r % 2][:, 0:P], XS[r][:, :], IDN).then_inc(S(f"x_transposed{l}"), 1)

                def hid(j, r):
                    e = pe.value_load(EID[l][b][0:1, ds(j, 1)], min_val=0, max_val=EX[l] - 1)
                    pe.wait_ge(S(f"xt_out{l}"), j + 1 + b * J)
                    if not isinstance(j, int) or b or j >= 2:
                        pe.wait_ge(S("hid1" if l else "h_free0"), j - 1 + b * J)
                    w = W12 if l else W1E
                    nc.tensor.matmul(banks[2 + r % 2][:, 0:(512 if l else P)], XTS[r % 2][:, :],
                                     w[:, ds(e, 1), :], start=True, stop=True).then_inc(S(f"h_full{l}"), 1)

                def th(j, r):
                    pe.wait_ge(S(f"hid{l}"), j + 1 + b * J)
                    if not isinstance(j, int) or b or j >= 2:
                        pe.wait_ge(S(f"ht_out{l}"), j - 1 + b * J)
                    for a in range(IN // P):
                        ins = nc.tensor.transpose(banks[4 + r % 2][:, a * P:(a + 1) * P], HD_[r % 2][:, a * P:(a + 1) * P], IDN)
                    ins.then_inc(S(f"ht_full{l}"), 1)

                def ym(j, r):
                    if isinstance(j, int) and j == 0 and b == 0:
                        pe.wait_ge(S(f"routed{l}1"), 1)
                    e = pe.value_load(EID[l][b][0:1, ds(j, 1)], min_val=0, max_val=EX[l] - 1)
                    pe.wait_ge(S(f"ht_out{l}"), j + 1 + b * J)
                    if not isinstance(j, int) or b or j >= 2:
                        pe.wait_ge(S(f"y_ready{l}"), j - 1 + b * J)
                    for a in range(IN // P):
                        rhs = W3[:, ds(e, 1), a, :] if l else W2E[:, ds(e, 1), :]
                        ins = nc.tensor.matmul(banks[6 + r % 2][:, 0:P], HTS[r % 2][:, a * P:(a + 1) * P], rhs,
                                               start=(a == 0), stop=(a == IN // P - 1))
                    ins.then_inc(S(f"y_full{l}"), 1)

                def step(j, r):
                    ok = lambda k: not isinstance(j, int) or 0 <= j - k < J
                    if ok(0):
                        tx(j, r)
                    if ok(3):
                        th(j - 3, (r + 1) % RING)
                    if ok(1):
                        hid(j - 1, (r + 3) % RING)
                    if ok(3):
                        ym(j - 3, (r + 1) % RING)

                for j in range(RING):
                    step(j, j)
                with pe.Fori(1, J // RING) as turn:
                    i = turn * RING
                    for r in range(RING):
                        step(i + r, r)
                for j in range(J, J + 3):
                    step(j, j % RING)

            def conv(b):
                pe.wait_ge(S("ln_done"), ln_no(("X", b)))
                if b == 0:
                    pe.wait_ge(S("xt_out0"), NB * TILES[0])
                for g in range(NG):
                    pe_group(pe, group_base[("c", "X", b)] + g, [TN[b][:, g * TG + k, :] for k in range(TG)])
                pe.wait_ge(S("t_free"), group_base[("c", "X", b)] + NG)
                if b == 0:
                    pe.wait_ge(S("h_free0"), NB * TILES[0])
                    pe.wait_ge(S("ht_out0"), NB * TILES[0])
                    pe.wait_ge(S("y_ready0"), NB * TILES[0])
                xin = QY[b][:, :].rearrange("p (n y x) -> p n y x", y=WS, x=WS)
                for hh in range(2):
                    for r in range(4):
                        ins = nc.tensor.matmul(banks[2 + hh][32 * r:32 * r + 32, 0:HALF], C1W[:, :],
                                               xin[:, hh * NW * NW // 2:(hh + 1) * NW * NW // 2, r, :], start=True, stop=True)
                ins.then_inc(S("conv1"), 1)

                def group_stats(mat, n):
                    pe.wait_ge(S("gn_in"), n + 1)
                    nc.tensor.matmul(banks[1][:, 0:2], mat, GV[:, 0:2], start=True, stop=True).then_inc(S("gn_sum"), 1)

                group_stats(G2, 3 * b)
                pe.wait_ge(S("hp_ready"), b + 1)
                if b == 0:
                    pe.wait_ge(S("toeplitz"), 1)
                for hh in range(2):
                    for n in range(KA * KX):
                        a, kx = divmod(n, KX)
                        ins = nc.tensor.matmul(banks[4 + hh][:, 0:HALF], TOEP[:, n, :],
                                               HP[:, hh * NW // 2 + a:hh * NW // 2 + a + NW // 2, kx:kx + IMG],
                                               start=(n == 0), stop=(n == KA * KX - 1))
                ins.then_inc(S("conv2"), 1)
                group_stats(G2, 3 * b + 1)
                pe.wait_ge(S("z_ready"), b + 1)
                for n in range(8):
                    r, hh = divmod(n, 2)
                    if n >= 4:
                        pe.wait_ge(S("up_out"), b * 8 + n - 3)
                    elif n == 0 and b:
                        pe.wait_ge(S("up_out"), 8 * b)
                    nc.tensor.matmul(banks[(2, 3, 6, 7)[n % 4]][:, 0:HALF], C2W[32 * r:32 * r + 32, :], HC[32 * r:32 * r + 32, hh, :],
                                     start=True, stop=True).then_inc(S("up"), 1)
                group_stats(G8, 3 * b + 2)
                pe.wait_ge(S("z3_ready"), b + 1)
                for g in range(NG):
                    if g == 0:
                        pe.wait_ge(S("gn_read"), 3 * b + 3)
                    pe_group(pe, group_base[("z", "X", b)] + g, [QY[b][:, (g * TG + k) * P:(g * TG + k + 1) * P] for k in range(TG)])

            run(pe, lna=lna, att=att, route=route, moe=moe, conv=conv)

        @block.scalar
        def _(act):
            def sqrt_of(ph):
                act.wait_ge(S("ln_var"), ln_no(ph))
                nc.scalar.activation(LNV[:, 4, :], LNV[:, 3, :], ACT.Sqrt).then_inc(S("ln_std"), 1)

            def evac(tag, ph, dst, sem="t_free"):
                for g in range(NG):
                    n = group_base[(tag,) + ph] + g
                    t_wait_full(act, n)
                    nc.scalar.activation(dst[:, g * TG * P:(g + 1) * TG * P], banks[n % 2][:, 0:TG * P], ACT.Copy).then_inc(S(sem), 1)

            def lna(b):
                sqrt_of(("LNA", b))
                if b == 0:
                    act.wait_ge(S("q_scaled"), 1)
                for g in range(NG):
                    n = group_base[("a", "LNA", b)] + g
                    t_wait_full(act, n)
                    src = banks[n % 2][:, 0:TG * P]
                    nc.scalar.activation(QY[b][:, g * TG * P:(g + 1) * TG * P], src, ACT.Identity, bias=QS[:, 1:2], scale=QS[:, 0:1]).then_inc(S("q_ready"), 1)
                    sw = src.rearrange("p (v w y x) -> p v w y x", v=2, y=WS, x=WS)
                    for v in range(2):
                        y0 = (2 * g + v) * WS
                        ins = nc.scalar.activation(XPAD[b][:, y0:y0 + WS, 0:IMG].rearrange("p y (w x) -> p w y x", x=WS), sw[:, v], ACT.Copy)
                    ins.then_inc(S("t_free"), 1)
                act.wait_ge(S("edge"), b + 1)
                nc.scalar.activation(KPAD[b], XPAD[b], ACT.Identity, bias=KB, scale=KW).then_inc(S("k_ready"), 1)

            def att(b):
                def value(s, hf, wy):
                    g = s + b * STEPS
                    if not isinstance(s, int) or g >= 2:
                        act.wait_ge(S("v_transposed"), g - 1)
                    a = XPAD[b][:, ds(wy * WS, WK), hf * HW_ * WS:hf * HW_ * WS + WK]
                    win = bass.AP(tensor=a.tensor, offset=a.offset, ap=[list(a.ap[0]), [WS, HW_], [PADI, WK], [1, WK]])
                    nc.scalar.activation(VST[hf].rearrange("p (w y x) -> p w y x", y=WK, x=WK), win, ACT.Identity, bias=VB, scale=VW).then_inc(S("v_staged"), 1)

                def expo(s, hf):
                    g = s + b * STEPS
                    act.wait_ge(S("shifted"), g + 1)
                    if not isinstance(s, int) or g >= 2:
                        act.wait_ge(S("probs"), g - 1)
                    nc.scalar.activation(PE_[hf], SB_[hf], ACT.Exp).then_inc(S("exps"), 1)

                def outs(s, hf):
                    g = s + b * STEPS
                    act.wait_ge(S("p_transposed"), g + 1)
                    if not isinstance(s, int) or g >= 2:
                        act.wait_ge(S("weighed"), g - 1)
                    nc.scalar.activation(PTS[hf], banks[5][:, 0:W], ACT.Copy).then_inc(S("pt_out"), 1)
                    act.wait_ge(S("v_transposed"), g + 1)
                    nc.scalar.activation(VTS[hf], banks[0][:, 0:W], ACT.Copy).then_inc(S("vt_out"), 1)

                def step(s, hf, wy, isint):
                    if not isint or s >= 3 and s - 3 < STEPS:
                        outs(s - 3, 1 - hf)
                    if not isint or 1 <= s <= STEPS:
                        expo(s - 1, 1 - hf)
                    if not isint or 2 <= s < STEPS + 2:
                        value(s - 2, hf, wy - 1)

                for s in range(4):
                    step(s, s % 2, s // 2, True)
                with act.Fori(2, NW) as i:
                    step(2 * i, 0, i, False)
                    step(2 * i + 1, 1, i, False)
                for s in range(STEPS, STEPS + 4):
                    step(s, s % 2, s // 2, True)

            def route(l, b):
                ph = ("R", l, b)
                sqrt_of(ph)
                if l == 1 or b == 1:
                    act.wait_ge(S("logits"), l * NB + b)
                if l == 1:
                    act.wait_ge(S("z3_ready"), b + 1)
                evac("r", ph, CM)
                n = l * NB + b
                act.wait_ge(S("logit_shift"), n + 1)
                nc.scalar.activation(RT[:, 1, 0:TT * EX[l]], RT[:, 0, 0:TT * EX[l]], ACT.Exp).then_inc(S("logit_exp"), 1)

            def moe(l, b):
                J = TILES[l]

                def xt(j, r):
                    act.wait_ge(S(f"x_transposed{l}"), j + 1 + b * J)
                    if not isinstance(j, int) or b or j >= 2:
                        act.wait_ge(S(f"h_full{l}"), j - 1 + b * J)
                    nc.scalar.activation(XTS[r % 2][:, :], banks[r % 2][:, 0:P], ACT.Copy).then_inc(S(f"xt_out{l}"), 1)

                def nonlin(j, r):
                    if l:
                        act.wait_ge(S("h_full1"), j + 1 + b * J)
                        if not isinstance(j, int) or b or j >= 2:
                            act.wait_ge(S("hid1"), j - 1 + b * J)
                        nc.scalar.activation(SG[r % 2][:, :], banks[2 + r % 2][:, 0:256], ACT.Silu).then_inc(S("silu"), 1)
                    else:
                        act.wait_ge(S("h_free0"), j + 1 + b * J)
                        if not isinstance(j, int) or b or j >= 2:
                            act.wait_ge(S("ht_full0"), j - 1 + b * J)
                        nc.scalar.activation(HD_[r % 2][:, 0:P], SG[r % 2][:, 0:P], ACT.Gelu).then_inc(S("hid0"), 1)

                def tail(j, r):
                    if l:
                        act.wait_ge(S("y_full1"), j + 1 + b * J)
                        if not isinstance(j, int) or b or j >= RING:
                            act.wait_ge(S(f"ys_out1{r}"), xs_value(j, r, b, J) - 16)
                        nc.scalar.activation(YS[r][:, :], banks[6 + r % 2][:, 0:P], ACT.Copy).then_inc(S("y_ready1"), 1)
                    else:
                        act.wait_ge(S("ht_full0"), j + 1 + b * J)
                        if not isinstance(j, int) or b or j >= 2:
                            act.wait_ge(S("y_full0"), j - 1 + b * J)
                        nc.scalar.activation(HTS[r % 2][:, 0:P], banks[4 + r % 2][:, 0:P], ACT.Copy).then_inc(S("ht_out0"), 1)

                def step(j, r):
                    ok = lambda k: not isinstance(j, int) or 0 <= j - k < J
                    if ok(0):
                        xt(j, r)
                    if not l and ok(3):
                        tail(j - 3, (r + 1) % RING)
                    if ok(1):
                        nonlin(j - 1, (r + 3) % RING)
                    if l and ok(3):
                        tail(j - 3, (r + 1) % RING)

                for j in range(RING):
                    step(j, j)
                with act.Fori(1, J // RING) as turn:
                    i = turn * RING
                    for r in range(RING):
                        step(i + r, r)
                for j in range(J, J + 3):
                    step(j, j % RING)

            def conv(b):
                sqrt_of(("X", b))
                evac("c", ("X", b), QY[b])

                def gn_sqrt(n):
                    act.wait_ge(S("gn_var"), n + 1)
                    nc.scalar.activation(GV[:, 6:7], GV[:, 5:6], ACT.Sqrt).then_inc(S("gn_std"), 1)

                act.wait_ge(S("conv1"), b + 1)
                for hh in range(2):
                    nc.scalar.activation(HC[:, hh, :], banks[2 + hh][:, 0:HALF], ACT.Identity, bias=C1B).then_inc(S("hc_ready"), 1)
                gn_sqrt(3 * b)
                act.wait_ge(S("gn_coef"), 3 * b + 1)
                act.wait_ge(S("pad_zero"), 1)
                for hh in range(2):
                    ins = nc.scalar.activation(HP[:, 1 + hh * NW // 2:1 + (hh + 1) * NW // 2, 4:4 + IMG], HC[:, hh, :].rearrange("p (a x) -> p a x", x=IMG),
                                               ACT.Identity, bias=GV[:, 8:9], scale=GV[:, 7:8])
                ins.then_inc(S("hp_ready"), 1)
                gn_sqrt(3 * b + 1)
                act.wait_ge(S("gn_coef"), 3 * b + 2)
                for hh in range(2):
                    ins = nc.scalar.activation(HC[:, hh, :], banks[4 + hh][:, 0:HALF], ACT.Relu, bias=GV[:, 8:9], scale=GV[:, 7:8])
                ins.then_inc(S("z_ready"), 1)
                cm = CM[:, :].rearrange("p (n y x) -> p n y x", y=WS, x=WS)
                for n in range(8):
                    r, hh = divmod(n, 2)
                    act.wait_ge(S("up"), b * 8 + n + 1)
                    nc.scalar.activation(cm[:, hh * NW * NW // 2:(hh + 1) * NW * NW // 2, r, :],
                                         banks[(2, 3, 6, 7)[n % 4]][:, 0:HALF].rearrange("p (n x) -> p n x", x=WS),
                                         ACT.Identity, bias=C2B).then_inc(S("up_out"), 1)
                gn_sqrt(3 * b + 2)
                act.wait_ge(S("gn_coef"), 3 * b + 3)
                nc.scalar.activation(QY[b][:, :], CM[:, :], ACT.Relu, bias=GV[:, 8:9], scale=GV[:, 7:8]).then_inc(S("z3_ready"), 1)

            act.wait_ge(S("consts_in"), 64)
            run(act, lna=lna, att=att, route=route, moe=moe, conv=conv)

        @block.vector
        def _(dve):
            chain = [0]

            def link(ins):
                chain[0] += 1
                ins.then_inc(S("dve_chain"), 1)
                dve.wait_ge(S("dve_chain"), chain[0])

            tt, ts = nc.vector.tensor_tensor, nc.vector.tensor_scalar

            def layer_norm(ph, b, eps):
                for t in range(TT):
                    ins = nc.vector.bn_stats(STT[:, t, :], XT[b][:, t, :])
                link(ins)
                me, ve, mo, vo = (STT[:, :, k] for k in (1, 2, 4, 5))
                tt(LNV[:, 0, :], me, mo, ALU.add)
                tt(LNV[:, 1, :], me, mo, ALU.subtract)
                link(tt(LNV[:, 2, :], ve, vo, ALU.add))
                ts(LNV[:, 0, :], LNV[:, 0, :], 0.5, None, ALU.mult)
                link(tt(LNV[:, 1, :], LNV[:, 1, :], LNV[:, 1, :], ALU.mult))
                link(nc.vector.scalar_tensor_tensor(LNV[:, 3, :], LNV[:, 1, :], float(P // 4), LNV[:, 2, :], ALU.mult, ALU.add))
                ts(LNV[:, 3, :], LNV[:, 3, :], 1.0 / P, eps, ALU.mult, ALU.add).then_inc(S("ln_var"), 1)
                dve.wait_ge(S("ln_std"), ln_no(ph))
                link(nc.vector.reciprocal(LNV[:, 5, :], LNV[:, 4, :]))
                for t in range(TT):
                    ins = ts(TN[b][:, t, :], XT[b][:, t, :], LNV[:, 0, t:t + 1], LNV[:, 5, t:t + 1], ALU.subtract, ALU.mult)
                ins.then_inc(S("ln_done"), 1)

            def lna(b):
                dve.wait_ge(S(f"x_in{b}"), 16)
                if b == 0:
                    dve.wait_ge(S("consts_in"), 64)
                    ts(QS[:, 0:1], QW, HD ** -0.5, None, ALU.mult)
                    ts(QS[:, 1:2], QB, HD ** -0.5, None, ALU.mult).then_inc(S("q_scaled"), 1)
                    for a in range(2):
                        ins = ts(OWP[:, a, :], OWT[:, :], PAR[:, a:a + 1], None, ALU.mult)
                    link(ins)
                layer_norm(("LNA", b), b, 1e-6)
                if b == 0:
                    dve.wait_ge(S("small_in"), 16 * 7)
                    for a in range(KA):
                        for r in range(4):
                            tt(TOEP[:, a * KX:(a + 1) * KX, 32 * r:32 * r + 32], I32.unsqueeze(1).broadcast_to([P, KX, 32]),
                               W2R[:, 4 * a - r + 3, :].unsqueeze(2).broadcast_to([P, KX, 32]), ALU.mult)
                    link(ts(BAND[:, :], DJ[:, 0:32], W1C[:, 1:2], None, ALU.mult))
                    for j in range(1, 7):
                        link(nc.vector.scalar_tensor_tensor(BAND[:, :], DJ[:, 32 * j:32 * j + 32], W1C[:, j + 1:j + 2], BAND[:, :], ALU.mult, ALU.add))
                    for r in range(4):
                        blk = TOEP[32 * r:32 * r + 32, KX + KX // 2, 32 * r:32 * r + 32]
                        ins = tt(blk, blk, BAND[32 * r:32 * r + 32, :], ALU.add)
                    ins.then_inc(S("toeplitz"), 1)
                dve.wait_ge(S("t_free"), group_base[("a", "LNA", b)] + NG)
                link(nc.vector.tensor_copy(XPAD[b][:, 0:IMG, IMG:PADI], XPAD[b][:, 0:IMG, IMG - 1:IMG].broadcast_to([P, IMG, PADI - IMG])))
                nc.vector.tensor_copy(XPAD[b][:, IMG:PADI, :], XPAD[b][:, IMG - 1:IMG, :].broadcast_to([P, PADI - IMG, PADI])).then_inc(S("edge"), 1)

            def att(b):
                def three(ap):
                    return ap.rearrange("p (w k) -> p w k", k=KEYS)

                def top(s, hf):
                    g = s + b * STEPS
                    dve.wait_ge(S("scores"), g + 1)
                    if not isinstance(s, int) or g >= 2:
                        dve.wait_ge(S("exps"), g - 1)
                    tt(three(SB_[hf]), three(banks[2 + hf][:, 0:W]), BIAS[:, :].unsqueeze(1).broadcast_to([P, HW_, KEYS]), ALU.add).then_inc(S("biased"), 1)
                    dve.wait_ge(S("biased"), g + 1)
                    nc.vector.tensor_reduce(MXS[:, hf, :], three(SB_[hf]), AX, ALU.max).then_inc(S("maxed"), 1)
                    dve.wait_ge(S("maxed"), g + 1)
                    tt(three(SB_[hf]), three(SB_[hf]), MXS[:, hf, :].unsqueeze(2).broadcast_to([P, HW_, KEYS]), ALU.subtract).then_inc(S("shifted"), 1)

                def sums(s, hf):
                    g = s + b * STEPS
                    dve.wait_ge(S("exps"), g + 1)
                    nc.vector.tensor_reduce(RSM[:, hf, :], three(PE_[hf]), AX, ALU.add).then_inc(S("summed"), 1)
                    dve.wait_ge(S("summed"), g + 1)
                    if not isinstance(s, int) or g >= 2:
                        dve.wait_ge(S("probs"), g - 1)
                    nc.vector.reciprocal(RRC[:, hf, :], RSM[:, hf, :]).then_inc(S("rsum"), 1)

                def o_out(s, hf):
                    g = s + b * STEPS
                    dve.wait_ge(S("weighed"), g + 1)
                    if not isinstance(s, int) or g >= 2:
                        dve.wait_ge(S("projected"), g - 1)
                    os_ = OS[hf].rearrange("p a (w l) q -> p l w a q", l=2)
                    for wl in range(2):
                        ins = nc.vector.tensor_copy(os_[:, wl], banks[6 + wl][:, 0:96].rearrange("p (w a q) -> p w a q", a=2, q=Q))
                    ins.then_inc(S("o_out"), 1)

                def y_out(s, hf, wy):
                    g = s + b * STEPS
                    dve.wait_ge(S("projected"), g + 1)
                    nc.vector.tensor_copy(QY[b][:, :].rearrange("p (n q) -> p n q", q=Q)[:, ds(wy * NW + hf * HW_, HW_), :],
                                          banks[1][:, 0:HW_ * Q].rearrange("p (n q) -> p n q", q=Q)).then_inc(S("attn_y"), 1)

                def step(s, hf, wy, isint):
                    if not isint or s < STEPS:
                        top(s, hf)
                    if not isint or s >= 5 and s - 5 < STEPS:
                        y_out(s - 5, 1 - hf, wy - 3 + hf)
                    if not isint or 1 <= s <= STEPS:
                        sums(s - 1, 1 - hf)
                    if not isint or s >= 3 and s - 3 < STEPS:
                        o_out(s - 3, 1 - hf)

                for s in range(6):
                    step(s, s % 2, s // 2, True)
                with dve.Fori(3, NW) as i:
                    step(2 * i, 0, i, False)
                    step(2 * i + 1, 1, i, False)
                for s in range(STEPS, STEPS + 5):
                    step(s, s % 2, s // 2, True)

            def route(l, b):
                E, ph, n, J = EX[l], ("R", l, b), l * NB + b, TILES[l]
                c = TT * E
                if l == 0:
                    for g in range(NG):
                        m = group_base[("y",) + ph] + g
                        t_wait_full(dve, m)
                        xt = XT[b][:, g * TG:(g + 1) * TG, :]
                        tt(xt, xt, banks[m % 2][:, 0:TG * P].rearrange("p (t c) -> p t c", c=P), ALU.add).then_inc(S("t_free"), 1)
                    dve.wait_ge(S("t_free"), group_base[("y",) + ph] + NG)
                layer_norm(ph, b, 1e-5)
                row = lambda k: RT[:, k, 0:c].rearrange("p (t e) -> p t e", e=E)
                over_e = lambda v: v.unsqueeze(2).broadcast_to([P, TT, E])
                over_t = lambda v: v.unsqueeze(1).broadcast_to([P, TT, E])
                v = [RV[:, k, :] for k in range(4)]
                dve.wait_ge(S("logits"), n + 1)
                lg = banks[2][:, 0:c].rearrange("p (t e) -> p t e", e=E)
                if l:
                    link(tt(row(0), lg, over_t(GB[:, :]), ALU.add))
                else:
                    link(nc.vector.tensor_copy(row(0), lg))
                link(nc.vector.tensor_reduce(v[0], row(0), AX, ALU.max))
                tt(row(0), row(0), over_e(v[0]), ALU.subtract).then_inc(S("logit_shift"), 1)
                dve.wait_ge(S("logit_exp"), n + 1)
                link(nc.vector.tensor_reduce(v[0], row(1), AX, ALU.add))
                link(nc.vector.reciprocal(v[1], v[0]))
                link(tt(row(1), row(1), over_e(v[1]), ALU.mult))
                for k in range(2):
                    link(nc.vector.tensor_reduce(v[k], row(1), AX, ALU.max))
                    link(tt(row(0), row(1), over_e(v[k]), ALU.is_equal))
                    link(tt(row(0), row(0), over_t(REV[:, 0:E]), ALU.mult))
                    link(nc.vector.tensor_reduce(v[2], row(0), AX, ALU.max))
                    link(tt(row(2 + k), row(0), over_e(v[2]), ALU.is_equal))
                    if k == 0:
                        link(nc.vector.scalar_tensor_tensor(row(1), row(2), -2.0, row(1), ALU.mult, ALU.add))
                tt(row(5), row(2), row(3), ALU.add).then_inc(S("chosen"), 1)
                link(tt(v[2], v[0], v[1], ALU.add))
                if l == 0:
                    link(nc.vector.tensor_scalar_max(v[2], v[2], 1e-12))
                link(nc.vector.reciprocal(v[3], v[2]))
                tt(GATE[b][:, 0, :], v[0], v[3], ALU.mult)
                tt(GATE[b][:, 1, :], v[1], v[3], ALU.mult)
                dve.wait_ge(S("prefix"), n + 1)
                tot = RT[:, 0, 0:c].rearrange("p (e t) -> p e t", t=TT)
                one = RT[:, 1, 0:c].rearrange("p (e t) -> p e t", t=TT)
                nc.vector.memset(RT[:, 1, 0:c], 1.0).then_inc(S("dve_chain"), 1)
                chain[0] += 1
                link(nc.vector.tensor_copy(tot, banks[7][:, 0:c].rearrange("p (t e) -> p e t", e=E)))
                link(nc.vector.memset(one[:, :, 0:1], 0.0))
                link(nc.vector.tensor_tensor_scan(RT[:, 4, 0:c], RT[:, 1, 0:c], RT[:, 0, 0:c], 0.0, ALU.mult, ALU.add))
                run_ = RT[:, 4, 0:c].rearrange("p (e t) -> p e t", t=TT)
                cnt, nt, st, en = (RS[:, k, 0:E] for k in range(4))
                nc.vector.tensor_copy(cnt, run_[:, :, TT - 1])
                link(tt(tot, run_, tot, ALU.subtract))
                tmp = RT[:, 1, 0:c].rearrange("p (e t) -> p e t", t=TT)
                if TT * P < NT:
                    raise ValueError
                link(tt(tmp, cnt.unsqueeze(2).broadcast_to([P, E, TT]), T128.unsqueeze(1).broadcast_to([P, E, TT]), ALU.is_gt))
                link(nc.vector.tensor_reduce(nt, tmp, AX, ALU.add))
                link(nc.vector.tensor_tensor_scan(en, ONE[:, 0:E], nt, 0.0, ALU.mult, ALU.add))
                link(tt(st, en, nt, ALU.subtract))
                ej = EJ[:, 0:E * J // 2].rearrange("p (j e) -> p j e", e=E)
                jh = J // 2
                for hh in range(2):
                    link(tt(ej, en.unsqueeze(1).broadcast_to([P, jh, E]), JI[:, hh * jh:(hh + 1) * jh].unsqueeze(2).broadcast_to([P, jh, E]), ALU.is_le))
                    link(nc.vector.tensor_reduce(RT[:, 1, hh * jh:(hh + 1) * jh], ej, AX, ALU.add))
                nc.vector.tensor_scalar_min(EID[l][b][:, :], RT[:, 1, 0:J], float(E - 1))
                link(nc.vector.scalar_tensor_tensor(RT[:, 4, 0:c].rearrange("p (t e) -> p e t", e=E), st.unsqueeze(2).broadcast_to([P, E, TT]),
                                                    float(P), tot, ALU.mult, ALU.add))
                link(tt(row(4), row(4), banks[6][:, 0:c].rearrange("p (t e) -> p t e", e=E), ALU.add))
                for k in range(2):
                    link(tt(row(0), row(2 + k), row(4), ALU.mult))
                    link(nc.vector.tensor_reduce(v[2], row(0), AX, ALU.add))
                    ins = nc.vector.tensor_copy(POS[b][:, k, :], v[2])
                    if k == 0:
                        link(ins)
                ins.then_inc(S(f"routed{l}{b}"), 1)

            def moe(l, b):
                J = TILES[l]

                def first(j, r):
                    if l:
                        dve.wait_ge(S("silu"), j + 1 + b * J)
                        if not isinstance(j, int) or b or j >= 2:
                            dve.wait_ge(S("ht_full1"), j - 1 + b * J)
                        tt(HD_[r % 2][:, :], SG[r % 2][:, :], banks[2 + r % 2][:, 256:512], ALU.mult).then_inc(S("hid1"), 1)
                        return
                    e = dve.value_load(EID[0][b][0:1, ds(j, 1)], min_val=0, max_val=EX[0] - 1)
                    dve.wait_ge(S("h_full0"), j + 1 + b * J)
                    if not isinstance(j, int) or b or j >= 2:
                        dve.wait_ge(S("hid0"), j - 1 + b * J)
                    tt(SG[r % 2][:, 0:P], banks[2 + r % 2][:, 0:P], B1E[:, ds(e, 1), :].rearrange("p a c -> p (a c)"), ALU.add).then_inc(S("h_free0"), 1)

                def second(j, r):
                    if l:
                        dve.wait_ge(S("ht_full1"), j + 1 + b * J)
                        if not isinstance(j, int) or b or j >= 2:
                            dve.wait_ge(S("y_full1"), j - 1 + b * J)
                        nc.vector.tensor_copy(HTS[r % 2][:, :], banks[4 + r % 2][:, 0:256]).then_inc(S("ht_out1"), 1)
                        return
                    e = dve.value_load(EID[0][b][0:1, ds(j, 1)], min_val=0, max_val=EX[0] - 1)
                    dve.wait_ge(S("y_full0"), j + 1 + b * J)
                    if not isinstance(j, int) or b or j >= RING:
                        dve.wait_ge(S(f"ys_out0{r}"), xs_value(j, r, b, J) - 16)
                    tt(YS[r][:, :], banks[6 + r % 2][:, 0:P], B2E[:, ds(e, 1), :].rearrange("p a c -> p (a c)"), ALU.add).then_inc(S("y_ready0"), 1)

                def step(j, r):
                    ok = lambda k: not isinstance(j, int) or 0 <= j - k < J
                    if l and ok(3):
                        second(j - 3, (r + 1) % RING)
                    if ok(1):
                        first(j - 1, (r + 3) % RING)
                    if not l and ok(3):
                        second(j - 3, (r + 1) % RING)

                for j in range(RING):
                    step(j, j)
                with dve.Fori(1, J // RING) as turn:
                    i = turn * RING
                    for r in range(RING):
                        step(i + r, r)
                for j in range(J, J + 3):
                    step(j, j % RING)

            def combine(l, b, done=None):
                if l == 0:
                    dve.wait_ge(S("scattered0%d" % b), 16 * 2 * TT)
                    link(tt(XT[b][:, :, :], XT[b][:, :, :], TN[b][:, :, :], ALU.add))
                for g in range(NG):
                    dve.wait_ge(S(f"gathered{g}"), 16 * 2 * TG * (l * NB + b + 1))
                    for k in range(2):
                        for t in range(g * TG, (g + 1) * TG):
                            ins = nc.vector.scalar_tensor_tensor(XT[b][:, t, :], G[k][:, t, :], GATE[b][:, k, t:t + 1], XT[b][:, t, :], ALU.mult, ALU.add)
                        if k == 0:
                            link(ins)
                    if done:
                        ins.then_inc(S(done), 1)
                    elif g < NG - 1:
                        link(ins)
                    else:
                        ins.then_inc(S("combined"), 1)
                        dve.wait_ge(S("combined"), b + 1)

            def conv(b):
                combine(0, b)
                layer_norm(("X", b), b, 1e-6)

                def gn(n, chunks, gamma, beta):
                    for k, a in enumerate(chunks):
                        ins = nc.vector.bn_stats(GST[:, k, :], a)
                    link(ins)
                    link(nc.vector.bn_aggr(GV[:, 2:4], GST[:, 0:len(chunks), :]))
                    ts(GV[:, 0:1], GV[:, 2:3], 1.0, None, ALU.mult)
                    link(tt(GV[:, 4:5], GV[:, 2:3], GV[:, 2:3], ALU.mult))
                    tt(GV[:, 1:2], GV[:, 4:5], GV[:, 3:4], ALU.add).then_inc(S("gn_in"), 1)
                    dve.wait_ge(S("gn_sum"), n + 1)
                    nc.vector.tensor_copy(GV[:, 2:4], banks[1][:, 0:2]).then_inc(S("gn_read"), 1)
                    dve.wait_ge(S("gn_read"), n + 1)
                    link(tt(GV[:, 4:5], GV[:, 2:3], GV[:, 2:3], ALU.mult))
                    link(tt(GV[:, 5:6], GV[:, 3:4], GV[:, 4:5], ALU.subtract))
                    ts(GV[:, 5:6], GV[:, 5:6], 1e-5, None, ALU.add).then_inc(S("gn_var"), 1)
                    dve.wait_ge(S("gn_std"), n + 1)
                    link(nc.vector.reciprocal(GV[:, 9:10], GV[:, 6:7]))
                    link(tt(GV[:, 7:8], GV[:, 9:10], gamma, ALU.mult))
                    link(tt(GV[:, 10:11], GV[:, 2:3], GV[:, 7:8], ALU.mult))
                    tt(GV[:, 8:9], beta, GV[:, 10:11], ALU.subtract).then_inc(S("gn_coef"), 1)

                dve.wait_ge(S("hc_ready"), 2 * (b + 1))
                gn(3 * b, [HC[:, hh, :] for hh in range(2)], N1G, N1B)
                dve.wait_ge(S("conv2"), b + 1)
                dve.wait_ge(S("hp_ready"), b + 1)
                gn(3 * b + 1, [banks[4 + hh][:, 0:HALF] for hh in range(2)], NMG, NMB)
                link(tt(XT[b][:, :, :], XT[b][:, :, :], TN[b][:, :, :], ALU.add))
                dve.wait_ge(S("z_ready"), b + 1)
                dve.wait_ge(S("up_out"), 8 * (b + 1))
                gn(3 * b + 2, [CM[:, k * NT // 6:(k + 1) * NT // 6] for k in range(6)], N2G, N2B)
                for g in range(NG):
                    m = group_base[("z", "X", b)] + g
                    t_wait_full(dve, m)
                    xt = XT[b][:, g * TG:(g + 1) * TG, :]
                    tt(xt, xt, banks[m % 2][:, 0:TG * P].rearrange("p (t c) -> p t c", c=P), ALU.add).then_inc(S("t_free"), 1)
                dve.wait_ge(S("t_free"), group_base[("z", "X", b)] + NG)

            run(dve, lna=lna, att=att, route=route, moe=moe, conv=conv, fin=lambda b: combine(1, b, "out_ready"))


def constants():
    import numpy as np
    P, E, J, TT = 128, 16, 52, 18
    p = np.arange(P)
    j = np.arange(7)[:, None, None] + 1
    d = ((p[None, :, None] % 32) - np.arange(32)[None, None, :] + 4 == j)
    cols = [np.eye(P), p[:, None] < p[None, :], np.ones((P, P)),
            ((p[:, None] % 32) // 2 == (p[None, :] % 32) // 2) / 8.0, (p[:, None] // 8 == p[None, :] // 8) / 8.0,
            p[:, None] // 16 == np.arange(8)[None, :], (p[:, None] // 16) % 2 == np.arange(2)[None, :],
            p[:, None] % 32 == np.arange(32)[None, :], d.transpose(1, 0, 2).reshape(P, 224),
            np.broadcast_to(E - np.arange(E), (P, E)), np.broadcast_to(np.arange(J), (P, J)),
            np.broadcast_to(128 * np.arange(TT), (P, TT))]
    return np.ascontiguousarray(np.concatenate([np.asarray(c, np.float32) for c in cols], axis=1))


def kernel(**inputs):
    import numpy as np
    import concourse.bacc as _bacc
    from concourse import mybir as _mybir
    from concourse.bass_utils import run_bass_kernel_spmd as _run

    a = {k: np.asarray(v) for k, v in inputs.items()}
    P = 128
    x = a["x"].reshape(2, P, 12, 4, 12, 4).transpose(0, 2, 4, 3, 5, 1).reshape(2, 18, P, P).transpose(0, 2, 1, 3)
    qw, qb = a["L0_conv_qkv_w"].reshape(3, P), a["L0_conv_qkv_b"].reshape(3, P)
    rep = lambda v: np.tile(v, 4)
    params = np.stack([qw[0], qb[0], qw[1], qb[1], qw[2], qb[2], rep(a["L1_conv_conv1_b"]), rep(a["L1_conv_gn1_g"]), rep(a["L1_conv_gn1_b"]),
                       rep(a["L1_conv_gnm_g"]), rep(a["L1_conv_gnm_b"]), a["L1_conv_conv2_b"], a["L1_conv_gn2_g"], a["L1_conv_gn2_b"],
                       a["L1_conv_gn2_b"], a["L1_conv_gn2_b"]], axis=1)
    qi, qj, ki, kj = np.ix_(np.arange(4), np.arange(4), np.arange(8), np.arange(8))
    index = ((qi - ki + 7) * 15 + (qj - kj + 7)).reshape(16, 64)
    pos_bias = a["L0_conv_pos_table"][index].transpose(2, 0, 1).reshape(P, 64)
    w2 = a["L1_conv_W2"][:, 0]
    w2_rows = np.zeros((4, 32, 12, 9), np.float32)
    for r in range(4):
        for m in range(12):
            if 0 <= m - 3 + r < 9:
                w2_rows[r, :, m] = w2[:, m - 3 + r]
    bc = lambda v: np.broadcast_to(v, (P,) + v.shape)
    arrays = {
        "x_tok": x, "params": params, "consts": constants(), "pos_bias": pos_bias,
        "out_wT": a["L0_conv_out_w"].T, "conv1_wT": a["L1_conv_conv1_w"].T, "conv2_wT": np.tile(a["L1_conv_conv2_w"].T, (4, 1)),
        "w2_rows": w2_rows.reshape(P, 12, 9), "w1_conv": bc(a["L1_conv_W1"].reshape(9)),
        "router_wT": a["L0_ffn_router_w"].T, "gate_wT": a["L1_ffn_gate_w"], "gate_b": bc(a["L1_ffn_gate_b"]),
        "moe0_w1": a["L0_ffn_w1"].transpose(1, 0, 2), "moe0_w2": a["L0_ffn_w2"].transpose(1, 0, 2),
        "moe0_b1": bc(a["L0_ffn_b1"]), "moe0_b2": bc(a["L0_ffn_b2"]),
        "moe1_w12": np.concatenate([a["L1_ffn_w1"], a["L1_ffn_w2"]], axis=2).transpose(1, 0, 2),
        "moe1_w3": a["L1_ffn_w3"].reshape(16, 2, P, P).transpose(2, 0, 1, 3),
    }
    nc = _bacc.Bacc("TRN2", target_bir_lowering=False, num_devices=1)
    args = []
    for name in arrays:
        arrays[name] = np.ascontiguousarray(arrays[name])
        args.append(nc.dram_tensor("in_" + name, arrays[name].shape, _mybir.dt.from_np(arrays[name].dtype), kind="ExternalInput").ap())
    args.append(nc.dram_tensor("out", (2, P, 18, P), _mybir.dt.float32, kind="ExternalOutput").ap())
    metaformer_program(nc, *args)
    r = _run(nc, [{"in_" + k: v for k, v in arrays.items()}], core_ids=[0])
    y = np.asarray(r.results[0]["out"])
    return np.ascontiguousarray(y.transpose(0, 2, 1, 3).reshape(2, 12, 12, 4, 4, P).transpose(0, 5, 1, 3, 2, 4).reshape(2, P, 48, 48))
```

```python
import concourse.bass as bass
from concourse import mybir
from contextlib import ExitStack


def metaformer_program(nc, x_tok, params, consts, pos_bias, out_wT, conv1_wT, conv2_wT, w2_rows, w1_conv,
                       router_wT, gate_wT, gate_b, moe0_w1, moe0_w2, moe0_b1, moe0_b2, moe1_w12, moe1_w3, out):
    fp32 = mybir.dt.float32
    i32 = mybir.dt.int32
    ALU = mybir.AluOpType
    ACT = mybir.ActivationFunctionType
    AX = mybir.AxisListType.X
    ds = bass.ds

    P = 128
    NB = 2
    IMG = 48
    NT = IMG * IMG
    TT = NT // P
    HEADS, HD, WS, WK = 8, 16, 4, 8
    NW = IMG // WS
    HW_ = NW // 2
    STEPS = 2 * NW
    Q = WS * WS
    KEYS = WK * WK
    PADI = IMG + WK - WS
    TG = 3
    NG = TT // TG
    EX = (8, 16)
    RING = 4
    TILES = tuple(-(-((2 * NT + (P - 1) * e) // P) // RING) * RING for e in EX)
    EMAX = max(EX)
    JMAX = max(TILES)
    C4 = 32
    CB, CX = NW + 2, IMG + 8
    HALF = NT // 4 // 2
    KX, KA = 9, 3

    names = {}
    ctx = ExitStack()
    with ctx:
        def sb(name, shape, dt=fp32):
            return ctx.enter_context(nc.sbuf_tensor(name, shape, dt))

        def S(name):
            if name not in names:
                names[name] = ctx.enter_context(nc.semaphore(name))
            return names[name]

        banks = [ctx.enter_context(nc.psum_tensor(f"bank{i}", [P, 512], fp32)) for i in range(8)]

        xs_dram = [[nc.dram_tensor(f"sorted_x{l}{b}", (TILES[l] * P, P), fp32).ap() for b in range(NB)] for l in range(2)]
        ys_dram = [[nc.dram_tensor(f"sorted_y{l}{b}", (TILES[l] * P, P), fp32).ap() for b in range(NB)] for l in range(2)]

        XT = [sb(f"residual{b}", [P, TT, P]) for b in range(NB)]
        TN = [sb(f"normed{b}", [P, TT, P]) for b in range(NB)]
        QY = [sb(f"qy{b}", [P, NT]) for b in range(NB)]
        CM = sb("chan_major", [P, NT])
        big = sb("padded_or_w12", [P, EX[1] * 512 + 4 * RING * P])
        XPAD = [big[:, b * PADI * PADI:(b + 1) * PADI * PADI].rearrange("p (y x) -> p y x", x=PADI) for b in range(NB)]
        o = NB * PADI * PADI
        KROW, VROW = ([big[:, o + (2 * k + h) * WK * PADI:o + (2 * k + h + 1) * WK * PADI] for h in range(2)] for k in range(2))
        W12 = big[:, 0:EX[1] * 512].rearrange("p (e h) -> p e h", h=512)
        W3 = sb("w3", [P, EX[1], 2, P])
        W1E = sb("moe0_w1", [P, EX[0], P])
        W2E = sb("moe0_w2", [P, EX[0], P])
        B1E = sb("moe0_b1", [P, EX[0], P])
        B2E = sb("moe0_b2", [P, EX[0], P])
        gath = sb("gathered_or_att", [P, 2 * TT * P])
        G = [gath[:, k * TT * P:(k + 1) * TT * P].rearrange("p (t c) -> p t c", c=P) for k in range(2)]
        W = HW_ * KEYS
        QBD = [gath[:, h * HW_ * P // 2:(h + 1) * HW_ * P // 2].rearrange("p (w m) -> p w m", m=P // 2) for h in range(2)]
        o = HW_ * P
        SB_, PE_, PN_ = ([gath[:, o + (2 * k + h) * W:o + (2 * k + h + 1) * W] for h in range(2)] for k in range(3))
        att2 = sb("att2_or_moe", [P, 6 * W])
        o += 6 * W
        PTB = gath[:, o:o + 4 * W]
        PTS = [PTB[:, 2 * h * W:2 * (h + 1) * W].rearrange("p (n w m) -> p n w m", w=2, m=P) for h in range(2)]
        VTS = [att2[:, h * W:(h + 1) * W] for h in range(2)]
        OS = [att2[:, 2 * W + h * 192:2 * W + (h + 1) * 192].rearrange("p (a w q) -> p a w q", a=2, q=Q) for h in range(2)]
        TOEP = sb("toeplitz", [P, KA * KX, P])
        CON = sb("consts", [P, 5 * P + HEADS // 2 + 2 + 32 + 7 * 32 + EMAX + JMAX + TT + RING])
        IDN, TRI, ONE, G2, G8 = (CON[:, k * P:(k + 1) * P] for k in range(5))
        o = 5 * P
        HM, PAR, I32, DJ = CON[:, o:o + 4], CON[:, o + 4:o + 6], CON[:, o + 6:o + 38], CON[:, o + 38:o + 38 + 224]
        o += 38 + 224
        REV, JI, T128 = CON[:, o:o + EMAX], CON[:, o + EMAX:o + EMAX + JMAX], CON[:, o + EMAX + JMAX:o + EMAX + JMAX + TT]
        POW = CON[:, o + EMAX + JMAX + TT:o + EMAX + JMAX + TT + RING]
        PRM = sb("params", [P, 16])
        (QW, QB, KW, KB, VW, VB, C1B, N1G, N1B, NMG, NMB, C2B, N2G, N2B) = (PRM[:, k:k + 1] for k in range(14))
        QS = sb("q_scaled", [P, 2])
        BIAS = sb("pos_bias", [P, KEYS])
        OWT = sb("out_w", [P, P])
        OWP = sb("out_w_parity", [P, 2, P])
        C1W = sb("conv1_w", [P, C4])
        C2W = sb("conv2_w", [P, P])
        W2R = sb("conv_rows", [P, 12, KX])
        W1C = sb("conv_chan", [P, 9])
        BAND = sb("band", [P, 32])
        RW = [sb("router_w", [P, EX[0]]), sb("gate_w", [P, EX[1]])]
        GB = sb("gate_b", [P, EX[1]])
        MXS = sb("score_max", [P, 2, HW_])
        RSM = sb("prob_sum", [P, 2, HW_])
        RRC = sb("prob_rsum", [P, 2, HW_])
        STT = sb("ln_stats", [P, TT, 6])
        LNV = sb("ln_values", [P, 6, TT])
        RT = sb("route", [P, 6, EMAX * TT])
        RS = sb("route_small", [P, 8, EMAX])
        RV = sb("route_rows", [P, 4, TT])
        RV4 = sb("route_packed", [P, JMAX // RING])
        EJ = sb("expert_cmp", [P, EMAX * JMAX // 2])
        EPK = [[sb(f"experts_of_group{l}{b}", [P, TILES[l] // RING], i32) for b in range(NB)] for l in range(2)]
        POS = [sb(f"slot{b}", [P, 2, TT], i32) for b in range(NB)]
        GATE = [sb(f"gate{b}", [P, 2, TT]) for b in range(NB)]
        o = 0

        def carve(n, width):
            nonlocal o
            views = [att2[:, o + k * width:o + (k + 1) * width] for k in range(n)]
            o += n * width
            return views

        XTS, SG, HD_, HTS = carve(2, P), carve(2, 256), carve(2, 256), carve(2, 256)
        o = EX[1] * 512
        XG, YG = ([big[:, o + (2 * k + h) * RING * P:o + (2 * k + h + 1) * RING * P].rearrange("p (r c) -> p r c", c=P)
                   for h in range(2)] for k in range(2))
        XS, YS = ([g[h][:, r, :] for h in range(2) for r in range(RING)] for g in (XG, YG))
        ZER = sb("zeros", [P, 512])
        HC = sb("conv_mid", [P, 2, HALF])
        HP = sb("conv_padded", [P, CB, CX])
        GST = sb("gn_stats", [P, 6, 6])
        GV = sb("gn_values", [P, 12])

        def of_step(a, wy, hf):
            return a[:, :].rearrange("p (r w h q) -> p r w h q", w=HW_, h=2, q=Q)[:, ds(wy, 1), :, hf, :].rearrange("p r w q -> p (r w) q")

        block = ctx.enter_context(nc.Block())

        order = ([("LNA", b) for b in range(NB)] + [("ATT", b) for b in range(NB)] +
                 [("R", 0, b) for b in range(NB)] + [("M", 0, b) for b in range(NB)] +
                 [p for b in range(NB) for p in (("X", b), ("R", 1, b))] +
                 [("M", 1, b) for b in range(NB)] + [("F", b) for b in range(NB)])
        group_base, n_groups = {}, 0
        for ph in order:
            for tag in {"LNA": ("a",), "R": ("y", "r") if ph[1] == 0 else ("r",), "X": ("c", "z")}.get(ph[0], ()):
                group_base[(tag,) + ph] = n_groups
                n_groups += NG

        def t_wait_full(eng, n):
            eng.wait_ge(S("t_full"), n + 1)

        lns = [ph for ph in order if ph[0] in ("LNA", "R", "X")]

        def pe_group(pe, n, srcs, ident=IDN):
            if n >= 2:
                pe.wait_ge(S("t_free"), n - 1)
            for k, a in enumerate(srcs):
                ins = nc.tensor.transpose(banks[n % 2][:, k * P:(k + 1) * P], a, ident)
            ins.then_inc(S("t_full"), 1)

        def ln_no(ph):
            return lns.index(ph) + 1

        def through_buffer(l, h):
            return (TILES[l] // RING + 1 - h) // 2

        def ys_free(eng, l, b, j, r, h):
            if r == 0 and (not isinstance(j, int) or b or j // RING >= 2):
                eng.wait_ge(S(f"ys_out{l}{h}"), (j - RING * h) * (16 // (2 * RING)) + 16 * b * through_buffer(l, h))

        def run(eng, lna, att, route, moe, conv, fin=None):
            for ph in order:
                if ph[0] == "LNA":
                    lna(ph[1])
                elif ph[0] == "ATT":
                    att(ph[1])
                elif ph[0] == "R":
                    route(ph[1], ph[2])
                elif ph[0] == "M":
                    moe(ph[1], ph[2])
                elif ph[0] == "X":
                    conv(ph[1])
                elif fin:
                    fin(ph[1])

        def tile_groups(eng, l, b, step, lag, experts=True):
            J, E = TILES[l], EX[l]
            words = EPK[l][b]
            held = eng.alloc_register(name=f"word_before_{eng.engine.name}{l}{b}") if experts else None
            top = 16 ** RING - 1

            def group(q, h, first=False, last=False):
                prev = eng.snap(held, min_val=0, max_val=top) if experts and not first else None
                now = []

                def load():
                    if experts and not last and not now:
                        now.append(eng.value_load(words[0:1, ds(q, 1)], min_val=0, max_val=top))

                for r in range(RING if not last else lag):
                    def expert(k):
                        word, slot = (now[0], r - k) if k <= r else (prev, RING + r - k)
                        return (word >> (4 * slot)) & (E - 1) if slot else word & (E - 1)
                    step(q * RING + r, r, h, expert, load)
                if experts and not last:
                    eng.reg_mov(held, now[0])

            n = J // RING
            turns = (n - 2) // 2
            group(0, 0, first=True)
            group(1, 1)
            with eng.Fori(1, turns + 1) as turn:
                for h in range(2):
                    group(turn * 2 + h, h)
            for q in range(2 * turns + 2, n):
                group(q, q % 2)
            group(n, n % 2, last=True)

        @block.sync
        def _(sp):
            for b in range(NB):
                sp.dma_start(XT[b][:, :, :], x_tok[b]).then_inc(S(f"x_in{b}"), 16)
                if b == 0:
                    sp.dma_start(CON[:, :], consts).then_inc(S("consts_in"), 16)
                    sp.dma_start(PRM[:, :], params).then_inc(S("consts_in"), 16)
                    sp.dma_start(BIAS[:, :], pos_bias).then_inc(S("consts_in"), 16)
                    sp.dma_start(OWT[:, :], out_wT).then_inc(S("consts_in"), 16)
            for dst, src in ((C1W, conv1_wT), (C2W, conv2_wT), (W1C, w1_conv), (RW[0], router_wT), (RW[1], gate_wT), (GB, gate_b)):
                sp.dma_start(dst[:, :], src).then_inc(S("small_in"), 16)
            sp.dma_start(W2R[:, :, :], w2_rows).then_inc(S("small_in"), 16)
            sp.dma_start(W1E[:, :, :], moe0_w1).then_inc(S("moe0_in"), 16)
            sp.dma_start(W2E[:, :, :], moe0_w2).then_inc(S("moe0_in"), 16)
            sp.dma_start(B1E[:, :, :], moe0_b1).then_inc(S("moe0_in"), 16)
            sp.dma_start(B2E[:, :, :], moe0_b2).then_inc(S("moe0_in"), 16)
            sp.dma_start(W3[:, :, :, :], moe1_w3).then_inc(S("moe1_in"), 16)
            sp.wait_ge(S("zeros_set"), 1)
            for l in range(2):
                for b in range(NB):
                    v = xs_dram[l][b].rearrange("(n r p) c -> n p r c", p=P, r=RING)
                    for n in range(TILES[l] // RING):
                        sp.dma_start(v[n], ZER[:, :].rearrange("p (r c) -> p r c", c=P)).then_inc(S(f"sorted_zero{l}{b}"), 16)

            def moe(l, b):
                J = TILES[l]
                n = J // RING
                xs = xs_dram[l][b].rearrange("(q r p) c -> q p r c", p=P, r=RING)
                ys = ys_dram[l][b].rearrange("(q r p) c -> q p r c", p=P, r=RING)

                def load(q, h):
                    if not isinstance(q, int) or q >= 2:
                        sp.wait_ge(S(f"x_transposed{l}"), RING * (q - 1) + b * J)
                    elif b:
                        sp.wait_ge(S(f"x_transposed{l}"), b * J)
                    sp.dma_start(XG[h], xs[ds(q, 1)].rearrange("o p r c -> p (o r) c")).then_inc(S(f"xs_in{l}{h}"), 16)

                def store(q, h):
                    sp.wait_ge(S(f"y_ready{l}"), RING * (q + 1) + b * J)
                    sp.dma_start(ys[ds(q, 1)].rearrange("o p r c -> p (o r) c"), YG[h]).then_inc(S(f"ys_out{l}{h}"), 16)

                sp.wait_ge(S(f"scattered{l}{b}"), 16 * 2 * TT)
                for q in range(2):
                    load(q, q)
                turns = (n - 2) // 2
                with sp.Fori(0, turns) as turn:
                    for h in range(2):
                        load(turn * 2 + (2 + h), h)
                        store(turn * 2 + h, h)
                for q in range(2 * turns, n):
                    if q + 2 < n:
                        load(q + 2, q % 2)
                    store(q, q % 2)

            sp.wait_ge(S("attn_y"), NB * STEPS)
            sp.wait_ge(S("scores"), NB * STEPS)
            sp.wait_ge(S("v_transposed"), NB * STEPS)
            sp.wait_ge(S("v_row"), NB * NW)
            sp.dma_start(W12, moe1_w12).then_inc(S("moe1_in"), 16)
            moe(0, 0)
            moe(0, 1)
            moe(1, 0)
            moe(1, 1)
            for b in range(NB):
                for g in range(NG):
                    sp.wait_ge(S("out_ready"), b * NG + g + 1)
                    sp.dma_start(out[b, :, g * TG:(g + 1) * TG, :], XT[b][:, g * TG:(g + 1) * TG, :]).then_inc(S("out_stored"), 16)
            sp.wait_ge(S("out_stored"), 16 * NB * NG)

        @block.gpsimd
        def _(pool):
            nc.gpsimd.memset(ZER[:, :], 0.0).then_inc(S("zeros_set"), 1)
            nc.gpsimd.memset(HP[:, :, :], 0.0).then_inc(S("pad_zero"), 1)
            nc.gpsimd.memset(PTB, 0.0).then_inc(S("pt_zero"), 1)
            pool.wait_ge(S("consts_in"), 64)
            for b in range(NB):
                def step(s, hf, wy, last):
                    g = s + b * STEPS
                    if last >= 1:
                        if not isinstance(s, int) or g >= 2:
                            pool.wait_ge(S("scores"), g - 1)
                        out_ = QBD[hf].rearrange("p w (h q) -> p w h q", q=Q)
                        q_ = of_step(QY[b], wy, hf)
                        nc.gpsimd.tensor_tensor(out_, q_.unsqueeze(2).broadcast_to([P, HW_, HEADS // 2, Q]),
                                                HM.unsqueeze(1).unsqueeze(3).broadcast_to([P, HW_, HEADS // 2, Q]),
                                                ALU.mult).then_inc(S("qbd"), 1)

                def norm(s, hf):
                    g = s + b * STEPS
                    pool.wait_ge(S("rsum"), g + 1)
                    if not isinstance(s, int) or g >= 2:
                        pool.wait_ge(S("p_transposed"), g - 1)
                    pn = PN_[hf].rearrange("p (w k) -> p w k", k=KEYS)
                    pe_ = PE_[hf].rearrange("p (w k) -> p w k", k=KEYS)
                    nc.gpsimd.tensor_tensor(pn, pe_, RRC[:, hf, :].unsqueeze(2).broadcast_to([P, HW_, KEYS]), ALU.mult).then_inc(S("probs"), 1)

                pool.wait_ge(S("q_ready"), NG * (b + 1))
                step(0, 0, 0, 1)
                step(1, 1, 0, 1)
                step(2, 0, 1, 1)
                norm(0, 0)
                step(3, 1, 1, 1)
                norm(1, 1)
                with pool.Fori(2, NW) as i:
                    step(2 * i, 0, i, 1)
                    norm(2 * i - 2, 0)
                    step(2 * i + 1, 1, i, 1)
                    norm(2 * i - 1, 1)
                norm(STEPS - 2, 0)
                norm(STEPS - 1, 1)

            def scatter(l, b):
                pool.wait_ge(S(f"routed{l}{b}"), 1)
                pool.wait_ge(S(f"sorted_zero{l}{b}"), 16 * (TILES[l] // RING))
                for t in range(TT):
                    for k in range(2):
                        nc.gpsimd.indirect_dma_start(xs_dram[l][b], bass.IndirectOffsetOnAxis(ap=POS[b][:, k, t:t + 1], axis=0),
                                                     TN[b][:, t, :], None).then_inc(S(f"scattered{l}{b}"), 16)

            def gather(l, b):
                n = l * NB + b
                for h in range(2):
                    pool.wait_ge(S(f"ys_out{l}{h}"), 16 * (b + 1) * through_buffer(l, h))
                if n == 3:
                    pool.wait_ge(S("out_ready"), NG)
                elif n:
                    pool.wait_ge(S("combined"), n)
                for t in range(TT):
                    for k in range(2):
                        nc.gpsimd.indirect_dma_start(G[k][:, t, :], None, ys_dram[l][b],
                                                     bass.IndirectOffsetOnAxis(ap=POS[b][:, k, t:t + 1], axis=0)
                                                     ).then_inc(S(f"gathered{t // TG}"), 16)

            scatter(0, 0)
            scatter(0, 1)
            gather(0, 0)
            gather(0, 1)
            scatter(1, 0)
            scatter(1, 1)
            gather(1, 0)
            gather(1, 1)

        @block.tensor
        def _(pe):
            def lna(b):
                pe.wait_ge(S("ln_done"), ln_no(("LNA", b)))
                for g in range(NG):
                    pe_group(pe, group_base[("a", "LNA", b)] + g, [TN[b][:, g * TG + k, :] for k in range(TG)])

            def att(b):
                if b == 0:
                    pe.wait_ge(S("t_free"), NB * NG)
                    pe.wait_ge(S("pt_zero"), 1)

                def scores(s, hf, wy, par):
                    g = s + b * STEPS
                    if isinstance(s, int):
                        pe.wait_ge(S("k_row"), wy + 1 + b * NW)
                        pe.wait_ge(S("qbd"), g + 1)
                    if isinstance(s, int) and s < 6 and g >= 2:
                        pe.wait_ge(S("biased"), g - 1)
                    for w in range(HW_):
                        k0 = (2 * w + hf) * WS * WK
                        for c in (slice(0, P // 2), slice(P // 2, P)):
                            ins = nc.tensor.matmul(banks[2 + hf][c, w * KEYS:(w + 1) * KEYS], QBD[hf][c, w, :],
                                                   KROW[par][c, k0:k0 + KEYS], start=True, stop=True)
                    ins.then_inc(S("scores"), 1)

                def transposes(s, hf, wy, par, next_wy=None):
                    g = s + b * STEPS
                    pe.wait_ge(S("probs"), g + 1)
                    for p in range(HW_ // 2):
                        ins = nc.tensor.transpose(banks[5][:, p * P:(p + 1) * P], PN_[hf][:, p * P:(p + 1) * P], IDN)
                    ins.then_inc(S("p_transposed"), 1)
                    if hf == 0:
                        pe.wait_ge(S("v_row"), wy + 1 + b * NW)
                    if next_wy is not None:
                        if hf == 1:
                            pe.wait_ge(S("k_row"), next_wy + 1 + b * NW)
                        pe.wait_ge(S("qbd"), g + 4)
                    for p in range(HW_ // 2):
                        k0 = (4 * p + hf) * WS * WK
                        ins = nc.tensor.transpose(banks[0][:, p * P:(p + 1) * P], VROW[par][:, k0:k0 + P], IDN)
                    ins.then_inc(S("v_transposed"), 1)

                def weigh(s, hf):
                    g = s + b * STEPS
                    pe.wait_ge(S("edge"), b + 1)
                    pe.wait_ge(S("vt_out"), g + 1)
                    for p in range(HW_ // 2):
                        for j in range(4):
                            m = slice(32 * j, 32 * j + 32)
                            ins = nc.tensor.matmul(banks[6 + hf][m, p * 64:(p + 1) * 64], VTS[hf][:, p * P + 32 * j:p * P + 32 * j + 32],
                                                   PTS[hf][:, p, :, m], start=True, stop=True)
                    ins.then_inc(S("weighed"), 1)

                def project(s, hf):
                    g = s + b * STEPS
                    pe.wait_ge(S("o_out"), g + 1)
                    if not isinstance(s, int) or g >= 1:
                        pe.wait_ge(S("attn_y"), g)
                    for a in range(2):
                        ins = nc.tensor.matmul(banks[1][:, 0:HW_ * Q], OWP[:, a, :], OS[hf][:, a, :, :].rearrange("p w q -> p (w q)"),
                                               start=(a == 0), stop=(a == 1))
                    ins.then_inc(S("projected"), 1)

                def step(s, c, wy, isint):
                    hf = c % 2
                    if not isint or s >= 3 and s - 3 < STEPS:
                        transposes(s - 3, 1 - hf, wy - 2 + c % 2, (c + 1) % 4 // 2, None if isint else wy)
                    if not isint or s < STEPS:
                        scores(s, hf, wy, c // 2)
                    if not isint or s >= 4 and s - 4 < STEPS:
                        project(s - 4, hf)
                    if not isint or s >= 3 and s - 3 < STEPS:
                        weigh(s - 3, 1 - hf)

                for s in range(4):
                    step(s, s % 4, s // 2, True)
                with pe.Fori(1, NW // 2) as i:
                    for c in range(4):
                        step(4 * i + c, c, 2 * i + c // 2, False)
                for s in range(STEPS, STEPS + 4):
                    step(s, s % 4, s // 2, True)

            def route(l, b):
                if l == 0:
                    for g in range(NG):
                        if g == 0:
                            pe.wait_ge(S("attn_y"), NB * STEPS)
                            pe.wait_ge(S("o_out"), NB * STEPS)
                            pe.wait_ge(S("vt_out"), NB * STEPS)
                        pe_group(pe, group_base[("y", "R", 0, b)] + g, [QY[b][:, (g * TG + k) * P:(g * TG + k + 1) * P] for k in range(TG)])
                pe.wait_ge(S("ln_done"), ln_no(("R", l, b)))
                for g in range(NG):
                    pe_group(pe, group_base[("r", "R", l, b)] + g, [TN[b][:, g * TG + k, :] for k in range(TG)])
                E = EX[l]
                pe.wait_ge(S("t_free"), group_base[("r", "R", l, b)] + NG)
                if l == 0 and b == 0:
                    pe.wait_ge(S("small_in"), 16 * 7)
                for t in range(TT):
                    ins = nc.tensor.matmul(banks[2][:, t * E:(t + 1) * E], CM[:, t * P:(t + 1) * P], RW[l][:, :], start=True, stop=True)
                ins.then_inc(S("logits"), 1)
                n = l * NB + b
                pe.wait_ge(S("chosen"), n + 1)
                nc.tensor.matmul(banks[6][:, 0:TT * E], TRI, RT[:, 5, 0:TT * E], start=True, stop=True)
                nc.tensor.matmul(banks[7][:, 0:TT * E], ONE, RT[:, 5, 0:TT * E], start=True, stop=True).then_inc(S("prefix"), 1)

            def moe(l, b):
                J = TILES[l]
                if b == 0:
                    pe.wait_ge(S("moe0_in" if l == 0 else "moe1_in"), 64 if l == 0 else 32)
                    pe.wait_ge(S("t_free"), max(v for k, v in group_base.items() if k[1:3] == ("R", l)) + NG)
                pe.wait_ge(S(f"routed{l}{b}"), 1)
                IN = 2 * P if l else P

                def tx(j, r, h):
                    if r == 0:
                        pe.wait_ge(S(f"xs_in{l}{h}"), (j - RING * h) * (16 // (2 * RING)) + 16 * (1 + b * through_buffer(l, h)))
                    if not isinstance(j, int) or b or j >= 2:
                        pe.wait_ge(S(f"xt_out{l}"), j - 1 + b * J)
                    nc.tensor.transpose(banks[r % 2][:, 0:P], XS[h * RING + r], IDN).then_inc(S(f"x_transposed{l}"), 1)

                def hid(j, r, e):
                    pe.wait_ge(S(f"xt_out{l}"), j + 1 + b * J)
                    if not isinstance(j, int) or b or j >= 2:
                        pe.wait_ge(S("hid1" if l else "h_free0"), j - 1 + b * J)
                    w = W12 if l else W1E
                    nc.tensor.matmul(banks[2 + r % 2][:, 0:(512 if l else P)], XTS[r % 2][:, :],
                                     w[:, ds(e, 1), :], start=True, stop=True).then_inc(S(f"h_full{l}"), 1)

                def th(j, r):
                    pe.wait_ge(S(f"hid{l}"), j + 1 + b * J)
                    if not isinstance(j, int) or b or j >= 2:
                        pe.wait_ge(S(f"ht_out{l}"), j - 1 + b * J)
                    for a in range(IN // P):
                        ins = nc.tensor.transpose(banks[4 + r % 2][:, a * P:(a + 1) * P], HD_[r % 2][:, a * P:(a + 1) * P], IDN)
                    ins.then_inc(S(f"ht_full{l}"), 1)

                def ym(j, r, e):
                    if isinstance(j, int) and j == 0 and b == 0:
                        pe.wait_ge(S(f"routed{l}1"), 1)
                    pe.wait_ge(S(f"ht_out{l}"), j + 1 + b * J)
                    if not isinstance(j, int) or b or j >= 2:
                        pe.wait_ge(S(f"y_ready{l}"), j - 1 + b * J)
                    for a in range(IN // P):
                        rhs = W3[:, ds(e, 1), a, :] if l else W2E[:, ds(e, 1), :]
                        ins = nc.tensor.matmul(banks[6 + r % 2][:, 0:P], HTS[r % 2][:, a * P:(a + 1) * P], rhs,
                                               start=(a == 0), stop=(a == IN // P - 1))
                    ins.then_inc(S(f"y_full{l}"), 1)

                def step(j, r, h, expert, load):
                    ok = lambda k: not isinstance(j, int) or 0 <= j - k < J
                    if ok(0):
                        tx(j, r, h)
                    if ok(3):
                        th(j - 3, (r + 1) % RING)
                    if ok(1):
                        hid(j - 1, (r + 3) % RING, expert(1))
                    if r == 0:
                        load()
                    if ok(4):
                        ym(j - 4, r, expert(4))

                tile_groups(pe, l, b, step, 4)

            def conv(b):
                pe.wait_ge(S("ln_done"), ln_no(("X", b)))
                if b == 0:
                    pe.wait_ge(S("xt_out0"), NB * TILES[0])
                for g in range(NG):
                    pe_group(pe, group_base[("c", "X", b)] + g, [TN[b][:, g * TG + k, :] for k in range(TG)])
                pe.wait_ge(S("t_free"), group_base[("c", "X", b)] + NG)
                if b == 0:
                    pe.wait_ge(S("h_free0"), NB * TILES[0])
                    pe.wait_ge(S("ht_out0"), NB * TILES[0])
                    pe.wait_ge(S("y_ready0"), NB * TILES[0])
                xin = QY[b][:, :].rearrange("p (n y x) -> p n y x", y=WS, x=WS)
                for hh in range(2):
                    for r in range(4):
                        ins = nc.tensor.matmul(banks[2 + hh][32 * r:32 * r + 32, 0:HALF], C1W[:, :],
                                               xin[:, hh * NW * NW // 2:(hh + 1) * NW * NW // 2, r, :], start=True, stop=True)
                ins.then_inc(S("conv1"), 1)

                def group_stats(mat, n):
                    pe.wait_ge(S("gn_in"), n + 1)
                    nc.tensor.matmul(banks[1][:, 0:2], mat, GV[:, 0:2], start=True, stop=True).then_inc(S("gn_sum"), 1)

                group_stats(G2, 3 * b)
                pe.wait_ge(S("hp_ready"), b + 1)
                if b == 0:
                    pe.wait_ge(S("toeplitz"), 1)
                for hh in range(2):
                    for n in range(KA * KX):
                        a, kx = divmod(n, KX)
                        ins = nc.tensor.matmul(banks[4 + hh][:, 0:HALF], TOEP[:, n, :],
                                               HP[:, hh * NW // 2 + a:hh * NW // 2 + a + NW // 2, kx:kx + IMG],
                                               start=(n == 0), stop=(n == KA * KX - 1))
                ins.then_inc(S("conv2"), 1)
                group_stats(G2, 3 * b + 1)
                pe.wait_ge(S("z_ready"), b + 1)
                for n in range(8):
                    r, hh = divmod(n, 2)
                    if n >= 4:
                        pe.wait_ge(S("up_out"), b * 8 + n - 3)
                    elif n == 0 and b:
                        pe.wait_ge(S("up_out"), 8 * b)
                    nc.tensor.matmul(banks[(2, 3, 6, 7)[n % 4]][:, 0:HALF], C2W[32 * r:32 * r + 32, :], HC[32 * r:32 * r + 32, hh, :],
                                     start=True, stop=True).then_inc(S("up"), 1)
                group_stats(G8, 3 * b + 2)
                pe.wait_ge(S("z3_ready"), b + 1)
                for g in range(NG):
                    if g == 0:
                        pe.wait_ge(S("gn_read"), 3 * b + 3)
                    pe_group(pe, group_base[("z", "X", b)] + g, [QY[b][:, (g * TG + k) * P:(g * TG + k + 1) * P] for k in range(TG)])

            run(pe, lna=lna, att=att, route=route, moe=moe, conv=conv)

        @block.scalar
        def _(act):
            def sqrt_of(ph):
                act.wait_ge(S("ln_var"), ln_no(ph))
                nc.scalar.activation(LNV[:, 4, :], LNV[:, 3, :], ACT.Sqrt).then_inc(S("ln_std"), 1)

            def evac(tag, ph, dst, sem="t_free"):
                for g in range(NG):
                    n = group_base[(tag,) + ph] + g
                    t_wait_full(act, n)
                    nc.scalar.activation(dst[:, g * TG * P:(g + 1) * TG * P], banks[n % 2][:, 0:TG * P], ACT.Copy).then_inc(S(sem), 1)

            def lna(b):
                sqrt_of(("LNA", b))
                if b == 0:
                    act.wait_ge(S("q_scaled"), 1)
                for g in range(NG):
                    n = group_base[("a", "LNA", b)] + g
                    t_wait_full(act, n)
                    src = banks[n % 2][:, 0:TG * P]
                    nc.scalar.activation(QY[b][:, g * TG * P:(g + 1) * TG * P], src, ACT.Identity, bias=QS[:, 1:2], scale=QS[:, 0:1]).then_inc(S("q_ready"), 1)
                    sw = src.rearrange("p (v w y x) -> p v w y x", v=2, y=WS, x=WS)
                    for v in range(2):
                        y0 = (2 * g + v) * WS
                        ins = nc.scalar.activation(XPAD[b][:, y0:y0 + WS, 0:IMG].rearrange("p y (w x) -> p w y x", x=WS), sw[:, v], ACT.Copy)
                    ins.then_inc(S("t_free"), 1)

            def att(b):
                def keys(row, par):
                    act.wait_ge(S("edge"), b + 1)
                    if not isinstance(row, int) or b or row >= 2:
                        act.wait_ge(S("scores"), 2 * (row - 1) + b * STEPS)
                    nc.scalar.activation(KROW[par].rearrange("p (x y) -> p y x", y=WK), XPAD[b][:, ds(row * WS, WK), :], ACT.Identity, bias=KB, scale=KW).then_inc(S("k_row"), 1)

                def values(row, par):
                    act.wait_ge(S("edge"), b + 1)
                    if not isinstance(row, int) or b or row >= 2:
                        act.wait_ge(S("v_transposed"), 2 * (row - 1) + b * STEPS)
                    nc.scalar.activation(VROW[par].rearrange("p (x y) -> p y x", y=WK), XPAD[b][:, ds(row * WS, WK), :], ACT.Identity, bias=VB, scale=VW).then_inc(S("v_row"), 1)

                def expo(s, hf):
                    g = s + b * STEPS
                    act.wait_ge(S("shifted"), g + 1)
                    if not isinstance(s, int) or g >= 2:
                        act.wait_ge(S("probs"), g - 1)
                    nc.scalar.activation(PE_[hf], SB_[hf], ACT.Exp).then_inc(S("exps"), 1)

                def outs(s, hf):
                    g = s + b * STEPS
                    act.wait_ge(S("p_transposed"), g + 1)
                    if not isinstance(s, int) or g >= 2:
                        act.wait_ge(S("weighed"), g - 1)
                    for wl in range(2):
                        k = slice(KEYS * wl, KEYS * (wl + 1))
                        ins = nc.scalar.activation(PTS[hf][k, :, wl, :], banks[5][k, 0:W].rearrange("p (n m) -> p n m", m=P), ACT.Copy)
                    ins.then_inc(S("pt_out"), 1)
                    act.wait_ge(S("v_transposed"), g + 1)
                    nc.scalar.activation(VTS[hf], banks[0][:, 0:W], ACT.Copy).then_inc(S("vt_out"), 1)

                def step(s, c, wy, isint, last=False):
                    hf = c % 2
                    if not isint or s >= 3 and s - 3 < STEPS:
                        outs(s - 3, 1 - hf)
                    if not isint or 1 <= s <= STEPS:
                        expo(s - 1, 1 - hf)
                    if hf == 0 and not last:
                        keys(wy + 1, 1 - c // 2)
                    if hf == 1 and (not isint or s < STEPS):
                        values(wy, c // 2)

                act.wait_ge(S("edge"), b + 1)
                keys(0, 0)
                for s in range(4):
                    step(s, s % 4, s // 2, True)
                with act.Fori(1, NW // 2 - 1) as i:
                    for c in range(4):
                        step(4 * i + c, c, 2 * i + c // 2, False)
                for s in range(STEPS - 4, STEPS + 4):
                    step(s, s % 4, s // 2, True, s >= STEPS - 2)

            def route(l, b):
                ph = ("R", l, b)
                sqrt_of(ph)
                if l == 1 or b == 1:
                    act.wait_ge(S("logits"), l * NB + b)
                if l == 1:
                    act.wait_ge(S("z3_ready"), b + 1)
                evac("r", ph, CM)
                n = l * NB + b
                act.wait_ge(S("logit_shift"), n + 1)
                nc.scalar.activation(RT[:, 1, 0:TT * EX[l]], RT[:, 0, 0:TT * EX[l]], ACT.Exp).then_inc(S("logit_exp"), 1)

            def moe(l, b):
                J = TILES[l]

                def xt(j, r):
                    act.wait_ge(S(f"x_transposed{l}"), j + 1 + b * J)
                    if not isinstance(j, int) or b or j >= 2:
                        act.wait_ge(S(f"h_full{l}"), j - 1 + b * J)
                    nc.scalar.activation(XTS[r % 2][:, :], banks[r % 2][:, 0:P], ACT.Copy).then_inc(S(f"xt_out{l}"), 1)

                def nonlin(j, r):
                    if l:
                        act.wait_ge(S("h_full1"), j + 1 + b * J)
                        if not isinstance(j, int) or b or j >= 2:
                            act.wait_ge(S("hid1"), j - 1 + b * J)
                        nc.scalar.activation(SG[r % 2][:, :], banks[2 + r % 2][:, 0:256], ACT.Silu).then_inc(S("silu"), 1)
                    else:
                        act.wait_ge(S("h_free0"), j + 1 + b * J)
                        if not isinstance(j, int) or b or j >= 2:
                            act.wait_ge(S("ht_full0"), j - 1 + b * J)
                        nc.scalar.activation(HD_[r % 2][:, 0:P], SG[r % 2][:, 0:P], ACT.Gelu).then_inc(S("hid0"), 1)

                def tail(j, r, h=None):
                    if l:
                        act.wait_ge(S("y_full1"), j + 1 + b * J)
                        ys_free(act, 1, b, j, r, h)
                        nc.scalar.activation(YS[h * RING + r], banks[6 + r % 2][:, 0:P], ACT.Copy).then_inc(S("y_ready1"), 1)
                    else:
                        act.wait_ge(S("ht_full0"), j + 1 + b * J)
                        if not isinstance(j, int) or b or j >= 2:
                            act.wait_ge(S("y_full0"), j - 1 + b * J)
                        nc.scalar.activation(HTS[r % 2][:, 0:P], banks[4 + r % 2][:, 0:P], ACT.Copy).then_inc(S("ht_out0"), 1)

                def step(j, r, h, expert, load):
                    ok = lambda k: not isinstance(j, int) or 0 <= j - k < J
                    if ok(0):
                        xt(j, r)
                    if not l and ok(3):
                        tail(j - 3, (r + 1) % RING)
                    if ok(1):
                        nonlin(j - 1, (r + 3) % RING)
                    if l and ok(4):
                        tail(j - 4, r, 1 - h)

                tile_groups(act, l, b, step, 4, experts=False)

            def conv(b):
                sqrt_of(("X", b))
                evac("c", ("X", b), QY[b])

                def gn_sqrt(n):
                    act.wait_ge(S("gn_var"), n + 1)
                    nc.scalar.activation(GV[:, 6:7], GV[:, 5:6], ACT.Sqrt).then_inc(S("gn_std"), 1)

                act.wait_ge(S("conv1"), b + 1)
                for hh in range(2):
                    nc.scalar.activation(HC[:, hh, :], banks[2 + hh][:, 0:HALF], ACT.Identity, bias=C1B).then_inc(S("hc_ready"), 1)
                gn_sqrt(3 * b)
                act.wait_ge(S("gn_coef"), 3 * b + 1)
                act.wait_ge(S("pad_zero"), 1)
                for hh in range(2):
                    ins = nc.scalar.activation(HP[:, 1 + hh * NW // 2:1 + (hh + 1) * NW // 2, 4:4 + IMG], HC[:, hh, :].rearrange("p (a x) -> p a x", x=IMG),
                                               ACT.Identity, bias=GV[:, 8:9], scale=GV[:, 7:8])
                ins.then_inc(S("hp_ready"), 1)
                gn_sqrt(3 * b + 1)
                act.wait_ge(S("gn_coef"), 3 * b + 2)
                for hh in range(2):
                    ins = nc.scalar.activation(HC[:, hh, :], banks[4 + hh][:, 0:HALF], ACT.Relu, bias=GV[:, 8:9], scale=GV[:, 7:8])
                ins.then_inc(S("z_ready"), 1)
                cm = CM[:, :].rearrange("p (n y x) -> p n y x", y=WS, x=WS)
                for n in range(8):
                    r, hh = divmod(n, 2)
                    act.wait_ge(S("up"), b * 8 + n + 1)
                    nc.scalar.activation(cm[:, hh * NW * NW // 2:(hh + 1) * NW * NW // 2, r, :],
                                         banks[(2, 3, 6, 7)[n % 4]][:, 0:HALF].rearrange("p (n x) -> p n x", x=WS),
                                         ACT.Identity, bias=C2B).then_inc(S("up_out"), 1)
                gn_sqrt(3 * b + 2)
                act.wait_ge(S("gn_coef"), 3 * b + 3)
                nc.scalar.activation(QY[b][:, :], CM[:, :], ACT.Relu, bias=GV[:, 8:9], scale=GV[:, 7:8]).then_inc(S("z3_ready"), 1)

            act.wait_ge(S("consts_in"), 64)
            run(act, lna=lna, att=att, route=route, moe=moe, conv=conv)

        @block.vector
        def _(dve):
            chain = [0]

            def link(ins):
                chain[0] += 1
                ins.then_inc(S("dve_chain"), 1)
                dve.wait_ge(S("dve_chain"), chain[0])

            tt, ts = nc.vector.tensor_tensor, nc.vector.tensor_scalar

            def layer_norm(ph, b, eps):
                for t in range(TT):
                    ins = nc.vector.bn_stats(STT[:, t, :], XT[b][:, t, :])
                link(ins)
                me, ve, mo, vo = (STT[:, :, k] for k in (1, 2, 4, 5))
                tt(LNV[:, 0, :], me, mo, ALU.add)
                tt(LNV[:, 1, :], me, mo, ALU.subtract)
                link(tt(LNV[:, 2, :], ve, vo, ALU.add))
                ts(LNV[:, 0, :], LNV[:, 0, :], 0.5, None, ALU.mult)
                link(tt(LNV[:, 1, :], LNV[:, 1, :], LNV[:, 1, :], ALU.mult))
                link(nc.vector.scalar_tensor_tensor(LNV[:, 3, :], LNV[:, 1, :], float(P // 4), LNV[:, 2, :], ALU.mult, ALU.add))
                ts(LNV[:, 3, :], LNV[:, 3, :], 1.0 / P, eps, ALU.mult, ALU.add).then_inc(S("ln_var"), 1)
                dve.wait_ge(S("ln_std"), ln_no(ph))
                link(nc.vector.reciprocal(LNV[:, 5, :], LNV[:, 4, :]))
                for t in range(TT):
                    ins = ts(TN[b][:, t, :], XT[b][:, t, :], LNV[:, 0, t:t + 1], LNV[:, 5, t:t + 1], ALU.subtract, ALU.mult)
                ins.then_inc(S("ln_done"), 1)

            def lna(b):
                dve.wait_ge(S(f"x_in{b}"), 16)
                if b == 0:
                    dve.wait_ge(S("consts_in"), 64)
                    ts(QS[:, 0:1], QW, HD ** -0.5, None, ALU.mult)
                    ts(QS[:, 1:2], QB, HD ** -0.5, None, ALU.mult).then_inc(S("q_scaled"), 1)
                    for a in range(2):
                        ins = ts(OWP[:, a, :], OWT[:, :], PAR[:, a:a + 1], None, ALU.mult)
                    link(ins)
                layer_norm(("LNA", b), b, 1e-6)
                if b == 0:
                    dve.wait_ge(S("small_in"), 16 * 7)
                    for a in range(KA):
                        for r in range(4):
                            tt(TOEP[:, a * KX:(a + 1) * KX, 32 * r:32 * r + 32], I32.unsqueeze(1).broadcast_to([P, KX, 32]),
                               W2R[:, 4 * a - r + 3, :].unsqueeze(2).broadcast_to([P, KX, 32]), ALU.mult)
                    link(ts(BAND[:, :], DJ[:, 0:32], W1C[:, 1:2], None, ALU.mult))
                    for j in range(1, 7):
                        link(nc.vector.scalar_tensor_tensor(BAND[:, :], DJ[:, 32 * j:32 * j + 32], W1C[:, j + 1:j + 2], BAND[:, :], ALU.mult, ALU.add))
                    for r in range(4):
                        blk = TOEP[32 * r:32 * r + 32, KX + KX // 2, 32 * r:32 * r + 32]
                        ins = tt(blk, blk, BAND[32 * r:32 * r + 32, :], ALU.add)
                    ins.then_inc(S("toeplitz"), 1)
                dve.wait_ge(S("t_free"), group_base[("a", "LNA", b)] + NG)
                link(nc.vector.tensor_copy(XPAD[b][:, 0:IMG, IMG:PADI], XPAD[b][:, 0:IMG, IMG - 1:IMG].broadcast_to([P, IMG, PADI - IMG])))
                nc.vector.tensor_copy(XPAD[b][:, IMG:PADI, :], XPAD[b][:, IMG - 1:IMG, :].broadcast_to([P, PADI - IMG, PADI])).then_inc(S("edge"), 1)

            def att(b):
                def three(ap):
                    return ap.rearrange("p (w k) -> p w k", k=KEYS)

                def top(s, hf):
                    g = s + b * STEPS
                    dve.wait_ge(S("scores"), g + 1)
                    if not isinstance(s, int) or g >= 2:
                        dve.wait_ge(S("exps"), g - 1)
                    tt(three(SB_[hf]), three(banks[2 + hf][:, 0:W]), BIAS[:, :].unsqueeze(1).broadcast_to([P, HW_, KEYS]), ALU.add).then_inc(S("biased"), 1)
                    dve.wait_ge(S("biased"), g + 1)
                    nc.vector.tensor_reduce(MXS[:, hf, :], three(SB_[hf]), AX, ALU.max).then_inc(S("maxed"), 1)
                    dve.wait_ge(S("maxed"), g + 1)
                    tt(three(SB_[hf]), three(SB_[hf]), MXS[:, hf, :].unsqueeze(2).broadcast_to([P, HW_, KEYS]), ALU.subtract).then_inc(S("shifted"), 1)

                def sums(s, hf):
                    g = s + b * STEPS
                    dve.wait_ge(S("exps"), g + 1)
                    nc.vector.tensor_reduce(RSM[:, hf, :], three(PE_[hf]), AX, ALU.add).then_inc(S("summed"), 1)
                    dve.wait_ge(S("summed"), g + 1)
                    if not isinstance(s, int) or g >= 2:
                        dve.wait_ge(S("probs"), g - 1)
                    nc.vector.reciprocal(RRC[:, hf, :], RSM[:, hf, :]).then_inc(S("rsum"), 1)

                def o_out(s, hf):
                    g = s + b * STEPS
                    dve.wait_ge(S("weighed"), g + 1)
                    if not isinstance(s, int) or g >= 2:
                        dve.wait_ge(S("projected"), g - 1)
                    nc.vector.tensor_copy(OS[hf].rearrange("p a w q -> p w a q"),
                                          banks[6 + hf][:, 0:192].rearrange("p (w a q) -> p w a q", a=2, q=Q)).then_inc(S("o_out"), 1)

                def y_out(s, hf, wy):
                    g = s + b * STEPS
                    dve.wait_ge(S("projected"), g + 1)
                    nc.vector.tensor_copy(of_step(QY[b], wy, hf), banks[1][:, 0:HW_ * Q].rearrange("p (n q) -> p n q", q=Q)).then_inc(S("attn_y"), 1)

                def step(s, hf, wy, isint):
                    if not isint or s >= 5 and s - 5 < STEPS:
                        y_out(s - 5, 1 - hf, wy - 3 + hf)
                    if not isint or s >= 4 and s - 4 < STEPS:
                        o_out(s - 4, hf)
                    if not isint or s < STEPS:
                        top(s, hf)
                    if not isint or 1 <= s <= STEPS:
                        sums(s - 1, 1 - hf)

                for s in range(6):
                    step(s, s % 2, s // 2, True)
                with dve.Fori(3, NW) as i:
                    step(2 * i, 0, i, False)
                    step(2 * i + 1, 1, i, False)
                for s in range(STEPS, STEPS + 5):
                    step(s, s % 2, s // 2, True)

            def route(l, b):
                E, ph, n, J = EX[l], ("R", l, b), l * NB + b, TILES[l]
                c = TT * E
                if l == 0:
                    for g in range(NG):
                        m = group_base[("y",) + ph] + g
                        t_wait_full(dve, m)
                        xt = XT[b][:, g * TG:(g + 1) * TG, :]
                        tt(xt, xt, banks[m % 2][:, 0:TG * P].rearrange("p (t c) -> p t c", c=P), ALU.add).then_inc(S("t_free"), 1)
                    dve.wait_ge(S("t_free"), group_base[("y",) + ph] + NG)
                layer_norm(ph, b, 1e-5)
                row = lambda k: RT[:, k, 0:c].rearrange("p (t e) -> p t e", e=E)
                over_e = lambda v: v.unsqueeze(2).broadcast_to([P, TT, E])
                over_t = lambda v: v.unsqueeze(1).broadcast_to([P, TT, E])
                v = [RV[:, k, :] for k in range(4)]
                dve.wait_ge(S("logits"), n + 1)
                lg = banks[2][:, 0:c].rearrange("p (t e) -> p t e", e=E)
                if l:
                    link(tt(row(0), lg, over_t(GB[:, :]), ALU.add))
                else:
                    link(nc.vector.tensor_copy(row(0), lg))
                link(nc.vector.tensor_reduce(v[0], row(0), AX, ALU.max))
                tt(row(0), row(0), over_e(v[0]), ALU.subtract).then_inc(S("logit_shift"), 1)
                dve.wait_ge(S("logit_exp"), n + 1)
                link(nc.vector.tensor_reduce(v[0], row(1), AX, ALU.add))
                link(nc.vector.reciprocal(v[1], v[0]))
                link(tt(row(1), row(1), over_e(v[1]), ALU.mult))
                for k in range(2):
                    link(nc.vector.tensor_reduce(v[k], row(1), AX, ALU.max))
                    link(tt(row(0), row(1), over_e(v[k]), ALU.is_equal))
                    link(tt(row(0), row(0), over_t(REV[:, 0:E]), ALU.mult))
                    link(nc.vector.tensor_reduce(v[2], row(0), AX, ALU.max))
                    link(tt(row(2 + k), row(0), over_e(v[2]), ALU.is_equal))
                    if k == 0:
                        link(nc.vector.scalar_tensor_tensor(row(1), row(2), -2.0, row(1), ALU.mult, ALU.add))
                tt(row(5), row(2), row(3), ALU.add).then_inc(S("chosen"), 1)
                link(tt(v[2], v[0], v[1], ALU.add))
                if l == 0:
                    link(nc.vector.tensor_scalar_max(v[2], v[2], 1e-12))
                link(nc.vector.reciprocal(v[3], v[2]))
                tt(GATE[b][:, 0, :], v[0], v[3], ALU.mult)
                tt(GATE[b][:, 1, :], v[1], v[3], ALU.mult)
                dve.wait_ge(S("prefix"), n + 1)
                tot = RT[:, 0, 0:c].rearrange("p (e t) -> p e t", t=TT)
                one = RT[:, 1, 0:c].rearrange("p (e t) -> p e t", t=TT)
                nc.vector.memset(RT[:, 1, 0:c], 1.0).then_inc(S("dve_chain"), 1)
                chain[0] += 1
                link(nc.vector.tensor_copy(tot, banks[7][:, 0:c].rearrange("p (t e) -> p e t", e=E)))
                link(nc.vector.memset(one[:, :, 0:1], 0.0))
                link(nc.vector.tensor_tensor_scan(RT[:, 4, 0:c], RT[:, 1, 0:c], RT[:, 0, 0:c], 0.0, ALU.mult, ALU.add))
                run_ = RT[:, 4, 0:c].rearrange("p (e t) -> p e t", t=TT)
                cnt, nt, st, en = (RS[:, k, 0:E] for k in range(4))
                nc.vector.tensor_copy(cnt, run_[:, :, TT - 1])
                link(tt(tot, run_, tot, ALU.subtract))
                tmp = RT[:, 1, 0:c].rearrange("p (e t) -> p e t", t=TT)
                if TT * P < NT:
                    raise ValueError
                link(tt(tmp, cnt.unsqueeze(2).broadcast_to([P, E, TT]), T128.unsqueeze(1).broadcast_to([P, E, TT]), ALU.is_gt))
                link(nc.vector.tensor_reduce(nt, tmp, AX, ALU.add))
                link(nc.vector.tensor_tensor_scan(en, ONE[:, 0:E], nt, 0.0, ALU.mult, ALU.add))
                link(tt(st, en, nt, ALU.subtract))
                ej = EJ[:, 0:E * J // 2].rearrange("p (j e) -> p j e", e=E)
                jh = J // 2
                for hh in range(2):
                    link(tt(ej, en.unsqueeze(1).broadcast_to([P, jh, E]), JI[:, hh * jh:(hh + 1) * jh].unsqueeze(2).broadcast_to([P, jh, E]), ALU.is_le))
                    link(nc.vector.tensor_reduce(RT[:, 1, hh * jh:(hh + 1) * jh], ej, AX, ALU.add))
                link(nc.vector.tensor_scalar_min(RT[:, 1, 0:J], RT[:, 1, 0:J], float(E - 1)))
                er = RT[:, 1, 0:J].rearrange("p (g r) -> p g r", r=RING)
                link(tt(er, er, POW.unsqueeze(1).broadcast_to([P, J // RING, RING]), ALU.mult))
                link(nc.vector.tensor_reduce(RV4[:, 0:J // RING], er, AX, ALU.add))
                nc.vector.tensor_copy(EPK[l][b][:, :], RV4[:, 0:J // RING])
                link(nc.vector.scalar_tensor_tensor(RT[:, 4, 0:c].rearrange("p (t e) -> p e t", e=E), st.unsqueeze(2).broadcast_to([P, E, TT]),
                                                    float(P), tot, ALU.mult, ALU.add))
                link(tt(row(4), row(4), banks[6][:, 0:c].rearrange("p (t e) -> p t e", e=E), ALU.add))
                for k in range(2):
                    link(tt(row(0), row(2 + k), row(4), ALU.mult))
                    link(nc.vector.tensor_reduce(v[2], row(0), AX, ALU.add))
                    ins = nc.vector.tensor_copy(POS[b][:, k, :], v[2])
                    if k == 0:
                        link(ins)
                ins.then_inc(S(f"routed{l}{b}"), 1)

            def moe(l, b):
                J = TILES[l]

                def first(j, r, e):
                    if l:
                        dve.wait_ge(S("silu"), j + 1 + b * J)
                        if not isinstance(j, int) or b or j >= 2:
                            dve.wait_ge(S("ht_full1"), j - 1 + b * J)
                        tt(HD_[r % 2][:, :], SG[r % 2][:, :], banks[2 + r % 2][:, 256:512], ALU.mult).then_inc(S("hid1"), 1)
                        return
                    dve.wait_ge(S("h_full0"), j + 1 + b * J)
                    if not isinstance(j, int) or b or j >= 2:
                        dve.wait_ge(S("hid0"), j - 1 + b * J)
                    tt(SG[r % 2][:, 0:P], banks[2 + r % 2][:, 0:P], B1E[:, ds(e, 1), :].rearrange("p a c -> p (a c)"), ALU.add).then_inc(S("h_free0"), 1)

                def second(j, r, e, h=None):
                    if l:
                        dve.wait_ge(S("ht_full1"), j + 1 + b * J)
                        if not isinstance(j, int) or b or j >= 2:
                            dve.wait_ge(S("y_full1"), j - 1 + b * J)
                        nc.vector.tensor_copy(HTS[r % 2][:, :], banks[4 + r % 2][:, 0:256]).then_inc(S("ht_out1"), 1)
                        return
                    dve.wait_ge(S("y_full0"), j + 1 + b * J)
                    ys_free(dve, 0, b, j, r, h)
                    tt(YS[h * RING + r], banks[6 + r % 2][:, 0:P], B2E[:, ds(e, 1), :].rearrange("p a c -> p (a c)"), ALU.add).then_inc(S("y_ready0"), 1)

                def step(j, r, h, expert, load):
                    ok = lambda k: not isinstance(j, int) or 0 <= j - k < J
                    if l and ok(3):
                        second(j - 3, (r + 1) % RING, None)
                    if ok(1):
                        first(j - 1, (r + 3) % RING, None if l else expert(1))
                    if r == 0:
                        load()
                    if not l and ok(4):
                        second(j - 4, r, expert(4), 1 - h)

                tile_groups(dve, l, b, step, 4, experts=not l)

            def combine(l, b, done=None):
                if l == 0:
                    dve.wait_ge(S("scattered0%d" % b), 16 * 2 * TT)
                    link(tt(XT[b][:, :, :], XT[b][:, :, :], TN[b][:, :, :], ALU.add))
                for g in range(NG):
                    dve.wait_ge(S(f"gathered{g}"), 16 * 2 * TG * (l * NB + b + 1))
                    for k in range(2):
                        for t in range(g * TG, (g + 1) * TG):
                            ins = nc.vector.scalar_tensor_tensor(XT[b][:, t, :], G[k][:, t, :], GATE[b][:, k, t:t + 1], XT[b][:, t, :], ALU.mult, ALU.add)
                        if k == 0:
                            link(ins)
                    if done:
                        ins.then_inc(S(done), 1)
                    elif g < NG - 1:
                        link(ins)
                    else:
                        ins.then_inc(S("combined"), 1)
                        dve.wait_ge(S("combined"), b + 1)

            def conv(b):
                combine(0, b)
                layer_norm(("X", b), b, 1e-6)

                def gn(n, chunks, gamma, beta):
                    for k, a in enumerate(chunks):
                        ins = nc.vector.bn_stats(GST[:, k, :], a)
                    link(ins)
                    link(nc.vector.bn_aggr(GV[:, 2:4], GST[:, 0:len(chunks), :]))
                    ts(GV[:, 0:1], GV[:, 2:3], 1.0, None, ALU.mult)
                    link(tt(GV[:, 4:5], GV[:, 2:3], GV[:, 2:3], ALU.mult))
                    tt(GV[:, 1:2], GV[:, 4:5], GV[:, 3:4], ALU.add).then_inc(S("gn_in"), 1)
                    dve.wait_ge(S("gn_sum"), n + 1)
                    nc.vector.tensor_copy(GV[:, 2:4], banks[1][:, 0:2]).then_inc(S("gn_read"), 1)
                    dve.wait_ge(S("gn_read"), n + 1)
                    link(tt(GV[:, 4:5], GV[:, 2:3], GV[:, 2:3], ALU.mult))
                    link(tt(GV[:, 5:6], GV[:, 3:4], GV[:, 4:5], ALU.subtract))
                    ts(GV[:, 5:6], GV[:, 5:6], 1e-5, None, ALU.add).then_inc(S("gn_var"), 1)
                    dve.wait_ge(S("gn_std"), n + 1)
                    link(nc.vector.reciprocal(GV[:, 9:10], GV[:, 6:7]))
                    link(tt(GV[:, 7:8], GV[:, 9:10], gamma, ALU.mult))
                    link(tt(GV[:, 10:11], GV[:, 2:3], GV[:, 7:8], ALU.mult))
                    tt(GV[:, 8:9], beta, GV[:, 10:11], ALU.subtract).then_inc(S("gn_coef"), 1)

                dve.wait_ge(S("hc_ready"), 2 * (b + 1))
                gn(3 * b, [HC[:, hh, :] for hh in range(2)], N1G, N1B)
                dve.wait_ge(S("conv2"), b + 1)
                dve.wait_ge(S("hp_ready"), b + 1)
                gn(3 * b + 1, [banks[4 + hh][:, 0:HALF] for hh in range(2)], NMG, NMB)
                link(tt(XT[b][:, :, :], XT[b][:, :, :], TN[b][:, :, :], ALU.add))
                dve.wait_ge(S("z_ready"), b + 1)
                dve.wait_ge(S("up_out"), 8 * (b + 1))
                gn(3 * b + 2, [CM[:, k * NT // 6:(k + 1) * NT // 6] for k in range(6)], N2G, N2B)
                for g in range(NG):
                    m = group_base[("z", "X", b)] + g
                    t_wait_full(dve, m)
                    xt = XT[b][:, g * TG:(g + 1) * TG, :]
                    tt(xt, xt, banks[m % 2][:, 0:TG * P].rearrange("p (t c) -> p t c", c=P), ALU.add).then_inc(S("t_free"), 1)
                dve.wait_ge(S("t_free"), group_base[("z", "X", b)] + NG)

            run(dve, lna=lna, att=att, route=route, moe=moe, conv=conv, fin=lambda b: combine(1, b, "out_ready"))


def constants():
    import numpy as np
    P, E, J, TT = 128, 16, 52, 18
    p = np.arange(P)
    j = np.arange(7)[:, None, None] + 1
    d = ((p[None, :, None] % 32) - np.arange(32)[None, None, :] + 4 == j)
    cols = [np.eye(P), p[:, None] < p[None, :], np.ones((P, P)),
            ((p[:, None] % 32) // 2 == (p[None, :] % 32) // 2) / 8.0, (p[:, None] // 8 == p[None, :] // 8) / 8.0,
            (p[:, None] // 16) % 4 == np.arange(4)[None, :], (p[:, None] // 16) % 2 == np.arange(2)[None, :],
            p[:, None] % 32 == np.arange(32)[None, :], d.transpose(1, 0, 2).reshape(P, 224),
            np.broadcast_to(E - np.arange(E), (P, E)), np.broadcast_to(np.arange(J), (P, J)),
            np.broadcast_to(128 * np.arange(TT), (P, TT)), np.broadcast_to(16 ** np.arange(4), (P, 4))]
    return np.ascontiguousarray(np.concatenate([np.asarray(c, np.float32) for c in cols], axis=1))


def kernel(**inputs):
    import numpy as np
    import concourse.bacc as _bacc
    from concourse import mybir as _mybir
    from concourse.bass_utils import run_bass_kernel_spmd as _run

    a = {k: np.asarray(v) for k, v in inputs.items()}
    P = 128
    x = a["x"].reshape(2, P, 12, 4, 12, 4).transpose(0, 2, 4, 3, 5, 1).reshape(2, 18, P, P).transpose(0, 2, 1, 3)
    qw, qb = a["L0_conv_qkv_w"].reshape(3, P), a["L0_conv_qkv_b"].reshape(3, P)
    rep = lambda v: np.tile(v, 4)
    params = np.stack([qw[0], qb[0], qw[1], qb[1], qw[2], qb[2], rep(a["L1_conv_conv1_b"]), rep(a["L1_conv_gn1_g"]), rep(a["L1_conv_gn1_b"]),
                       rep(a["L1_conv_gnm_g"]), rep(a["L1_conv_gnm_b"]), a["L1_conv_conv2_b"], a["L1_conv_gn2_g"], a["L1_conv_gn2_b"],
                       a["L1_conv_gn2_b"], a["L1_conv_gn2_b"]], axis=1)
    qi, qj, kj, ki = np.ix_(np.arange(4), np.arange(4), np.arange(8), np.arange(8))
    index = ((qi - ki + 7) * 15 + (qj - kj + 7)).reshape(16, 64)
    pos_bias = a["L0_conv_pos_table"][index].transpose(2, 0, 1).reshape(P, 64)
    w2 = a["L1_conv_W2"][:, 0]
    w2_rows = np.zeros((4, 32, 12, 9), np.float32)
    for r in range(4):
        for m in range(12):
            if 0 <= m - 3 + r < 9:
                w2_rows[r, :, m] = w2[:, m - 3 + r]
    bc = lambda v: np.broadcast_to(v, (P,) + v.shape)
    arrays = {
        "x_tok": x, "params": params, "consts": constants(), "pos_bias": pos_bias,
        "out_wT": a["L0_conv_out_w"].T, "conv1_wT": a["L1_conv_conv1_w"].T, "conv2_wT": np.tile(a["L1_conv_conv2_w"].T, (4, 1)),
        "w2_rows": w2_rows.reshape(P, 12, 9), "w1_conv": bc(a["L1_conv_W1"].reshape(9)),
        "router_wT": a["L0_ffn_router_w"].T, "gate_wT": a["L1_ffn_gate_w"], "gate_b": bc(a["L1_ffn_gate_b"]),
        "moe0_w1": a["L0_ffn_w1"].transpose(1, 0, 2), "moe0_w2": a["L0_ffn_w2"].transpose(1, 0, 2),
        "moe0_b1": bc(a["L0_ffn_b1"]), "moe0_b2": bc(a["L0_ffn_b2"]),
        "moe1_w12": np.concatenate([a["L1_ffn_w1"], a["L1_ffn_w2"]], axis=2).transpose(1, 0, 2),
        "moe1_w3": a["L1_ffn_w3"].reshape(16, 2, P, P).transpose(2, 0, 1, 3),
    }
    nc = _bacc.Bacc("TRN2", target_bir_lowering=False, num_devices=1)
    args = []
    for name in arrays:
        arrays[name] = np.ascontiguousarray(arrays[name])
        args.append(nc.dram_tensor("in_" + name, arrays[name].shape, _mybir.dt.from_np(arrays[name].dtype), kind="ExternalInput").ap())
    args.append(nc.dram_tensor("out", (2, P, 18, P), _mybir.dt.float32, kind="ExternalOutput").ap())
    metaformer_program(nc, *args)
    r = _run(nc, [{"in_" + k: v for k, v in arrays.items()}], core_ids=[0])
    y = np.asarray(r.results[0]["out"])
    return np.ascontiguousarray(y.transpose(0, 2, 1, 3).reshape(2, 12, 12, 4, 4, P).transpose(0, 5, 1, 3, 2, 4).reshape(2, P, 48, 48))
```

```python
import concourse.bass as bass
from concourse import mybir
from contextlib import ExitStack


def metaformer_program(nc, x_tok, params, consts, pos_bias, out_wT, conv1_wT, conv2_wT, w2_rows, w1_conv,
                       router_wT, gate_wT, gate_b, moe0_w1, moe0_w2, moe0_b1, moe0_b2, moe1_w12, moe1_w3, out):
    fp32 = mybir.dt.float32
    i32 = mybir.dt.int32
    ALU = mybir.AluOpType
    ACT = mybir.ActivationFunctionType
    AX = mybir.AxisListType.X
    ds = bass.ds

    P = 128
    NB = 2
    IMG = 48
    NT = IMG * IMG
    TT = NT // P
    HEADS, HD, WS, WK = 8, 16, 4, 8
    NW = IMG // WS
    HW_ = NW // 2
    STEPS = 2 * NW
    Q = WS * WS
    KEYS = WK * WK
    PADI = IMG + WK - WS
    TG = 3
    NG = TT // TG
    EX = (8, 16)
    RING = 4
    GW = (2, 1)
    BITS = (3, 4)
    TILES = tuple(-(-((2 * NT + (P - 1) * e) // P) // RING) * RING for e in EX)
    WORDS = tuple(-(-TILES[l] // (GW[l] * RING)) for l in range(2))
    EMAX = max(EX)
    JMAX = max(TILES)
    C4 = 32
    CB, CX = NW + 2, IMG + 8
    HALF = NT // 4 // 2
    KX, KA = 9, 3

    names = {}
    ctx = ExitStack()
    with ctx:
        def sb(name, shape, dt=fp32):
            return ctx.enter_context(nc.sbuf_tensor(name, shape, dt))

        def S(name):
            if name not in names:
                names[name] = ctx.enter_context(nc.semaphore(name))
            return names[name]

        banks = [ctx.enter_context(nc.psum_tensor(f"bank{i}", [P, 512], fp32)) for i in range(8)]

        xs_dram = [[nc.dram_tensor(f"sorted_x{l}{b}", (TILES[l] * P, P), fp32).ap() for b in range(NB)] for l in range(2)]
        ys_dram = [[nc.dram_tensor(f"sorted_y{l}{b}", (TILES[l] * P, P), fp32).ap() for b in range(NB)] for l in range(2)]

        XT = [sb(f"residual{b}", [P, TT, P]) for b in range(NB)]
        TN = [sb(f"normed{b}", [P, TT, P]) for b in range(NB)]
        QY = [sb(f"qy{b}", [P, NT]) for b in range(NB)]
        big = sb("padded_or_w12", [P, EX[1] * 512 + 4 * RING * P])
        XPAD = [big[:, b * PADI * PADI:(b + 1) * PADI * PADI].rearrange("p (y x) -> p y x", x=PADI) for b in range(NB)]
        o = NB * PADI * PADI
        KROW, VROW = ([big[:, o + (2 * k + h) * WK * PADI:o + (2 * k + h + 1) * WK * PADI] for h in range(2)] for k in range(2))
        W12 = big[:, 0:EX[1] * 512].rearrange("p (e h) -> p e h", h=512)
        W3 = sb("w3", [P, EX[1], 2, P])
        n = EX[0] * P
        moe0 = sb("moe0_or_conv1", [P, 4 * n])
        W1E, W2E, B1E, B2E = (moe0[:, k * n:(k + 1) * n].rearrange("p (e c) -> p e c", c=P) for k in range(4))
        CM = [sb("chan_major", [P, NT]), moe0[:, 0:NT]]
        o = NT + 2 * HALF
        HC = [sb("conv_mid", [P, 2, HALF]), moe0[:, NT:o].rearrange("p (h n) -> p h n", n=HALF)]
        HP = [sb("conv_padded", [P, CB, CX]), moe0[:, o:o + CB * CX].rearrange("p (a x) -> p a x", x=CX)]
        gath = sb("gathered_or_att", [P, 2 * TT * P])
        G = [gath[:, k * TT * P:(k + 1) * TT * P].rearrange("p (t c) -> p t c", c=P) for k in range(2)]
        W = HW_ * KEYS
        o = NB * PADI * PADI + 4 * WK * PADI
        QBD = [big[:, o + k * W:o + (k + 1) * W].rearrange("p (w m) -> p w m", m=P // 2) for k in range(4)]
        SB_, PE_, PN_ = ([gath[:, (2 * k + h) * W:(2 * k + h + 1) * W] for h in range(2)] for k in range(3))
        att2 = sb("att2_or_moe", [P, 14 * P])
        PTB = gath[:, 6 * W:10 * W]
        PTS = [PTB[:, 2 * h * W:2 * (h + 1) * W].rearrange("p (n w m) -> p n w m", w=2, m=P) for h in range(2)]
        VTS = [att2[:, h * W:(h + 1) * W] for h in range(2)]
        OS = [att2[:, (2 + h) * W:(3 + h) * W].rearrange("p (a h w q) -> p a h w q", a=2, h=2, q=Q) for h in range(2)]
        TOEP = sb("toeplitz", [P, KA * KX, P])
        CON = sb("consts", [P, 5 * P + HEADS // 2 + 2 + 32 + 7 * 32 + EMAX + JMAX + TT + RING + 2 * RING])
        IDN, TRI, ONE, G2, G8 = (CON[:, k * P:(k + 1) * P] for k in range(5))
        o = 5 * P
        HM, PAR, I32, DJ = CON[:, o:o + 4], CON[:, o + 4:o + 6], CON[:, o + 6:o + 38], CON[:, o + 38:o + 38 + 224]
        o += 38 + 224
        REV, JI, T128 = CON[:, o:o + EMAX], CON[:, o + EMAX:o + EMAX + JMAX], CON[:, o + EMAX + JMAX:o + EMAX + JMAX + TT]
        o += EMAX + JMAX + TT
        POW = (CON[:, o + RING:o + 3 * RING], CON[:, o:o + RING])
        PRM = sb("params", [P, 16])
        (QW, QB, KW, KB, VW, VB, C1B, N1G, N1B, NMG, NMB, C2B, N2G, N2B) = (PRM[:, k:k + 1] for k in range(14))
        QS = sb("q_scaled", [P, 2])
        BIAS = sb("pos_bias", [P, KEYS])
        OWT = sb("out_w", [P, P])
        OWP = sb("out_w_parity", [P, 2, P])
        C1W = sb("conv1_w", [P, C4])
        C2W = sb("conv2_w", [P, P])
        W2R = sb("conv_rows", [P, 12, KX])
        W1C = sb("conv_chan", [P, 9])
        BAND = sb("band", [P, 32])
        BND = sb("band_term", [P, 32])
        RW = [sb("router_w", [P, EX[0]]), sb("gate_w", [P, EX[1]])]
        GB = sb("gate_b", [P, EX[1]])
        MXS = sb("score_max", [P, 2, HW_])
        RSM = sb("prob_sum", [P, 2, HW_])
        RRC = sb("prob_rsum", [P, 2, HW_])
        STT = sb("ln_stats", [P, TT, 6])
        LNV = sb("ln_values", [P, 6, TT])
        RT = sb("route", [P, 6, EMAX * TT])
        RS = sb("route_small", [P, 8, EMAX])
        RV = sb("route_rows", [P, 4, TT])
        RV4 = sb("route_packed", [P, JMAX // RING])
        EJ = sb("expert_cmp", [P, EMAX * JMAX // 2])
        EPK = [[sb(f"experts_of_tiles{l}{b}", [P, WORDS[l]], i32) for b in range(NB)] for l in range(2)]
        POS = [sb(f"slot{b}", [P, 2, TT], i32) for b in range(NB)]
        GATE = [sb(f"gate{b}", [P, 2, TT]) for b in range(NB)]
        o = 0

        def carve(n, width):
            nonlocal o
            views = [att2[:, o + k * width:o + (k + 1) * width] for k in range(n)]
            o += n * width
            return views

        XTS, SG, HD_, HTS = carve(2, P), carve(2, 256), carve(2, 256), carve(2, 256)
        o = EX[1] * 512
        XG, YG = ([big[:, o + (2 * k + h) * RING * P:o + (2 * k + h + 1) * RING * P].rearrange("p (r c) -> p r c", c=P)
                   for h in range(2)] for k in range(2))
        XS, YS = ([g[h][:, r, :] for h in range(2) for r in range(RING)] for g in (XG, YG))
        ZER = sb("zeros", [P, 512])
        GST = sb("gn_stats", [P, 6, 6])
        GVB = [sb(f"gn_values{b}", [P, 12]) for b in range(NB)]

        def of_step(a, wy, hf):
            return a[:, :].rearrange("p (r w h q) -> p r w h q", w=HW_, h=2, q=Q)[:, ds(wy, 1), :, hf, :].rearrange("p r w q -> p (r w) q")

        def att_steps(eng, b, step, lead, lag):
            def whole(n):
                def at(k):
                    b, s = divmod(n - k, STEPS)
                    return (b, s, s // 2) if 0 <= b < NB else None
                step(n % 4, at)

            for n in range(b * STEPS, b * STEPS + 4 * lag):
                whole(n)
            with eng.Fori(lag, NW // 2 - lead) as i:
                for c in range(4):
                    step(c, lambda k: (b, 4 * i + (c - k), 2 * i + (c - k) // 2))
            for n in range((b + 1) * STEPS - 4 * lead, (b + 1) * STEPS):
                whole(n)
            if b == NB - 1:
                for n in range(NB * STEPS, NB * STEPS + 8):
                    whole(n)

        block = ctx.enter_context(nc.Block())

        order = ([("LNA", b) for b in range(NB)] + [("ATT", b) for b in range(NB)] +
                 [(p, 0, b) for b in range(NB) for p in ("RA", "RC", "RS")] + [("M", 0, b) for b in range(NB)] +
                 [("XL", 0), ("XC", 0), ("XT", 0, 0, 1), ("XL", 1), ("XM", 0), ("XC", 1), ("XU", 0), ("XT", 1, 0, 1 / 6), ("XZ", 0),
                  ("XT", 1, 1 / 6, 4 / 9), ("RA", 1, 0), ("RC", 1, 0), ("XT", 1, 4 / 9, 1), ("XM", 1), ("RS", 1, 0),
                  ("XU", 1), ("XZ", 1), ("RA", 1, 1), ("RC", 1, 1), ("RS", 1, 1)] +
                 [("M", 1, b) for b in range(NB)] + [("F", b) for b in range(NB)])
        group_base, n_groups = {}, 0
        for ph in order:
            for tag in {"LNA": ("a",), "RA": ("y", "r") if ph[1] == 0 else ("r",), "XL": ("c",), "XZ": ("z",)}.get(ph[0], ()):
                group_base[(tag,) + ph] = n_groups
                n_groups += NG
        lns = [ph for ph in order if ph[0] in ("LNA", "RA", "XL")]
        gns = [ph for ph in order if ph[0] in ("XC", "XM", "XU")]

        def t_wait_full(eng, n):
            eng.wait_ge(S("t_full"), n + 1)

        groups_done, gn_done = [0], [0]

        def normed_group(pe, tag, ph, b, g):
            pe.wait_ge(S("ln_done"), lns.index(ph) * NG + g + 1)
            pe_group(pe, group_base[(tag,) + ph] + g, [TN[b][:, g * TG + k, :] for k in range(TG)])

        def pe_group(pe, n, srcs, ident=IDN):
            if n >= 2:
                pe.wait_ge(S("t_free"), n - 1)
            if n % 2 and gn_done[0]:
                pe.wait_ge(S("gn_read"), gn_done[0])
            groups_done[0] = n + 1
            for k, a in enumerate(srcs):
                ins = nc.tensor.transpose(banks[n % 2][:, k * P:(k + 1) * P], a, ident)
            ins.then_inc(S("t_full"), 1)

        UP = ((2, 3, 6, 7), (4, 5, 3, 0))

        def ln_no(ph):
            return lns.index(ph) + 1

        def through_buffer(l, h):
            return (TILES[l] // RING + 1 - h) // 2

        def ys_free(eng, l, b, j, r, h):
            if r == 0 and (not isinstance(j, int) or b or j // RING >= 2):
                eng.wait_ge(S(f"ys_out{l}{h}"), (j - RING * h) * (16 // (2 * RING)) + 16 * b * through_buffer(l, h))

        def gather_part(t):
            return t // TG if t < TT - 1 else NG

        def gn_no(ph):
            return gns.index(ph)

        def run(**phases):
            for name, *where in order:
                if name in phases:
                    phases[name](*where)

        def tile_groups(eng, l, b, step, lag, experts=True):
            J, E = TILES[l], EX[l]
            words = EPK[l][b]
            held = eng.alloc_register(name=f"word_before_{eng.engine.name}{l}{b}") if experts else None
            top = 2 ** (BITS[l] * GW[l] * RING) - 1
            word = {}

            def group(q, h, w, first=False, last=False):
                part = h % GW[l]
                if part == 0:
                    word["before"] = eng.snap(held, min_val=0, max_val=top) if experts and not first else None

                def load():
                    if experts and part == 0 and not last:
                        word["now"] = eng.value_load(words[0:1, ds(w, 1)], min_val=0, max_val=top)

                for r in range(RING if not last else lag):
                    def expert(k):
                        slot = part * RING + r - k
                        bits = word["now"] if slot >= 0 else word["before"]
                        shift = BITS[l] * (slot % (GW[l] * RING))
                        return (bits >> shift) & (E - 1) if shift else bits & (E - 1)
                    step(q * RING + r, r, h, expert, load)
                if experts and not last and part == GW[l] - 1:
                    eng.reg_mov(held, word["now"])

            n = J // RING
            turns = (n - 2) // 2
            group(0, 0, 0, first=True)
            group(1, 1, 1 // GW[l])
            with eng.Fori(1, turns + 1) as turn:
                for h in range(2):
                    group(turn * 2 + h, h, turn * (2 // GW[l]) + h // GW[l])
            for q in range(2 * turns + 2, n):
                group(q, q % 2, q // GW[l])
            group(n, n % 2, None, last=True)

        @block.sync
        def _(sp):
            for b in range(NB):
                sp.dma_start(XT[b][:, :, :], x_tok[b]).then_inc(S(f"x_in{b}"), 16)
                if b == 0:
                    sp.dma_start(CON[:, :], consts).then_inc(S("consts_in"), 16)
                    sp.dma_start(PRM[:, :], params).then_inc(S("consts_in"), 16)
                    sp.dma_start(BIAS[:, :], pos_bias).then_inc(S("consts_in"), 16)
                    sp.dma_start(OWT[:, :], out_wT).then_inc(S("consts_in"), 16)
            for dst, src in ((C1W, conv1_wT), (C2W, conv2_wT), (W1C, w1_conv), (RW[0], router_wT), (RW[1], gate_wT), (GB, gate_b)):
                sp.dma_start(dst[:, :], src).then_inc(S("small_in"), 16)
            sp.dma_start(W2R[:, :, :], w2_rows).then_inc(S("small_in"), 16)
            sp.dma_start(W1E[:, :, :], moe0_w1).then_inc(S("moe0_in"), 16)
            sp.dma_start(W2E[:, :, :], moe0_w2).then_inc(S("moe0_in"), 16)
            sp.dma_start(B1E[:, :, :], moe0_b1).then_inc(S("moe0_in"), 16)
            sp.dma_start(B2E[:, :, :], moe0_b2).then_inc(S("moe0_in"), 16)
            sp.dma_start(W3[:, :, :, :], moe1_w3).then_inc(S("moe1_in"), 16)
            sp.wait_ge(S("zeros_set"), 1)
            for l in range(2):
                for b in range(NB):
                    v = xs_dram[l][b].rearrange("(n r p) c -> n p r c", p=P, r=RING)
                    for n in range(TILES[l] // RING):
                        sp.dma_start(v[n], ZER[:, :].rearrange("p (r c) -> p r c", c=P)).then_inc(S(f"sorted_zero{l}{b}"), 16)

            def moe(l, b):
                J = TILES[l]
                n = J // RING
                ys = ys_dram[l][b].rearrange("(q r p) c -> q p r c", p=P, r=RING)

                def load(q, h, b=b):
                    xs = xs_dram[l][b].rearrange("(q r p) c -> q p r c", p=P, r=RING)
                    if not isinstance(q, int) or q >= 2:
                        sp.wait_ge(S(f"x_transposed{l}"), RING * (q - 1) + b * J)
                    elif b:
                        sp.wait_ge(S(f"x_transposed{l}"), b * J)
                    sp.dma_start(XG[h], xs[ds(q, 1)].rearrange("o p r c -> p (o r) c")).then_inc(S(f"xs_in{l}{h}"), 16)

                def store(q, h):
                    sp.wait_ge(S(f"y_ready{l}"), RING * (q + 1) + b * J)
                    sp.dma_start(ys[ds(q, 1)].rearrange("o p r c -> p (o r) c"), YG[h]).then_inc(S(f"ys_out{l}{h}"), 16)

                def load_first(b):
                    sp.wait_ge(S(f"scattered{l}{b}"), 16 * 2 * TT)
                    for q in range(2):
                        load(q, q, b)

                if b == 0:
                    load_first(0)
                turns = (n - 2) // 2
                with sp.Fori(0, turns) as turn:
                    for h in range(2):
                        load(turn * 2 + (2 + h), h)
                        store(turn * 2 + h, h)
                for q in range(2 * turns, n):
                    if q + 2 < n:
                        load(q + 2, q % 2)
                    elif q == n - 1 and b == 0:
                        load_first(1)
                    store(q, q % 2)

            sp.wait_ge(S("attn_y"), NB * NW)
            sp.wait_ge(S("scores"), NB * STEPS)
            sp.wait_ge(S("v_transposed"), NB * STEPS)
            sp.wait_ge(S("v_row"), NB * NW)
            sp.dma_start(W12, moe1_w12).then_inc(S("moe1_in"), 16)
            moe(0, 0)
            moe(0, 1)
            moe(1, 0)
            moe(1, 1)
            for b in range(NB):
                for g in range(NG):
                    sp.wait_ge(S("out_ready"), b * NG + g + 1)
                    sp.dma_start(out[b, :, g * TG:(g + 1) * TG, :], XT[b][:, g * TG:(g + 1) * TG, :]).then_inc(S("out_stored"), 16)
            sp.wait_ge(S("out_stored"), 16 * NB * NG)

        @block.gpsimd
        def _(pool):
            nc.gpsimd.memset(ZER[:, :], 0.0).then_inc(S("zeros_set"), 1)
            nc.gpsimd.memset(HP[0][:, :, :], 0.0).then_inc(S("pad_zero"), 1)
            nc.gpsimd.memset(PTB, 0.0).then_inc(S("pt_zero"), 1)
            pool.wait_ge(S("consts_in"), 64)
            pool.wait_ge(S("small_in"), 16 * 7)
            for a in range(KA):
                for r in range(4):
                    nc.gpsimd.tensor_tensor(TOEP[:, a * KX:(a + 1) * KX, 32 * r:32 * r + 32], I32.unsqueeze(1).broadcast_to([P, KX, 32]),
                                            W2R[:, 4 * a - r + 3, :].unsqueeze(2).broadcast_to([P, KX, 32]), ALU.mult)
            nc.gpsimd.tensor_scalar(BAND[:, :], DJ[:, 0:32], W1C[:, 1:2], None, ALU.mult).then_inc(S("band"), 1)
            for j in range(1, 7):
                nc.gpsimd.tensor_scalar(BND[:, :], DJ[:, 32 * j:32 * j + 32], W1C[:, j + 1:j + 2], None, ALU.mult).then_inc(S("band"), 1)
                pool.wait_ge(S("band"), 2 * j)
                nc.gpsimd.tensor_tensor(BAND[:, :], BAND[:, :], BND[:, :], ALU.add).then_inc(S("band"), 1)
                pool.wait_ge(S("band"), 2 * j + 1)
            for r in range(4):
                blk = TOEP[32 * r:32 * r + 32, KX + KX // 2, 32 * r:32 * r + 32]
                nc.gpsimd.tensor_tensor(blk, blk, BAND[32 * r:32 * r + 32, :], ALU.add).then_inc(S("toeplitz"), 1)
                pool.wait_ge(S("toeplitz"), r + 1)

            def queries(b, s, row, c):
                g = s + b * STEPS
                if isinstance(s, int) and s == 0:
                    pool.wait_ge(S("q_ready"), NG * (b + 1))
                if not isinstance(s, int) or g >= 4:
                    pool.wait_ge(S("scores"), g - 3)
                out_ = QBD[c].rearrange("p w (h q) -> p w h q", q=Q)
                nc.gpsimd.tensor_tensor(out_, of_step(QY[b], row, c % 2).unsqueeze(2).broadcast_to([P, HW_, HEADS // 2, Q]),
                                        HM.unsqueeze(1).unsqueeze(3).broadcast_to([P, HW_, HEADS // 2, Q]),
                                        ALU.mult).then_inc(S("qbd"), 1)

            def norm(b, s, hf):
                g = s + b * STEPS
                pool.wait_ge(S("rsum"), g + 1)
                if not isinstance(s, int) or g >= 2:
                    pool.wait_ge(S("p_transposed"), g - 1)
                pn = PN_[hf].rearrange("p (w k) -> p w k", k=KEYS)
                pe_ = PE_[hf].rearrange("p (w k) -> p w k", k=KEYS)
                nc.gpsimd.tensor_tensor(pn, pe_, RRC[:, hf, :].unsqueeze(2).broadcast_to([P, HW_, KEYS]), ALU.mult).then_inc(S("probs"), 1)

            def step(c, at):
                if at(-1):
                    queries(*at(-1), (c + 1) % 4)
                if at(2):
                    norm(*at(2)[:2], c % 2)

            queries(0, 0, 0, 0)
            for b in range(NB):
                att_steps(pool, b, step, 1, 1)

            def scatter(l, b):
                pool.wait_ge(S(f"routed{l}{b}"), 1)
                pool.wait_ge(S(f"sorted_zero{l}{b}"), 16 * (TILES[l] // RING))
                for t in range(TT):
                    for k in range(2):
                        nc.gpsimd.indirect_dma_start(xs_dram[l][b], bass.IndirectOffsetOnAxis(ap=POS[b][:, k, t:t + 1], axis=0),
                                                     TN[b][:, t, :], None).then_inc(S(f"scattered{l}{b}"), 16)

            def gather(l, b):
                n = l * NB + b
                for h in range(2):
                    pool.wait_ge(S(f"ys_out{l}{h}"), 16 * (b + 1) * through_buffer(l, h))
                if n == 1:
                    nc.gpsimd.memset(HP[1][:, :, :], 0.0).then_inc(S("pad_zero"), 1)
                for t in range(TT):
                    if n and t % TG == 0:
                        if n == 3:
                            pool.wait_ge(S("out_ready"), t // TG + 1)
                        else:
                            pool.wait_ge(S("combined"), (n - 1) * NG + t // TG + 1)
                    for k in range(2):
                        nc.gpsimd.indirect_dma_start(G[k][:, t, :], None, ys_dram[l][b],
                                                     bass.IndirectOffsetOnAxis(ap=POS[b][:, k, t:t + 1], axis=0)
                                                     ).then_inc(S(f"gathered{gather_part(t)}"), 16)

            def add_normed(b):
                nc.gpsimd.tensor_tensor(XT[b][:, :, :], XT[b][:, :, :], TN[b][:, :, :], ALU.add).then_inc(S(f"normed_added{b}"), 1)

            scatter(0, 0)
            scatter(0, 1)
            for b in range(NB):
                add_normed(b)
            gather(0, 0)
            gather(0, 1)
            for b in range(NB):
                pool.wait_ge(S("ln_done"), (lns.index(("XL", b)) + 1) * NG)
                add_normed(b)
            scatter(1, 0)
            scatter(1, 1)
            gather(1, 0)
            gather(1, 1)

        @block.tensor
        def _(pe):
            def lna(b):
                for g in range(NG):
                    normed_group(pe, "a", ("LNA", b), b, g)

            def att(b):
                if b == 0:
                    pe.wait_ge(S("t_free"), NB * NG)
                    pe.wait_ge(S("pt_zero"), 1)

                def scores(b, s, row, hf, par):
                    g = s + b * STEPS
                    if isinstance(s, int):
                        pe.wait_ge(S("k_row"), row + 1 + b * NW)
                        pe.wait_ge(S("qbd"), g + 1)
                        if g >= 2:
                            pe.wait_ge(S("biased"), g - 1)
                    for w in range(HW_):
                        k0 = (2 * w + hf) * WS * WK
                        for m in (slice(0, P // 2), slice(P // 2, P)):
                            ins = nc.tensor.matmul(banks[2 + hf][m, w * KEYS:(w + 1) * KEYS], QBD[2 * par + hf][m, w, :],
                                                   KROW[par][m, k0:k0 + KEYS], start=True, stop=True)
                    ins.then_inc(S("scores"), 1)

                def transposes(b, s, row, hf, par):
                    g = s + b * STEPS
                    pe.wait_ge(S("probs"), g + 1)
                    for p in range(HW_ // 2):
                        ins = nc.tensor.transpose(banks[5][:, p * P:(p + 1) * P], PN_[hf][:, p * P:(p + 1) * P], IDN)
                    ins.then_inc(S("p_transposed"), 1)
                    if hf == 0:
                        pe.wait_ge(S("v_row"), row + 1 + b * NW)
                    if not isinstance(s, int):
                        if hf == 1:
                            pe.wait_ge(S("k_row"), row + 3 + b * NW)
                        pe.wait_ge(S("qbd"), g + 4)
                        pe.wait_ge(S("biased"), g + 2)
                    for p in range(HW_ // 2):
                        k0 = (4 * p + hf) * WS * WK
                        ins = nc.tensor.transpose(banks[0][:, p * P:(p + 1) * P], VROW[par][:, k0:k0 + P], IDN)
                    ins.then_inc(S("v_transposed"), 1)

                def weigh(b, s, hf):
                    pe.wait_ge(S("edge"), b + 1)
                    pe.wait_ge(S("vt_out"), s + b * STEPS + 1)
                    if hf == 0 and (not isinstance(s, int) or s + b * STEPS >= 2):
                        pe.wait_ge(S("o_out"), s + b * STEPS - 1)
                    for p in range(HW_ // 2):
                        for j in range(4):
                            m = slice(32 * j, 32 * j + 32)
                            ins = nc.tensor.matmul(banks[6 + hf][m, p * 64:(p + 1) * 64], VTS[hf][:, p * P + 32 * j:p * P + 32 * j + 32],
                                                   PTS[hf][:, p, :, m], start=True, stop=True)
                    ins.then_inc(S("weighed"), 1)

                def project(b, s, row, par):
                    pe.wait_ge(S("o_out"), s + b * STEPS + 1)
                    if not isinstance(s, int) or row + b >= 1:
                        pe.wait_ge(S("attn_y"), row + b * NW)
                    for a in range(2):
                        ins = nc.tensor.matmul(banks[1][:, 0:NW * Q], OWP[:, a, :], OS[par][:, a].rearrange("p h w q -> p (h w q)"),
                                               start=(a == 0), stop=(a == 1))
                    ins.then_inc(S("projected"), 1)

                def step(c, at):
                    hf = c % 2
                    if at(3):
                        transposes(*at(3), 1 - hf, (c + 1) % 4 // 2)
                    if at(0):
                        scores(*at(0), hf, c // 2)
                    if at(3):
                        weigh(*at(3)[:2], 1 - hf)
                    if hf and at(4):
                        project(*at(4), c // 2)

                att_steps(pe, b, step, 0, 1)

            def route_a(l, b):
                if l == 0:
                    for g in range(NG):
                        if g == 0:
                            pe.wait_ge(S("attn_y"), NB * NW)
                            pe.wait_ge(S("o_out"), NB * STEPS)
                            pe.wait_ge(S("vt_out"), NB * STEPS)
                        pe_group(pe, group_base[("y", "RA", 0, b)] + g, [QY[b][:, (g * TG + k) * P:(g * TG + k + 1) * P] for k in range(TG)])
                E, base = EX[l], group_base[("r", "RA", l, b)]
                for g in range(NG + 1):
                    if g < NG:
                        normed_group(pe, "r", ("RA", l, b), b, g)
                    if g:
                        pe.wait_ge(S("t_free"), base + g)
                        if g == 1 and l == 0 and b == 0:
                            pe.wait_ge(S("small_in"), 16 * 7)
                        for t in range((g - 1) * TG, g * TG):
                            ins = nc.tensor.matmul(banks[2][:, t * E:(t + 1) * E], CM[l * b][:, t * P:(t + 1) * P], RW[l][:, :], start=True, stop=True)
                ins.then_inc(S("logits"), 1)

            def route_b(l, b):
                E, n = EX[l], l * NB + b
                pe.wait_ge(S("chosen"), n + 1)
                nc.tensor.matmul(banks[6][:, 0:TT * E], TRI, RT[:, 5, 0:TT * E], start=True, stop=True)
                nc.tensor.matmul(banks[7][:, 0:TT * E], ONE, RT[:, 5, 0:TT * E], start=True, stop=True).then_inc(S("prefix"), 1)

            def moe(l, b):
                J = TILES[l]
                if b == 0:
                    pe.wait_ge(S("moe0_in" if l == 0 else "moe1_in"), 64 if l == 0 else 32)
                    pe.wait_ge(S("t_free"), max(v for k, v in group_base.items() if k[1:3] == ("RA", l)) + NG)
                pe.wait_ge(S(f"experts{l}{b}"), 1)
                IN = 2 * P if l else P

                def tx(j, r, h):
                    if r == 0:
                        pe.wait_ge(S(f"xs_in{l}{h}"), (j - RING * h) * (16 // (2 * RING)) + 16 * (1 + b * through_buffer(l, h)))
                    nc.tensor.transpose(banks[r % 2][:, 0:P], XS[h * RING + r], IDN).then_inc(S(f"x_transposed{l}"), 1)

                def hid(j, r, e):
                    pe.wait_ge(S(f"xt_out{l}"), j + 1 + b * J)
                    w = W12 if l else W1E
                    nc.tensor.matmul(banks[2 + r % 2][:, 0:(512 if l else P)], XTS[r % 2][:, :],
                                     w[:, ds(e, 1), :], start=True, stop=True).then_inc(S(f"h_full{l}"), 1)

                def th(j, r):
                    pe.wait_ge(S(f"hid{l}"), j + 1 + b * J)
                    for a in range(IN // P):
                        ins = nc.tensor.transpose(banks[4 + r % 2][:, a * P:(a + 1) * P], HD_[r % 2][:, a * P:(a + 1) * P], IDN)
                    ins.then_inc(S(f"ht_full{l}"), 1)

                def ym(j, r, e):
                    if isinstance(j, int) and j == 0 and b == 0:
                        pe.wait_ge(S(f"routed{l}1"), 1)
                    pe.wait_ge(S(f"ht_out{l}"), j + 1 + b * J)
                    if l == 0 and not isinstance(j, int) or isinstance(j, int) and (b or j >= 2):
                        pe.wait_ge(S(f"y_ready{l}"), j - 1 + b * J)
                    for a in range(IN // P):
                        rhs = W3[:, ds(e, 1), a, :] if l else W2E[:, ds(e, 1), :]
                        ins = nc.tensor.matmul(banks[6 + r % 2][:, 0:P], HTS[r % 2][:, a * P:(a + 1) * P], rhs,
                                               start=(a == 0), stop=(a == IN // P - 1))
                    ins.then_inc(S(f"y_full{l}"), 1)

                def step(j, r, h, expert, load):
                    ok = lambda k: not isinstance(j, int) or 0 <= j - k < J
                    if ok(0):
                        tx(j, r, h)
                    if ok(3):
                        th(j - 3, (r + 1) % RING)
                    if ok(1):
                        hid(j - 1, (r + 3) % RING, expert(1))
                    if r == 0:
                        load()
                    if ok(4):
                        ym(j - 4, r, expert(4))

                tile_groups(pe, l, b, step, 4)

            def conv_norm(b):
                if b == 0:
                    pe.wait_ge(S("xt_out0"), NB * TILES[0])
                for g in range(NG):
                    normed_group(pe, "c", ("XL", b), b, g)

            def group_stats(mat, ph):
                b, n = ph[1], gn_no(ph)
                pe.wait_ge(S("t_free"), groups_done[0])
                if n:
                    pe.wait_ge(S("gn_read"), n)
                pe.wait_ge(S("gn_in"), n + 1)
                nc.tensor.matmul(banks[1][:, 0:2], mat, GVB[b][:, 0:2], start=True, stop=True).then_inc(S("gn_sum"), 1)
                gn_done[0] = n + 1

            def conv1(b):
                pe.wait_ge(S("t_free"), group_base[("c", "XL", b)] + NG)
                if b == 0:
                    pe.wait_ge(S("h_free0"), NB * TILES[0])
                    pe.wait_ge(S("ht_out0"), NB * TILES[0])
                    pe.wait_ge(S("y_ready0"), NB * TILES[0])
                xin = QY[b][:, :].rearrange("p (n y x) -> p n y x", y=WS, x=WS)
                for hh in range(2):
                    for r in range(4):
                        ins = nc.tensor.matmul(banks[2 + hh][32 * r:32 * r + 32, 0:HALF], C1W[:, :],
                                               xin[:, hh * NW * NW // 2:(hh + 1) * NW * NW // 2, r, :], start=True, stop=True)
                ins.then_inc(S("conv1"), 1)
                group_stats(G2, ("XC", b))

            def taps(b, first, last):
                if first == 0:
                    pe.wait_ge(S("hp_ready"), b + 1)
                    if b == 0:
                        pe.wait_ge(S("toeplitz"), 4)
                count = 2 * KA * KX
                for m in range(round(first * count), round(last * count)):
                    hh, n = divmod(m, KA * KX)
                    a, kx = divmod(n, KX)
                    ins = nc.tensor.matmul(banks[4 + hh][:, 0:HALF], TOEP[:, n, :],
                                           HP[b][:, hh * NW // 2 + a:hh * NW // 2 + a + NW // 2, kx:kx + IMG],
                                           start=(n == 0), stop=(n == KA * KX - 1))
                if last == 1:
                    ins.then_inc(S("conv2"), 1)

            def conv2(b):
                pe.wait_ge(S("z_ready"), b + 1)
                for n in range(8):
                    r, hh = divmod(n, 2)
                    if n >= 4:
                        pe.wait_ge(S("up_out"), b * 8 + n - 3)
                    elif n == 0 and b:
                        pe.wait_ge(S("up_out"), 8 * b)
                    nc.tensor.matmul(banks[UP[b][n % 4]][:, 0:HALF], C2W[32 * r:32 * r + 32, :], HC[b][32 * r:32 * r + 32, hh, :],
                                     start=True, stop=True).then_inc(S("up"), 1)
                group_stats(G8, ("XU", b))

            def conv_sum(b):
                pe.wait_ge(S("z3_ready"), b + 1)
                for g in range(NG):
                    pe_group(pe, group_base[("z", "XZ", b)] + g, [QY[b][:, (g * TG + k) * P:(g * TG + k + 1) * P] for k in range(TG)])

            run(LNA=lna, ATT=att, RA=route_a, RS=route_b, M=moe, XL=conv_norm, XC=conv1, XT=taps,
                XM=lambda b: group_stats(G2, ("XM", b)), XU=conv2, XZ=conv_sum)

        @block.scalar
        def _(act):
            def sqrt_of(ph):
                act.wait_ge(S("ln_var"), ln_no(ph))
                nc.scalar.activation(LNV[:, 4, :], LNV[:, 3, :], ACT.Sqrt).then_inc(S("ln_std"), 1)

            def evac(tag, ph, dst, sem="t_free"):
                for g in range(NG):
                    n = group_base[(tag,) + ph] + g
                    t_wait_full(act, n)
                    nc.scalar.activation(dst[:, g * TG * P:(g + 1) * TG * P], banks[n % 2][:, 0:TG * P], ACT.Copy).then_inc(S(sem), 1)

            def lna(b):
                sqrt_of(("LNA", b))
                if b == 0:
                    act.wait_ge(S("q_scaled"), 1)
                for g in range(NG):
                    n = group_base[("a", "LNA", b)] + g
                    t_wait_full(act, n)
                    src = banks[n % 2][:, 0:TG * P]
                    nc.scalar.activation(QY[b][:, g * TG * P:(g + 1) * TG * P], src, ACT.Identity, bias=QS[:, 1:2], scale=QS[:, 0:1]).then_inc(S("q_ready"), 1)
                    sw = src.rearrange("p (v w y x) -> p v w y x", v=2, y=WS, x=WS)
                    for v in range(2):
                        y0 = (2 * g + v) * WS
                        ins = nc.scalar.activation(XPAD[b][:, y0:y0 + WS, 0:IMG].rearrange("p y (w x) -> p w y x", x=WS), sw[:, v], ACT.Copy)
                    ins.then_inc(S("t_free"), 1)

            def att(b):
                def keys(b, row, par):
                    act.wait_ge(S("edge"), b + 1)
                    if not isinstance(row, int) or b or row >= 2:
                        act.wait_ge(S("scores"), 2 * (row - 1) + b * STEPS)
                    nc.scalar.activation(KROW[par].rearrange("p (x y) -> p y x", y=WK), XPAD[b][:, ds(row * WS, WK), :],
                                         ACT.Identity, bias=KB, scale=KW).then_inc(S("k_row"), 1)

                def values(b, row, par):
                    act.wait_ge(S("edge"), b + 1)
                    if not isinstance(row, int) or b or row >= 2:
                        act.wait_ge(S("v_transposed"), 2 * (row - 1) + b * STEPS)
                    nc.scalar.activation(VROW[par].rearrange("p (x y) -> p y x", y=WK), XPAD[b][:, ds(row * WS, WK), :],
                                         ACT.Identity, bias=VB, scale=VW).then_inc(S("v_row"), 1)

                def expo(b, s, hf):
                    g = s + b * STEPS
                    act.wait_ge(S("shifted"), g + 1)
                    if not isinstance(s, int) or g >= 2:
                        act.wait_ge(S("probs"), g - 1)
                    nc.scalar.activation(PE_[hf], SB_[hf], ACT.Exp).then_inc(S("exps"), 1)

                def outs(b, s, hf):
                    g = s + b * STEPS
                    act.wait_ge(S("p_transposed"), g + 1)
                    if not isinstance(s, int) or g >= 2:
                        act.wait_ge(S("weighed"), g - 1)
                    for wl in range(2):
                        k = slice(KEYS * wl, KEYS * (wl + 1))
                        ins = nc.scalar.activation(PTS[hf][k, :, wl, :], banks[5][k, 0:W].rearrange("p (n m) -> p n m", m=P), ACT.Copy)
                    ins.then_inc(S("pt_out"), 1)
                    act.wait_ge(S("v_transposed"), g + 1)
                    nc.scalar.activation(VTS[hf], banks[0][:, 0:W], ACT.Copy).then_inc(S("vt_out"), 1)

                def y_out(b, row):
                    act.wait_ge(S("edge"), b + 1)
                    act.wait_ge(S("projected"), row + 1 + b * NW)
                    nc.scalar.activation(QY[b][:, :].rearrange("p (r w h q) -> p r w h q", w=HW_, h=2, q=Q)[:, ds(row, 1)].rearrange("p r w h q -> p (r w) h q"),
                                         banks[1][:, 0:NW * Q].rearrange("p (h w q) -> p w h q", h=2, q=Q), ACT.Copy).then_inc(S("attn_y"), 1)

                def step(c, at):
                    hf = c % 2
                    if hf == 0 and at(6):
                        y_out(at(6)[0], at(6)[2])
                    if at(3):
                        outs(*at(3)[:2], 1 - hf)
                    if at(1):
                        expo(*at(1)[:2], 1 - hf)
                    if hf == 0 and at(-2):
                        keys(at(-2)[0], at(-2)[2], 1 - c // 2)
                    if hf == 1 and at(0):
                        values(at(0)[0], at(0)[2], c // 2)

                if b == 0:
                    keys(0, 0, 0)
                att_steps(act, b, step, 1, 2)

            def route_a(l, b):
                ph = ("RA", l, b)
                sqrt_of(ph)
                if l == 0 and b == 1:
                    act.wait_ge(S("logits"), 1)
                if l == 1:
                    act.wait_ge(S("z3_ready"), b + 1)
                evac("r", ph, CM[l * b])

            def route_b(l, b):
                act.wait_ge(S("logit_shift"), l * NB + b + 1)
                nc.scalar.activation(RT[:, 1, 0:TT * EX[l]], RT[:, 0, 0:TT * EX[l]], ACT.Exp).then_inc(S("logit_exp"), 1)

            def moe(l, b):
                J = TILES[l]

                def xt(j, r):
                    act.wait_ge(S(f"x_transposed{l}"), j + 1 + b * J)
                    nc.scalar.activation(XTS[r % 2][:, :], banks[r % 2][:, 0:P], ACT.Copy).then_inc(S(f"xt_out{l}"), 1)

                def nonlin(j, r):
                    if l:
                        act.wait_ge(S("h_full1"), j + 1 + b * J)
                        if not isinstance(j, int) or b or j >= 2:
                            act.wait_ge(S("hid1"), j - 1 + b * J)
                        nc.scalar.activation(SG[r % 2][:, :], banks[2 + r % 2][:, 0:256], ACT.Silu).then_inc(S("silu"), 1)
                    else:
                        act.wait_ge(S("h_free0"), j + 1 + b * J)
                        nc.scalar.activation(HD_[r % 2][:, 0:P], SG[r % 2][:, 0:P], ACT.Gelu).then_inc(S("hid0"), 1)

                def tail(j, r, h=None):
                    if l:
                        act.wait_ge(S("y_full1"), j + 1 + b * J)
                        ys_free(act, 1, b, j, r, h)
                        nc.scalar.activation(YS[h * RING + r], banks[6 + r % 2][:, 0:P], ACT.Copy).then_inc(S("y_ready1"), 1)
                    else:
                        act.wait_ge(S("ht_full0"), j + 1 + b * J)
                        nc.scalar.activation(HTS[r % 2][:, 0:P], banks[4 + r % 2][:, 0:P], ACT.Copy).then_inc(S("ht_out0"), 1)

                def step(j, r, h, expert, load):
                    ok = lambda k: not isinstance(j, int) or 0 <= j - k < J
                    if ok(0):
                        xt(j, r)
                    if not l and ok(3):
                        tail(j - 3, (r + 1) % RING)
                    if ok(1):
                        nonlin(j - 1, (r + 3) % RING)
                    if l and ok(4):
                        tail(j - 4, r, 1 - h)

                tile_groups(act, l, b, step, 4, experts=False)

            def conv_norm(b):
                sqrt_of(("XL", b))
                evac("c", ("XL", b), QY[b])

            def gn_sqrt(ph):
                gv, n = GVB[ph[1]], gn_no(ph)
                act.wait_ge(S("gn_var"), n + 1)
                nc.scalar.activation(gv[:, 6:7], gv[:, 5:6], ACT.Sqrt).then_inc(S("gn_std"), 1)
                act.wait_ge(S("gn_coef"), n + 1)
                return {"bias": gv[:, 8:9], "scale": gv[:, 7:8]}

            def conv1(b):
                act.wait_ge(S("conv1"), b + 1)
                for hh in range(2):
                    nc.scalar.activation(HC[b][:, hh, :], banks[2 + hh][:, 0:HALF], ACT.Identity, bias=C1B).then_inc(S("hc_ready"), 1)
                norm = gn_sqrt(("XC", b))
                act.wait_ge(S("pad_zero"), b + 1)
                for hh in range(2):
                    ins = nc.scalar.activation(HP[b][:, 1 + hh * NW // 2:1 + (hh + 1) * NW // 2, 4:4 + IMG],
                                               HC[b][:, hh, :].rearrange("p (a x) -> p a x", x=IMG), ACT.Identity, **norm)
                ins.then_inc(S("hp_ready"), 1)

            def conv_mid(b):
                norm = gn_sqrt(("XM", b))
                for hh in range(2):
                    ins = nc.scalar.activation(HC[b][:, hh, :], banks[4 + hh][:, 0:HALF], ACT.Relu, **norm)
                ins.then_inc(S("z_ready"), 1)

            def conv2(b):
                cm = CM[b][:, :].rearrange("p (n y x) -> p n y x", y=WS, x=WS)
                for n in range(8):
                    r, hh = divmod(n, 2)
                    act.wait_ge(S("up"), b * 8 + n + 1)
                    nc.scalar.activation(cm[:, hh * NW * NW // 2:(hh + 1) * NW * NW // 2, r, :],
                                         banks[UP[b][n % 4]][:, 0:HALF].rearrange("p (n x) -> p n x", x=WS),
                                         ACT.Identity, bias=C2B).then_inc(S("up_out"), 1)
                nc.scalar.activation(QY[b][:, :], CM[b][:, :], ACT.Relu, **gn_sqrt(("XU", b))).then_inc(S("z3_ready"), 1)

            act.wait_ge(S("consts_in"), 64)
            run(LNA=lna, ATT=att, RA=route_a, RC=route_b, M=moe, XL=conv_norm, XC=conv1, XM=conv_mid, XU=conv2)

        @block.vector
        def _(dve):
            chain = [0]

            def link(ins):
                chain[0] += 1
                ins.then_inc(S("dve_chain"), 1)
                dve.wait_ge(S("dve_chain"), chain[0])

            tt, ts = nc.vector.tensor_tensor, nc.vector.tensor_scalar

            def tile_stats(b, g):
                for t in range(g * TG, (g + 1) * TG):
                    ins = nc.vector.bn_stats(STT[:, t, :], XT[b][:, t, :])
                if g == NG - 1:
                    link(ins)

            def layer_norm(ph, b, eps):
                me, ve, mo, vo = (STT[:, :, k] for k in (1, 2, 4, 5))
                tt(LNV[:, 0, :], me, mo, ALU.add)
                tt(LNV[:, 1, :], me, mo, ALU.subtract)
                link(tt(LNV[:, 2, :], ve, vo, ALU.add))
                ts(LNV[:, 0, :], LNV[:, 0, :], 0.5, None, ALU.mult)
                link(tt(LNV[:, 1, :], LNV[:, 1, :], LNV[:, 1, :], ALU.mult))
                link(nc.vector.scalar_tensor_tensor(LNV[:, 3, :], LNV[:, 1, :], float(P // 4), LNV[:, 2, :], ALU.mult, ALU.add))
                ts(LNV[:, 3, :], LNV[:, 3, :], 1.0 / P, eps, ALU.mult, ALU.add).then_inc(S("ln_var"), 1)
                dve.wait_ge(S("ln_std"), ln_no(ph))
                link(nc.vector.reciprocal(LNV[:, 5, :], LNV[:, 4, :]))
                for t in range(TT):
                    ins = ts(TN[b][:, t, :], XT[b][:, t, :], LNV[:, 0, t:t + 1], LNV[:, 5, t:t + 1], ALU.subtract, ALU.mult)
                    if t % TG == TG - 1:
                        ins.then_inc(S("ln_done"), 1)

            def lna(b):
                dve.wait_ge(S(f"x_in{b}"), 16)
                if b == 0:
                    dve.wait_ge(S("consts_in"), 64)
                    ts(QS[:, 0:1], QW, HD ** -0.5, None, ALU.mult)
                    ts(QS[:, 1:2], QB, HD ** -0.5, None, ALU.mult).then_inc(S("q_scaled"), 1)
                    for a in range(2):
                        ins = ts(OWP[:, a, :], OWT[:, :], PAR[:, a:a + 1], None, ALU.mult)
                    link(ins)
                for g in range(NG):
                    tile_stats(b, g)
                layer_norm(("LNA", b), b, 1e-6)
                for k in range(NB if b == NB - 1 else 0):
                    dve.wait_ge(S("t_free"), group_base[("a", "LNA", k)] + NG)
                    link(nc.vector.tensor_copy(XPAD[k][:, 0:IMG, IMG:PADI], XPAD[k][:, 0:IMG, IMG - 1:IMG].broadcast_to([P, IMG, PADI - IMG])))
                    nc.vector.tensor_copy(XPAD[k][:, IMG:PADI, :], XPAD[k][:, IMG - 1:IMG, :].broadcast_to([P, PADI - IMG, PADI])).then_inc(S("edge"), 1)

            def att(b):
                def three(ap):
                    return ap.rearrange("p (w k) -> p w k", k=KEYS)

                def top(b, s, hf):
                    g = s + b * STEPS
                    dve.wait_ge(S("scores"), g + 1)
                    if not isinstance(s, int) or g >= 2:
                        dve.wait_ge(S("exps"), g - 1)
                    tt(three(SB_[hf]), three(banks[2 + hf][:, 0:W]), BIAS[:, :].unsqueeze(1).broadcast_to([P, HW_, KEYS]), ALU.add).then_inc(S("biased"), 1)
                    dve.wait_ge(S("biased"), g + 1)
                    nc.vector.tensor_reduce(MXS[:, hf, :], three(SB_[hf]), AX, ALU.max).then_inc(S("maxed"), 1)
                    dve.wait_ge(S("maxed"), g + 1)
                    tt(three(SB_[hf]), three(SB_[hf]), MXS[:, hf, :].unsqueeze(2).broadcast_to([P, HW_, KEYS]), ALU.subtract).then_inc(S("shifted"), 1)

                def sums(b, s, hf):
                    g = s + b * STEPS
                    dve.wait_ge(S("exps"), g + 1)
                    nc.vector.tensor_reduce(RSM[:, hf, :], three(PE_[hf]), AX, ALU.add).then_inc(S("summed"), 1)
                    dve.wait_ge(S("summed"), g + 1)
                    if not isinstance(s, int) or g >= 2:
                        dve.wait_ge(S("probs"), g - 1)
                    nc.vector.reciprocal(RRC[:, hf, :], RSM[:, hf, :]).then_inc(S("rsum"), 1)

                def o_out(b, s, row, hf, par):
                    dve.wait_ge(S("weighed"), s + b * STEPS + 1)
                    if hf == 0 and (not isinstance(s, int) or row + b >= 2 or b):
                        dve.wait_ge(S("projected"), row - 1 + b * NW)
                    nc.vector.tensor_copy(OS[par][:, :, hf].rearrange("p a w q -> p w a q"),
                                          banks[6 + hf][:, 0:192].rearrange("p (w a q) -> p w a q", a=2, q=Q)).then_inc(S("o_out"), 1)

                def step(c, at):
                    hf = c % 2
                    if at(4):
                        o_out(*at(4), hf, c // 2)
                    if at(0):
                        top(*at(0)[:2], hf)
                    if at(1):
                        sums(*at(1)[:2], 1 - hf)

                att_steps(dve, b, step, 0, 2)

            def route_a(l, b):
                ph = ("RA", l, b)
                if l == 0:
                    for g in range(NG):
                        m = group_base[("y",) + ph] + g
                        t_wait_full(dve, m)
                        xt = XT[b][:, g * TG:(g + 1) * TG, :]
                        tt(xt, xt, banks[m % 2][:, 0:TG * P].rearrange("p (t c) -> p t c", c=P), ALU.add).then_inc(S("t_free"), 1)
                        if g:
                            dve.wait_ge(S("t_free"), m)
                            tile_stats(b, g - 1)
                    dve.wait_ge(S("t_free"), m + 1)
                    tile_stats(b, NG - 1)
                layer_norm(ph, b, 1e-5)

            def route_views(l):
                E = EX[l]
                return (lambda k: RT[:, k, 0:TT * E].rearrange("p (t e) -> p t e", e=E), [RV[:, k, :] for k in range(4)],
                        lambda v: v.unsqueeze(2).broadcast_to([P, TT, E]), lambda v: v.unsqueeze(1).broadcast_to([P, TT, E]))

            def choose(l, b):
                E, n = EX[l], l * NB + b
                c = TT * E
                row, v, over_e, over_t = route_views(l)
                dve.wait_ge(S("logits"), n + 1)
                lg = banks[2][:, 0:c].rearrange("p (t e) -> p t e", e=E)
                if l:
                    link(tt(row(0), lg, over_t(GB[:, :]), ALU.add))
                    lg = row(0)
                link(nc.vector.tensor_reduce(v[0], lg, AX, ALU.max))
                tt(row(0), lg, over_e(v[0]), ALU.subtract).then_inc(S("logit_shift"), 1)
                dve.wait_ge(S("logit_exp"), n + 1)
                link(nc.vector.tensor_reduce(v[0], row(1), AX, ALU.add))
                link(nc.vector.reciprocal(v[1], v[0]))
                link(tt(row(1), row(1), over_e(v[1]), ALU.mult))
                for k in range(2):
                    link(nc.vector.tensor_reduce(v[k], row(1), AX, ALU.max))
                    link(tt(row(0), row(1), over_e(v[k]), ALU.is_equal))
                    link(tt(row(0), row(0), over_t(REV[:, 0:E]), ALU.mult))
                    link(nc.vector.tensor_reduce(v[2], row(0), AX, ALU.max))
                    link(tt(row(2 + k), row(0), over_e(v[2]), ALU.is_equal))
                    if k == 0:
                        link(nc.vector.scalar_tensor_tensor(row(1), row(2), -2.0, row(1), ALU.mult, ALU.add))
                tt(row(5), row(2), row(3), ALU.add).then_inc(S("chosen"), 1)
                link(tt(v[2], v[0], v[1], ALU.add))
                if l == 0:
                    link(nc.vector.tensor_scalar_max(v[2], v[2], 1e-12))
                link(nc.vector.reciprocal(v[3], v[2]))
                tt(GATE[b][:, 0, :], v[0], v[3], ALU.mult)
                tt(GATE[b][:, 1, :], v[1], v[3], ALU.mult)

            def slots(l, b):
                E, n, J = EX[l], l * NB + b, TILES[l]
                c = TT * E
                row, v, over_e, over_t = route_views(l)
                dve.wait_ge(S("prefix"), n + 1)
                tot = RT[:, 0, 0:c].rearrange("p (e t) -> p e t", t=TT)
                one = RT[:, 1, 0:c].rearrange("p (e t) -> p e t", t=TT)
                nc.vector.memset(RT[:, 1, 0:c], 1.0).then_inc(S("dve_chain"), 1)
                chain[0] += 1
                link(nc.vector.tensor_copy(tot, banks[7][:, 0:c].rearrange("p (t e) -> p e t", e=E)))
                link(nc.vector.memset(one[:, :, 0:1], 0.0))
                link(nc.vector.tensor_tensor_scan(RT[:, 4, 0:c], RT[:, 1, 0:c], RT[:, 0, 0:c], 0.0, ALU.mult, ALU.add))
                run_ = RT[:, 4, 0:c].rearrange("p (e t) -> p e t", t=TT)
                cnt, nt, st, en = (RS[:, k, 0:E] for k in range(4))
                nc.vector.tensor_copy(cnt, run_[:, :, TT - 1])
                link(tt(tot, run_, tot, ALU.subtract))
                tmp = RT[:, 1, 0:c].rearrange("p (e t) -> p e t", t=TT)
                link(tt(tmp, cnt.unsqueeze(2).broadcast_to([P, E, TT]), T128.unsqueeze(1).broadcast_to([P, E, TT]), ALU.is_gt))
                link(nc.vector.tensor_reduce(nt, tmp, AX, ALU.add))
                link(nc.vector.tensor_tensor_scan(en, ONE[:, 0:E], nt, 0.0, ALU.mult, ALU.add))
                link(tt(st, en, nt, ALU.subtract))
                link(nc.vector.scalar_tensor_tensor(RT[:, 4, 0:c].rearrange("p (t e) -> p e t", e=E), st.unsqueeze(2).broadcast_to([P, E, TT]),
                                                    float(P), tot, ALU.mult, ALU.add))
                link(tt(row(4), row(4), banks[6][:, 0:c].rearrange("p (t e) -> p t e", e=E), ALU.add))
                for k in range(2):
                    link(tt(row(0), row(2 + k), row(4), ALU.mult))
                    link(nc.vector.tensor_reduce(v[2], row(0), AX, ALU.add))
                    ins = nc.vector.tensor_copy(POS[b][:, k, :], v[2])
                    if k == 0:
                        link(ins)
                ins.then_inc(S(f"routed{l}{b}"), 1)
                jw = WORDS[l] * GW[l] * RING
                jh = jw // 2
                ej = EJ[:, 0:E * jh].rearrange("p (j e) -> p j e", e=E)
                for hh in range(2):
                    link(tt(ej, en.unsqueeze(1).broadcast_to([P, jh, E]), JI[:, hh * jh:(hh + 1) * jh].unsqueeze(2).broadcast_to([P, jh, E]), ALU.is_le))
                    link(nc.vector.tensor_reduce(RT[:, 1, hh * jh:(hh + 1) * jh], ej, AX, ALU.add))
                link(nc.vector.tensor_scalar_min(RT[:, 1, 0:jw], RT[:, 1, 0:jw], float(E - 1)))
                er = RT[:, 1, 0:jw].rearrange("p (g r) -> p g r", r=GW[l] * RING)
                link(tt(er, er, POW[l].unsqueeze(1).broadcast_to([P, WORDS[l], GW[l] * RING]), ALU.mult))
                link(nc.vector.tensor_reduce(RV4[:, 0:WORDS[l]], er, AX, ALU.add))
                nc.vector.tensor_copy(EPK[l][b][:, :], RV4[:, 0:WORDS[l]]).then_inc(S(f"experts{l}{b}"), 1)

            def moe(l, b):
                J = TILES[l]

                def first(j, r, e):
                    if l:
                        dve.wait_ge(S("silu"), j + 1 + b * J)
                        tt(HD_[r % 2][:, :], SG[r % 2][:, :], banks[2 + r % 2][:, 256:512], ALU.mult).then_inc(S("hid1"), 1)
                        return
                    dve.wait_ge(S("h_full0"), j + 1 + b * J)
                    tt(SG[r % 2][:, 0:P], banks[2 + r % 2][:, 0:P], B1E[:, ds(e, 1), :].rearrange("p a c -> p (a c)"), ALU.add).then_inc(S("h_free0"), 1)

                def second(j, r, e, h=None):
                    if l:
                        dve.wait_ge(S("ht_full1"), j + 1 + b * J)
                        nc.vector.tensor_copy(HTS[r % 2][:, :], banks[4 + r % 2][:, 0:256]).then_inc(S("ht_out1"), 1)
                        return
                    dve.wait_ge(S("y_full0"), j + 1 + b * J)
                    ys_free(dve, 0, b, j, r, h)
                    tt(YS[h * RING + r], banks[6 + r % 2][:, 0:P], B2E[:, ds(e, 1), :].rearrange("p a c -> p (a c)"), ALU.add).then_inc(S("y_ready0"), 1)

                def step(j, r, h, expert, load):
                    ok = lambda k: not isinstance(j, int) or 0 <= j - k < J
                    if l and ok(3):
                        second(j - 3, (r + 1) % RING, None)
                    if ok(1):
                        first(j - 1, (r + 3) % RING, None if l else expert(1))
                    if r == 0:
                        load()
                    if not l and ok(4):
                        second(j - 4, r, expert(4), 1 - h)

                tile_groups(dve, l, b, step, 4, experts=not l)

            def combine(l, b, done):
                if l == 0:
                    dve.wait_ge(S(f"normed_added{b}"), 1)
                    dve.wait_ge(S(f"scattered0{b}"), 16 * 2 * TT)
                for g in range(NG):
                    for part in range(g, g + (2 if g == NG - 1 else 1)):
                        tiles = [t for t in range(g * TG, (g + 1) * TG) if gather_part(t) == part]
                        dve.wait_ge(S(f"gathered{part}"), 16 * 2 * len(tiles) * (l * NB + b + 1))
                        for k in range(2):
                            for t in tiles:
                                ins = nc.vector.scalar_tensor_tensor(XT[b][:, t, :], G[k][:, t, :], GATE[b][:, k, t:t + 1], XT[b][:, t, :], ALU.mult, ALU.add)
                            if k == 0:
                                link(ins)
                    ins.then_inc(S(done), 1)
                    if l == 0 and g:
                        dve.wait_ge(S(done), NG * b + g)
                        tile_stats(b, g - 1)
                if l == 0:
                    dve.wait_ge(S(done), NG * (b + 1))
                    tile_stats(b, NG - 1)

            def gn(ph, chunks, gamma, beta):
                gv, n = GVB[ph[1]], gn_no(ph)
                for k, a in enumerate(chunks):
                    ins = nc.vector.bn_stats(GST[:, k, :], a)
                link(ins)
                link(nc.vector.bn_aggr(gv[:, 2:4], GST[:, 0:len(chunks), :]))
                ts(gv[:, 0:1], gv[:, 2:3], 1.0, None, ALU.mult)
                link(tt(gv[:, 4:5], gv[:, 2:3], gv[:, 2:3], ALU.mult))
                tt(gv[:, 1:2], gv[:, 4:5], gv[:, 3:4], ALU.add).then_inc(S("gn_in"), 1)
                dve.wait_ge(S("gn_sum"), n + 1)
                nc.vector.tensor_copy(gv[:, 2:4], banks[1][:, 0:2]).then_inc(S("gn_read"), 1)
                dve.wait_ge(S("gn_read"), n + 1)
                link(tt(gv[:, 4:5], gv[:, 2:3], gv[:, 2:3], ALU.mult))
                link(tt(gv[:, 5:6], gv[:, 3:4], gv[:, 4:5], ALU.subtract))
                ts(gv[:, 5:6], gv[:, 5:6], 1e-5, None, ALU.add).then_inc(S("gn_var"), 1)
                dve.wait_ge(S("gn_std"), n + 1)
                link(nc.vector.reciprocal(gv[:, 9:10], gv[:, 6:7]))
                link(tt(gv[:, 7:8], gv[:, 9:10], gamma, ALU.mult))
                link(tt(gv[:, 10:11], gv[:, 2:3], gv[:, 7:8], ALU.mult))
                tt(gv[:, 8:9], beta, gv[:, 10:11], ALU.subtract).then_inc(S("gn_coef"), 1)

            def conv_norm(b):
                combine(0, b, "combined")
                layer_norm(("XL", b), b, 1e-6)

            def conv1(b):
                dve.wait_ge(S("hc_ready"), 2 * (b + 1))
                gn(("XC", b), [HC[b][:, hh, :] for hh in range(2)], N1G, N1B)

            def conv_mid(b):
                dve.wait_ge(S("conv2"), b + 1)
                dve.wait_ge(S("hp_ready"), b + 1)
                gn(("XM", b), [banks[4 + hh][:, 0:HALF] for hh in range(2)], NMG, NMB)

            def conv2(b):
                dve.wait_ge(S("z_ready"), b + 1)
                dve.wait_ge(S("up_out"), 8 * (b + 1))
                gn(("XU", b), [CM[b][:, k * NT // 6:(k + 1) * NT // 6] for k in range(6)], N2G, N2B)

            def conv_sum(b):
                dve.wait_ge(S(f"normed_added{b}"), 2)
                for g in range(NG):
                    m = group_base[("z", "XZ", b)] + g
                    t_wait_full(dve, m)
                    xt = XT[b][:, g * TG:(g + 1) * TG, :]
                    tt(xt, xt, banks[m % 2][:, 0:TG * P].rearrange("p (t c) -> p t c", c=P), ALU.add).then_inc(S("t_free"), 1)
                    if g:
                        dve.wait_ge(S("t_free"), m)
                        tile_stats(b, g - 1)
                dve.wait_ge(S("t_free"), m + 1)
                tile_stats(b, NG - 1)

            run(LNA=lna, ATT=att, RA=route_a, RC=choose, RS=slots, M=moe, XL=conv_norm, XC=conv1, XM=conv_mid, XU=conv2, XZ=conv_sum,
                F=lambda b: combine(1, b, "out_ready"))


def constants():
    import numpy as np
    P, E, J, TT = 128, 16, 52, 18
    p = np.arange(P)
    j = np.arange(7)[:, None, None] + 1
    d = ((p[None, :, None] % 32) - np.arange(32)[None, None, :] + 4 == j)
    cols = [np.eye(P), p[:, None] < p[None, :], np.ones((P, P)),
            ((p[:, None] % 32) // 2 == (p[None, :] % 32) // 2) / 8.0, (p[:, None] // 8 == p[None, :] // 8) / 8.0,
            (p[:, None] // 16) % 4 == np.arange(4)[None, :], (p[:, None] // 16) % 2 == np.arange(2)[None, :],
            p[:, None] % 32 == np.arange(32)[None, :], d.transpose(1, 0, 2).reshape(P, 224),
            np.broadcast_to(E - np.arange(E), (P, E)), np.broadcast_to(np.arange(J), (P, J)),
            np.broadcast_to(128 * np.arange(TT), (P, TT)), np.broadcast_to(16 ** np.arange(4), (P, 4)),
            np.broadcast_to(8 ** np.arange(8), (P, 8))]
    return np.ascontiguousarray(np.concatenate([np.asarray(c, np.float32) for c in cols], axis=1))


def kernel(**inputs):
    import numpy as np
    import concourse.bacc as _bacc
    from concourse import mybir as _mybir
    from concourse.bass_utils import run_bass_kernel_spmd as _run

    a = {k: np.asarray(v) for k, v in inputs.items()}
    P = 128
    x = a["x"].reshape(2, P, 12, 4, 12, 4).transpose(0, 2, 4, 3, 5, 1).reshape(2, 18, P, P).transpose(0, 2, 1, 3)
    qw, qb = a["L0_conv_qkv_w"].reshape(3, P), a["L0_conv_qkv_b"].reshape(3, P)
    rep = lambda v: np.tile(v, 4)
    params = np.stack([qw[0], qb[0], qw[1], qb[1], qw[2], qb[2], rep(a["L1_conv_conv1_b"]), rep(a["L1_conv_gn1_g"]), rep(a["L1_conv_gn1_b"]),
                       rep(a["L1_conv_gnm_g"]), rep(a["L1_conv_gnm_b"]), a["L1_conv_conv2_b"], a["L1_conv_gn2_g"], a["L1_conv_gn2_b"],
                       a["L1_conv_gn2_b"], a["L1_conv_gn2_b"]], axis=1)
    qi, qj, kj, ki = np.ix_(np.arange(4), np.arange(4), np.arange(8), np.arange(8))
    index = ((qi - ki + 7) * 15 + (qj - kj + 7)).reshape(16, 64)
    pos_bias = a["L0_conv_pos_table"][index].transpose(2, 0, 1).reshape(P, 64)
    w2 = a["L1_conv_W2"][:, 0]
    w2_rows = np.zeros((4, 32, 12, 9), np.float32)
    for r in range(4):
        for m in range(12):
            if 0 <= m - 3 + r < 9:
                w2_rows[r, :, m] = w2[:, m - 3 + r]
    bc = lambda v: np.broadcast_to(v, (P,) + v.shape)
    arrays = {
        "x_tok": x, "params": params, "consts": constants(), "pos_bias": pos_bias,
        "out_wT": a["L0_conv_out_w"].T, "conv1_wT": a["L1_conv_conv1_w"].T, "conv2_wT": np.tile(a["L1_conv_conv2_w"].T, (4, 1)),
        "w2_rows": w2_rows.reshape(P, 12, 9), "w1_conv": bc(a["L1_conv_W1"].reshape(9)),
        "router_wT": a["L0_ffn_router_w"].T, "gate_wT": a["L1_ffn_gate_w"], "gate_b": bc(a["L1_ffn_gate_b"]),
        "moe0_w1": a["L0_ffn_w1"].transpose(1, 0, 2), "moe0_w2": a["L0_ffn_w2"].transpose(1, 0, 2),
        "moe0_b1": bc(a["L0_ffn_b1"]), "moe0_b2": bc(a["L0_ffn_b2"]),
        "moe1_w12": np.concatenate([a["L1_ffn_w1"], a["L1_ffn_w2"]], axis=2).transpose(1, 0, 2),
        "moe1_w3": a["L1_ffn_w3"].reshape(16, 2, P, P).transpose(2, 0, 1, 3),
    }
    nc = _bacc.Bacc("TRN2", target_bir_lowering=False, num_devices=1)
    args = []
    for name in arrays:
        arrays[name] = np.ascontiguousarray(arrays[name])
        args.append(nc.dram_tensor("in_" + name, arrays[name].shape, _mybir.dt.from_np(arrays[name].dtype), kind="ExternalInput").ap())
    args.append(nc.dram_tensor("out", (2, P, 18, P), _mybir.dt.float32, kind="ExternalOutput").ap())
    metaformer_program(nc, *args)
    r = _run(nc, [{"in_" + k: v for k, v in arrays.items()}], core_ids=[0])
    y = np.asarray(r.results[0]["out"])
    return np.ascontiguousarray(y.transpose(0, 2, 1, 3).reshape(2, 12, 12, 4, 4, P).transpose(0, 5, 1, 3, 2, 4).reshape(2, P, 48, 48))
```
